# Optimizing a Trainium2 kernel written in Bass

```python
import numpy as np
import jax
import jax.numpy as jnp

def _softmax(x, axis=-1):
    return jax.nn.softmax(x, axis=axis)

def _gelu(x):
    return jax.nn.gelu(x, approximate=True)

def _silu(x):
    return jax.nn.silu(x)

def _sigmoid(x):
    return jax.nn.sigmoid(x)

def _layernorm(x, axis=-1, eps=1e-05):
    m = jnp.mean(x, axis=axis, keepdims=True)
    v = jnp.var(x, axis=axis, keepdims=True)
    return (x - m) / jnp.sqrt(v + eps)

def _scatter_add(tgt, idx, src, axis=0):
    return tgt.at[idx].add(src)

def _segment_sum(src, seg, n):
    return jax.ops.segment_sum(src, seg, n)
kernel_name = 'mk_seq_preln_d1_jaxref_r8_426b5c'

def setup_inputs(seed: int=0):
    np.random.seed(seed)
    _w = jnp.asarray

    def _L0_attn_setup():
        import jax, jax.numpy as jnp
        from jax import lax
        import numpy as np
        D = 128
        H = 6
        DK = 128
        DV = 32
        KD = H * DK
        VD = H * DV
        KS = 4
        EPS = 1e-05
        B, L = (2, 128)

        def _causal_conv_silu(x, w):
            xt = jnp.transpose(x, (0, 2, 1))
            out = lax.conv_general_dilated(xt, w[:, None, :], window_strides=(1,), padding=[(KS - 1, 0)], feature_group_count=w.shape[0])
            return jnp.transpose(jax.nn.silu(out), (0, 2, 1))

        def _l2norm(t):
            return t * lax.rsqrt(jnp.sum(t * t, axis=-1, keepdims=True) + 1e-12)

        def _reference_tuple_inner(x, Wq, Wk, Wv, Wb, Wa, A_log, dt_bias, conv_q, conv_k, conv_v, Wg, norm_w, Wo):
            Bc, Lc, _ = x.shape
            q = _causal_conv_silu(x @ Wq, conv_q).reshape(Bc, Lc, H, DK)
            k = _causal_conv_silu(x @ Wk, conv_k).reshape(Bc, Lc, H, DK)
            v = _causal_conv_silu(x @ Wv, conv_v).reshape(Bc, Lc, H, DV)
            beta = jax.nn.sigmoid(x @ Wb)
            g = -jnp.exp(A_log) * jax.nn.softplus(x @ Wa + dt_bias)
            q = _l2norm(q) * DK ** (-0.5)
            k = _l2norm(k)
            qt = jnp.moveaxis(q, 1, 0)
            kt = jnp.moveaxis(k, 1, 0)
            vt = jnp.moveaxis(v, 1, 0)
            gt = jnp.moveaxis(g, 1, 0)
            bt = jnp.moveaxis(beta, 1, 0)
            S0 = jnp.zeros((Bc, H, DK, DV), dtype=x.dtype)

            def step(S, inp):
                q_t, k_t, v_t, g_t, b_t = inp
                S = S * jnp.exp(g_t)[..., None, None]
                corr = jnp.einsum('bhk,bhkv->bhv', k_t, S)
                u = (v_t - corr) * b_t[..., None]
                S = S + k_t[..., None] * u[:, :, None, :]
                o_t = jnp.einsum('bhk,bhkv->bhv', q_t, S)
                return (S, o_t)
            S, o = lax.scan(step, S0, (qt, kt, vt, gt, bt))
            o = jnp.moveaxis(o, 0, 1)
            gate = (x @ Wg).reshape(Bc, Lc, H, DV)
            o = o * lax.rsqrt(jnp.mean(o * o, axis=-1, keepdims=True) + EPS)
            o = o * norm_w * jax.nn.silu(gate)
            o = o.reshape(Bc, Lc, VD) @ Wo
            return (o, S)
        key = jax.random.key(seed)
        ks = jax.random.split(key, 16)
        s = 0.02
        x = jax.random.normal(ks[0], (B, L, D), dtype=jnp.float32)
        Wq = jax.random.normal(ks[1], (D, KD), dtype=jnp.float32) * s
        Wk = jax.random.normal(ks[2], (D, KD), dtype=jnp.float32) * s
        Wv = jax.random.normal(ks[3], (D, VD), dtype=jnp.float32) * s
        Wb = jax.random.normal(ks[4], (D, H), dtype=jnp.float32) * s
        Wa = jax.random.normal(ks[5], (D, H), dtype=jnp.float32) * s
        A_log = jnp.log(jax.random.uniform(ks[6], (H,), minval=0.001, maxval=16.0))
        dt = jnp.exp(jax.random.uniform(ks[7], (H,)) * (np.log(0.1) - np.log(0.001)) + np.log(0.001))
        dt = jnp.clip(dt, 0.0001)
        dt_bias = dt + jnp.log(-jnp.expm1(-dt))
        conv_q = jax.random.normal(ks[8], (KD, KS), dtype=jnp.float32) * 0.3
        conv_k = jax.random.normal(ks[9], (KD, KS), dtype=jnp.float32) * 0.3
        conv_v = jax.random.normal(ks[10], (VD, KS), dtype=jnp.float32) * 0.3
        Wg = jax.random.normal(ks[11], (D, VD), dtype=jnp.float32) * s
        norm_w = jnp.ones((DV,), dtype=jnp.float32)
        Wo = jax.random.normal(ks[12], (VD, D), dtype=jnp.float32) * s
        return {'x': x, 'Wq': Wq, 'Wk': Wk, 'Wv': Wv, 'Wb': Wb, 'Wa': Wa, 'A_log': A_log, 'dt_bias': dt_bias, 'conv_q': conv_q, 'conv_k': conv_k, 'conv_v': conv_v, 'Wg': Wg, 'norm_w': norm_w, 'Wo': Wo}
    _L0_attn_in = _L0_attn_setup()

    def _L0_ffn_setup():
        import jax, jax.numpy as jnp
        import numpy as np
        DIM = 128
        DEPTH = 6
        HEADS = 16
        DIM_HEAD = 64
        WINDOW = 32
        INNER = HEADS * DIM_HEAD
        DIM_INNER = int(DIM * 4 * 2 / 3)
        QK_SCALE = 8.0

        def shift_tokens(t):
            a, s = jnp.split(t, 2, -1)
            s = jnp.pad(s, ((0, 0), (1, 0), (0, 0)))[:, :-1]
            return jnp.concatenate([a, s], -1)

        def l2norm(t):
            return t / jnp.maximum(jnp.linalg.norm(t, axis=-1, keepdims=True), 1e-12)

        def rotate_half(x):
            x1, x2 = jnp.split(x, 2, -1)
            return jnp.concatenate([-x2, x1], -1)

        def rotary_tables(n):
            half = jnp.arange(0, DIM_HEAD, 2, dtype=jnp.float32)
            inv_freq = 1.0 / 10000.0 ** (half / DIM_HEAD)
            t = jnp.arange(n, dtype=jnp.float32)
            freqs = t[:, None] * inv_freq[None, :]
            freqs = jnp.concatenate([freqs, freqs], -1)
            base_scale = (half + 0.4 * DIM_HEAD) / (1.4 * DIM_HEAD)
            power = (t - n // 2) / (WINDOW // 2)
            scale = base_scale[None, :] ** power[:, None]
            scale = jnp.concatenate([scale, scale], -1)
            return (freqs, scale)

        def local_attention(q, k, v):
            b, h, n, d = q.shape
            w = WINDOW
            nw = n // w
            bq = q.reshape(b, h, nw, w, d)
            bk = k.reshape(b, h, nw, w, d)
            bv = v.reshape(b, h, nw, w, d)

            def look(t):
                p = jnp.pad(t, ((0, 0), (0, 0), (1, 0), (0, 0), (0, 0)))
                return jnp.concatenate([p[:, :, :nw], p[:, :, 1:]], axis=3)
            bk2, bv2 = (look(bk), look(bv))
            seq = jnp.arange(n).reshape(nw, w)
            seq_p = jnp.pad(seq, ((1, 0), (0, 0)), constant_values=-1)
            jt = jnp.concatenate([seq_p[:nw], seq_p[1:]], axis=1)
            it = seq[:, :, None]
            jb = jt[:, None, :]
            mask = (it < jb) | (it > jb + w) | (jb == -1)
            sim = jnp.einsum('bhwie,bhwje->bhwij', bq, bk2) * QK_SCALE
            sim = jnp.where(mask, -jnp.finfo(sim.dtype).max, sim)
            attn = jax.nn.softmax(sim, -1)
            out = jnp.einsum('bhwij,bhwje->bhwie', attn, bv2)
            return out.reshape(b, h, n, d)

        def attn_layer(x, Wqkv, qs, ksc, Wo):
            b, n, _ = x.shape
            qkv = x @ Wqkv
            q, k, v = jnp.split(qkv, 3, -1)
            sh = lambda t: t.reshape(b, n, HEADS, DIM_HEAD).transpose(0, 2, 1, 3)
            q, k, v = (sh(q), sh(k), sh(v))
            q = l2norm(q) * qs
            k = l2norm(k) * ksc
            freqs, scale = rotary_tables(n)
            cos, sin = (jnp.cos(freqs), jnp.sin(freqs))
            q = q * cos * scale + rotate_half(q) * sin * scale
            inv = 1.0 / scale
            k = k * cos * inv + rotate_half(k) * sin * inv
            out = local_attention(q, k, v)
            out = out.transpose(0, 2, 1, 3).reshape(b, n, INNER)
            return out @ Wo

        def ffn_layer(x, g, bln, W1, b1, W2, b2):
            mu = x.mean(-1, keepdims=True)
            var = ((x - mu) ** 2).mean(-1, keepdims=True)
            xn = (x - mu) / jnp.sqrt(var + 1e-05) * g + bln
            hg = xn @ W1 + b1
            a, gate = jnp.split(hg, 2, -1)
            return a * jax.nn.gelu(gate, approximate=False) @ W2 + b2
        key = jax.random.key(seed)
        ks = jax.random.split(key, 8)
        B, N = (2, 256)
        init = lambda k, shape: jax.random.normal(k, shape, jnp.float32) * 0.02
        return {'x': jax.random.normal(ks[0], (B, N, DIM), jnp.float32), 'Wqkv': init(ks[1], (DEPTH, DIM, 3 * INNER)), 'q_scale': jnp.ones((DEPTH, DIM_HEAD), jnp.float32), 'k_scale': jnp.ones((DEPTH, DIM_HEAD), jnp.float32), 'Wo': init(ks[2], (DEPTH, INNER, DIM)), 'ln_g': jnp.ones((DEPTH, DIM), jnp.float32), 'ln_b': jnp.zeros((DEPTH, DIM), jnp.float32), 'W1': init(ks[3], (DEPTH, DIM, 2 * DIM_INNER)), 'b1': jnp.zeros((DEPTH, 2 * DIM_INNER), jnp.float32), 'W2': init(ks[4], (DEPTH, DIM_INNER, DIM)), 'b2': jnp.zeros((DEPTH, DIM), jnp.float32)}
    _L0_ffn_in = _L0_ffn_setup()
    _d = {'L0_attn_x': _L0_attn_in['x'], 'L0_attn_Wq': _L0_attn_in['Wq'], 'L0_attn_Wk': _L0_attn_in['Wk'], 'L0_attn_Wv': _L0_attn_in['Wv'], 'L0_attn_Wb': _L0_attn_in['Wb'], 'L0_attn_Wa': _L0_attn_in['Wa'], 'L0_attn_A_log': _L0_attn_in['A_log'], 'L0_attn_dt_bias': _L0_attn_in['dt_bias'], 'L0_attn_conv_q': _L0_attn_in['conv_q'], 'L0_attn_conv_k': _L0_attn_in['conv_k'], 'L0_attn_conv_v': _L0_attn_in['conv_v'], 'L0_attn_Wg': _L0_attn_in['Wg'], 'L0_attn_norm_w': _L0_attn_in['norm_w'], 'L0_attn_Wo': _L0_attn_in['Wo'], 'L0_ffn_Wqkv': _L0_ffn_in['Wqkv'], 'L0_ffn_q_scale': _L0_ffn_in['q_scale'], 'L0_ffn_k_scale': _L0_ffn_in['k_scale'], 'L0_ffn_Wo': _L0_ffn_in['Wo'], 'L0_ffn_ln_g': _L0_ffn_in['ln_g'], 'L0_ffn_ln_b': _L0_ffn_in['ln_b'], 'L0_ffn_W1': _L0_ffn_in['W1'], 'L0_ffn_b1': _L0_ffn_in['b1'], 'L0_ffn_W2': _L0_ffn_in['W2'], 'L0_ffn_b2': _L0_ffn_in['b2']}
    _x0 = _d['L0_attn_x']
    _d['L0_attn_x'] = jax.random.normal(jax.random.fold_in(jax.random.key(seed), 1), (4, 1024, 128), dtype=_x0.dtype)
    del _x0
    return _d

def reference(L0_attn_x, L0_attn_Wq, L0_attn_Wk, L0_attn_Wv, L0_attn_Wb, L0_attn_Wa, L0_attn_A_log, L0_attn_dt_bias, L0_attn_conv_q, L0_attn_conv_k, L0_attn_conv_v, L0_attn_Wg, L0_attn_norm_w, L0_attn_Wo, L0_ffn_Wqkv, L0_ffn_q_scale, L0_ffn_k_scale, L0_ffn_Wo, L0_ffn_ln_g, L0_ffn_ln_b, L0_ffn_W1, L0_ffn_b1, L0_ffn_W2, L0_ffn_b2):

    def _L0_attn_ref(x, Wq, Wk, Wv, Wb, Wa, A_log, dt_bias, conv_q, conv_k, conv_v, Wg, norm_w, Wo):
        import jax, jax.numpy as jnp
        from jax import lax
        import numpy as np
        D = 128
        H = 6
        DK = 128
        DV = 32
        KD = H * DK
        VD = H * DV
        KS = 4
        EPS = 1e-05
        B, L = (2, 128)

        def _causal_conv_silu(x, w):
            xt = jnp.transpose(x, (0, 2, 1))
            out = lax.conv_general_dilated(xt, w[:, None, :], window_strides=(1,), padding=[(KS - 1, 0)], feature_group_count=w.shape[0])
            return jnp.transpose(jax.nn.silu(out), (0, 2, 1))

        def _l2norm(t):
            return t * lax.rsqrt(jnp.sum(t * t, axis=-1, keepdims=True) + 1e-12)

        def _reference_tuple_inner(x, Wq, Wk, Wv, Wb, Wa, A_log, dt_bias, conv_q, conv_k, conv_v, Wg, norm_w, Wo):
            Bc, Lc, _ = x.shape
            q = _causal_conv_silu(x @ Wq, conv_q).reshape(Bc, Lc, H, DK)
            k = _causal_conv_silu(x @ Wk, conv_k).reshape(Bc, Lc, H, DK)
            v = _causal_conv_silu(x @ Wv, conv_v).reshape(Bc, Lc, H, DV)
            beta = jax.nn.sigmoid(x @ Wb)
            g = -jnp.exp(A_log) * jax.nn.softplus(x @ Wa + dt_bias)
            q = _l2norm(q) * DK ** (-0.5)
            k = _l2norm(k)
            qt = jnp.moveaxis(q, 1, 0)
            kt = jnp.moveaxis(k, 1, 0)
            vt = jnp.moveaxis(v, 1, 0)
            gt = jnp.moveaxis(g, 1, 0)
            bt = jnp.moveaxis(beta, 1, 0)
            S0 = jnp.zeros((Bc, H, DK, DV), dtype=x.dtype)

            def step(S, inp):
                q_t, k_t, v_t, g_t, b_t = inp
                S = S * jnp.exp(g_t)[..., None, None]
                corr = jnp.einsum('bhk,bhkv->bhv', k_t, S)
                u = (v_t - corr) * b_t[..., None]
                S = S + k_t[..., None] * u[:, :, None, :]
                o_t = jnp.einsum('bhk,bhkv->bhv', q_t, S)
                return (S, o_t)
            S, o = lax.scan(step, S0, (qt, kt, vt, gt, bt))
            o = jnp.moveaxis(o, 0, 1)
            gate = (x @ Wg).reshape(Bc, Lc, H, DV)
            o = o * lax.rsqrt(jnp.mean(o * o, axis=-1, keepdims=True) + EPS)
            o = o * norm_w * jax.nn.silu(gate)
            o = o.reshape(Bc, Lc, VD) @ Wo
            return (o, S)
        return _reference_tuple_inner(x, Wq, Wk, Wv, Wb, Wa, A_log, dt_bias, conv_q, conv_k, conv_v, Wg, norm_w, Wo)[0]

    def _L0_ffn_ref(x, Wqkv, q_scale, k_scale, Wo, ln_g, ln_b, W1, b1, W2, b2):
        import jax, jax.numpy as jnp
        import numpy as np
        DIM = 128
        DEPTH = 6
        HEADS = 16
        DIM_HEAD = 64
        WINDOW = 32
        INNER = HEADS * DIM_HEAD
        DIM_INNER = int(DIM * 4 * 2 / 3)
        QK_SCALE = 8.0

        def shift_tokens(t):
            a, s = jnp.split(t, 2, -1)
            s = jnp.pad(s, ((0, 0), (1, 0), (0, 0)))[:, :-1]
            return jnp.concatenate([a, s], -1)

        def l2norm(t):
            return t / jnp.maximum(jnp.linalg.norm(t, axis=-1, keepdims=True), 1e-12)

        def rotate_half(x):
            x1, x2 = jnp.split(x, 2, -1)
            return jnp.concatenate([-x2, x1], -1)

        def rotary_tables(n):
            half = jnp.arange(0, DIM_HEAD, 2, dtype=jnp.float32)
            inv_freq = 1.0 / 10000.0 ** (half / DIM_HEAD)
            t = jnp.arange(n, dtype=jnp.float32)
            freqs = t[:, None] * inv_freq[None, :]
            freqs = jnp.concatenate([freqs, freqs], -1)
            base_scale = (half + 0.4 * DIM_HEAD) / (1.4 * DIM_HEAD)
            power = (t - n // 2) / (WINDOW // 2)
            scale = base_scale[None, :] ** power[:, None]
            scale = jnp.concatenate([scale, scale], -1)
            return (freqs, scale)

        def local_attention(q, k, v):
            b, h, n, d = q.shape
            w = WINDOW
            nw = n // w
            bq = q.reshape(b, h, nw, w, d)
            bk = k.reshape(b, h, nw, w, d)
            bv = v.reshape(b, h, nw, w, d)

            def look(t):
                p = jnp.pad(t, ((0, 0), (0, 0), (1, 0), (0, 0), (0, 0)))
                return jnp.concatenate([p[:, :, :nw], p[:, :, 1:]], axis=3)
            bk2, bv2 = (look(bk), look(bv))
            seq = jnp.arange(n).reshape(nw, w)
            seq_p = jnp.pad(seq, ((1, 0), (0, 0)), constant_values=-1)
            jt = jnp.concatenate([seq_p[:nw], seq_p[1:]], axis=1)
            it = seq[:, :, None]
            jb = jt[:, None, :]
            mask = (it < jb) | (it > jb + w) | (jb == -1)
            sim = jnp.einsum('bhwie,bhwje->bhwij', bq, bk2) * QK_SCALE
            sim = jnp.where(mask, -jnp.finfo(sim.dtype).max, sim)
            attn = jax.nn.softmax(sim, -1)
            out = jnp.einsum('bhwij,bhwje->bhwie', attn, bv2)
            return out.reshape(b, h, n, d)

        def attn_layer(x, Wqkv, qs, ksc, Wo):
            b, n, _ = x.shape
            qkv = x @ Wqkv
            q, k, v = jnp.split(qkv, 3, -1)
            sh = lambda t: t.reshape(b, n, HEADS, DIM_HEAD).transpose(0, 2, 1, 3)
            q, k, v = (sh(q), sh(k), sh(v))
            q = l2norm(q) * qs
            k = l2norm(k) * ksc
            freqs, scale = rotary_tables(n)
            cos, sin = (jnp.cos(freqs), jnp.sin(freqs))
            q = q * cos * scale + rotate_half(q) * sin * scale
            inv = 1.0 / scale
            k = k * cos * inv + rotate_half(k) * sin * inv
            out = local_attention(q, k, v)
            out = out.transpose(0, 2, 1, 3).reshape(b, n, INNER)
            return out @ Wo

        def ffn_layer(x, g, bln, W1, b1, W2, b2):
            mu = x.mean(-1, keepdims=True)
            var = ((x - mu) ** 2).mean(-1, keepdims=True)
            xn = (x - mu) / jnp.sqrt(var + 1e-05) * g + bln
            hg = xn @ W1 + b1
            a, gate = jnp.split(hg, 2, -1)
            return a * jax.nn.gelu(gate, approximate=False) @ W2 + b2
        for i in range(DEPTH):
            x = attn_layer(shift_tokens(x), Wqkv[i], q_scale[i], k_scale[i], Wo[i]) + x
            x = ffn_layer(shift_tokens(x), ln_g[i], ln_b[i], W1[i], b1[i], W2[i], b2[i]) + x
        return x
    x = L0_attn_x
    x = x + _L0_attn_ref(_layernorm(x, axis=-1), L0_attn_Wq, L0_attn_Wk, L0_attn_Wv, L0_attn_Wb, L0_attn_Wa, L0_attn_A_log, L0_attn_dt_bias, L0_attn_conv_q, L0_attn_conv_k, L0_attn_conv_v, L0_attn_Wg, L0_attn_norm_w, L0_attn_Wo)
    x = x + _L0_ffn_ref(_layernorm(x, axis=-1), L0_ffn_Wqkv, L0_ffn_q_scale, L0_ffn_k_scale, L0_ffn_Wo, L0_ffn_ln_g, L0_ffn_ln_b, L0_ffn_W1, L0_ffn_b1, L0_ffn_W2, L0_ffn_b2)
    return x

_drawn_inputs = setup_inputs


def setup_inputs(seed=0):
    import zlib

    import numpy as np

    out = dict(_drawn_inputs(seed))
    spreads = {'L0_attn_norm_w': (1.0, 0.6),
     'L0_ffn_q_scale': (1.0, 0.6),
     'L0_ffn_k_scale': (1.0, 0.6),
     'L0_ffn_ln_g': (1.0, 0.6),
     'L0_ffn_ln_b': (0.0, 0.8),
     'L0_ffn_b1': (0.0, 0.8),
     'L0_ffn_b2': (0.0, 0.1)}
    factors = {'L0_attn_Wq': 5.727,
     'L0_attn_Wk': 5.728,
     'L0_attn_Wv': 5.675,
     'L0_attn_Wb': 8.0,
     'L0_attn_Wa': 24.947,
     'L0_attn_A_log': 8.0,
     'L0_attn_dt_bias': 8.0,
     'L0_attn_conv_q': 5.723,
     'L0_attn_conv_k': 5.522,
     'L0_attn_conv_v': 5.5,
     'L0_attn_Wg': 5.772,
     'L0_attn_Wo': 5.655,
     'L0_ffn_W1': 3.639,
     'L0_ffn_W2': 3.574}
    for name, (base, spread) in spreads.items():
        noise = np.random.default_rng([zlib.crc32(name.encode()), seed]).standard_normal(out[name].shape)
        drawn = base * np.exp(spread * noise) if base else spread * noise
        out[name] = jnp.asarray(drawn.astype(out[name].dtype))
    for name, factor in factors.items():
        out[name] = (out[name] * factor).astype(out[name].dtype)
    return out
```

```python
from contextlib import ExitStack

import numpy as np

import concourse.bass as bass
from concourse import mybir

ALU = mybir.AluOpType
ACT = mybir.ActivationFunctionType
AX = mybir.AxisListType
F32 = mybir.dt.float32
BF16 = mybir.dt.bfloat16

P = 128
NB = 4
L = 1024
NT = L // P
C = NB * P
EPS = 1e-5

H1, DV, KS = 6, 32, 4
VD = H1 * DV
NQK = 2 * H1
NCH = NQK + 2
GW = VD + 2 * H1
LEVELS = 7
ATANH_TERMS = 9

DEPTH, HEADS, DH, WIN = 6, 16, 64, 32
INNER = HEADS * DH
NP2 = HEADS // 2
FF = 341
FC = 3
FROWS = [P, P, FF - 2 * P]
KX = WIN + P
NW = P // WIN
QK_SCALE = 8.0
MASKED = -1e30
LN_EXP = "natural_log_exp_and_others"
LN_SHIFT = 20

W_Q, W_K, W_V = 0, INNER, 2 * INNER
W_QR, W_KR = 3 * INNER, 4 * INNER
W_1 = 5 * INNER
W_O = W_1 + 2 * FF
W_2 = W_O + NP2 * P
W_VEC = W_2 + FC * P
V_G, V_B, V_A, V_GATE, V_B2, V_ROT = 0, 1, 2, 5, 8, 9
WCOLS = W_VEC + 13

M_ID, M_LE, M_GT, M_MEAN, M_ONES, M_HEADS, M_OFF = 0, 1, 2, 3, 4, 5, 6
NM = M_OFF + 2 * LEVELS


def linker(eng, sem):
    count = [0]

    def link(ins):
        count[0] += 1
        ins.then_inc(sem, 1)
        eng.wait_ge(sem, count[0])

    return link


def over_batches(ap, n=NB):
    return ap.unsqueeze(1).to_broadcast([ap.shape[0], n, ap.shape[1]])


def along(ap, m):
    return ap.unsqueeze(2).to_broadcast([ap.shape[0], ap.shape[1], m])


def blocks(ap, n=NB):
    return ap.rearrange("p (b n) -> p b n", b=n)


def build(nc, x, w1, conv, wo1, rows1, masks, key_mask, rot, weights, out, x1_dram):
    with ExitStack() as whole:
        def names(*words):
            return [whole.enter_context(nc.semaphore(w)) for w in words]

        def sbuf(ctx, name, shape, dt=F32):
            return ctx.enter_context(nc.sbuf_tensor(name, shape, dt))

        bank = [whole.enter_context(nc.psum_tensor(f"bank{i}", [P, 512], F32)) for i in range(4)]
        qq = whole.enter_context(nc.psum_tensor("qq", [P, 2, 512], F32))
        kk = whole.enter_context(nc.psum_tensor("kk", [P, 2, 512], F32))
        p = bank + [qq[:, 0, :], qq[:, 1, :], kk[:, 0, :], kk[:, 1, :]]
        p = [bank[0][:], bank[1][:], bank[2][:], bank[3][:]] + p[4:]

        y = sbuf(whole, "y", [P, NB, L])
        msk = sbuf(whole, "msk", [P, NM, P])
        cst = sbuf(whole, "cst", [P, 8])
        ident = msk[:, M_ID, :]
        ones = msk[:, M_ONES, :]
        C_EPS, C_L2, C_QSC, C_ZERO, C_NORM, C_NSC = range(6)

        def c(i):
            return cst[:, i:i + 1]

        load_done, init_done = names("load_done", "init_done")
        delta_layer(nc, sbuf, names, p, y, msk, ident, ones, cst, c,
                    (C_EPS, C_L2, C_QSC, C_ZERO, C_NORM, C_NSC), load_done, init_done,
                    x, w1, conv, wo1, rows1, masks, x1_dram)
        local_layers(nc, sbuf, names, p, bank, qq, kk, y, msk, ident, c,
                     (C_EPS, C_ZERO, C_NORM, C_NSC), key_mask, rot, weights)
        final_sum(nc, sbuf, names, p, y, ident, x1_dram, out)


def delta_layer(nc, sbuf, names, p, y, msk, ident, ones, cst, c, cols, load_done, init_done,
                x, w1, conv, wo1, rows1, masks, x1_dram):
    C_EPS, C_L2, C_QSC, C_ZERO, C_NORM, C_NSC = cols
    le, gt, mean_m = msk[:, M_LE, :], msk[:, M_GT, :], msk[:, M_MEAN, :]
    with ExitStack() as ctx:
        def sb(name, shape, dt=F32):
            return sbuf(ctx, name, shape, dt)

        w = sb("w1s", [P, NQK * P + VD + GW])
        cw = sb("cw", [P, NCH, KS])
        wo = sb("wo1s", [P, 2, P])
        rows = sb("rows", [P, 2 * H1 + DV])
        neg_a = sb("neg_a", [P, H1])
        pre = sb("pre", [P, NCH, NB, KS - 1 + P])
        act_qkv = sb("act_qkv", [P, NCH, C])
        state = sb("state", [P, H1, NB, DV])
        xin = sb("xin", [P, NB, P])
        xt = sb("xt", [P, C])
        xc = sb("xc", [P, C])
        xn = sb("xn", [P, C])
        sq = sb("sq", [P, 2, C])
        lg = sb("lg", [P, 2, C])
        rs = sb("rs", [P, 2, C])
        cv = sb("cv", [P, 2, C])
        vt = sb("vt", [P, NB, VD])
        sg = sb("sg", [P, NB, VD])
        ba = sb("ba", [P, NB, 2 * H1])
        t24 = sb("t24", [P, 12, NB, H1])
        ex = sb("ex", [P, 3, NB, H1])
        gm = sb("gm", [P, 2, NB, P])
        gam = sb("gam", [P, 2, NB, P])
        gat = sb("gat", [P, 2, NB, P])
        am = sb("am", [P, NB, P])
        at = sb("at", [P, NB, P])
        tmp = sb("tmp", [P, NB, P])
        pm = sb("pm", [P, 2, NB, P])
        kt = sb("kt", [P, 2, NB, P])
        ao = sb("ao", [P, 2, NB, P])
        tt = sb("tt", [P, NB, P])
        tr = sb("tr", [P, NB, P])
        p1 = sb("p1", [P, NB, P])
        r1 = sb("r1", [P, 3, NB, DV])
        u = sb("u", [P, 2, NB, DV])
        o = sb("o", [P, NB, VD])
        o2 = sb("o2", [P, NB, DV])
        ot = sb("ot", [P, 2, C])
        osq = sb("osq", [P, NB, VD])
        om = sb("om", [P, 4, NB * H1])
        x1 = sb("x1", [P, C])

        dve_step, act_step, pool_step = names("dve_step", "act_step", "pool_step")
        (x_loaded, x_turned, xt_ready, mean_ready, xc_ready, lnsq_ready, var_ready, rstd_ready,
         xn_ready, proj_ready, pre_ready, conv_ready, silu_ready, gates_ready, gates_taken,
         sq_ready, ss_ready, rn_ready, qk_ready) = names(
            "x_loaded", "x_turned", "xt_ready", "mean_ready", "xc_ready", "lnsq_ready", "var_ready",
            "rstd_ready", "xn_ready", "proj_ready", "pre_ready", "conv_ready", "silu_ready",
            "gates_ready", "gates_taken", "sq_ready", "ss_ready", "rn_ready", "qk_ready")
        (v_turned, v_ready, e1_asked, e1_ready, g_ready, cum_ready, cum_exp, gm_ready, decay_ready,
         decay_exp, kk_ready, a_ready, a_turned, at_ready, t_ready, ao_ready, p1_ready, p1_taken,
         delta_ready, tri_ready, ktok_ready, kt_ready, pm_ready) = names(
            "v_turned", "v_ready", "e1_asked", "e1_ready", "g_ready", "cum_ready", "cum_exp",
            "gm_ready", "decay_ready", "decay_exp", "kk_ready", "a_ready", "a_turned", "at_ready",
            "t_ready", "ao_ready", "p1_ready", "p1_taken", "delta_ready", "tri_ready", "ktok_ready",
            "kt_ready", "pm_ready")
        (ks_ready, r_ready, u_ready, u_taken, o_ready, s_ready, o_done, om_ready, ostd_ready,
         on_ready, on_turned, ot_ready, wo_ready, x1_ready, x1_stored) = names(
            "ks_ready", "r_ready", "u_ready", "u_taken", "o_ready", "s_ready", "o_done", "om_ready",
            "ostd_ready", "on_ready", "on_turned", "ot_ready", "wo_ready", "x1_ready", "x1_stored")

        with nc.Block() as block:
            @block.sync
            def _(sp):
                for dst, src in ((w[:], w1), (cw[:], conv), (wo[:], wo1), (msk[:], masks),
                                 (rows[:], rows1.partition_broadcast(P))):
                    sp.dma_start(dst, src).then_inc(load_done, 16)
                sp.wait_ge(load_done, 5 * 16)

            @block.vector
            def _(v):
                for i, value in ((C_EPS, EPS), (C_L2, 1e-12), (C_QSC, -0.5 * float(np.log(P))),
                                 (C_ZERO, 0.0), (C_NORM, 1e-24 * 2.0 ** LN_SHIFT),
                                 (C_NSC, 0.5 * LN_SHIFT * float(np.log(2.0)))):
                    v.memset(c(i), value)
                v.memset(pre[:], 0.0)
                v.memset(act_qkv[:], 0.0)
                v.memset(cv[:], 0.0)
                v.memset(state[:], 0.0).then_inc(init_done, 1)
                v.wait_ge(init_done, 1)
                v.wait_ge(init_done, 2)
                v.tensor_scalar(neg_a[:], neg_a[:], -1.0, None, ALU.mult).then_inc(init_done, 1)
                v.wait_ge(init_done, 3)

            @block.scalar
            def _(a):
                a.wait_ge(load_done, 5 * 16)
                a.wait_ge(init_done, 1)
                a.activation(neg_a[:], rows[:, 0:H1], ACT.Exp).then_inc(init_done, 1)
                a.wait_ge(init_done, 3)

        first = dve_step.num
        with nc.Fori(0, NT) as t:
            with nc.Block(no_gpsimd_drain=True) as block:
                @block.sync
                def _(sp):
                    sp.dma_start(xin[:], x[:, bass.ds(t * P, P), :].rearrange("b p d -> p b d"))\
                        .then_inc(x_loaded, 16)
                    sp.wait_ge(x_loaded, 16)
                    sp.wait_ge(x1_ready, 1)
                    sp.dma_start(x1_dram[:, :, bass.ds(t * P, P)], blocks(x1[:])).then_inc(x1_stored, 16)
                    sp.wait_ge(x1_stored, 16)

                @block.tensor
                def _(pe):
                    pe.wait_ge(x_loaded, 16)
                    for b in range(NB):
                        last = pe.transpose(p[0][:, b * P:(b + 1) * P], xin[:, b, :], ident)
                    last.then_inc(x_turned, 1)
                    pe.wait_ge(xt_ready, 1)
                    pe.matmul(p[1], mean_m, xt[:], start=True, stop=True).then_inc(mean_ready, 1)
                    pe.wait_ge(lnsq_ready, 1)
                    pe.matmul(p[0], mean_m, sq[:, 0, :], start=True, stop=True).then_inc(var_ready, 1)
                    pe.wait_ge(xn_ready, 1)
                    for n in range(NCH):
                        m = P if n < NCH - 1 else VD - P
                        if n >= 4:
                            pe.wait_ge(pre_ready, n - 3)
                        pe.matmul(p[n % 4][0:m, :], w[:, n * P:n * P + m], xn[:], start=True, stop=True)\
                            .then_inc(proj_ready, 1)
                    for b in range(NB):
                        last = pe.matmul(p[4 + b // 2][:, (b % 2) * GW:(b % 2 + 1) * GW],
                                         xn[:, b * P:(b + 1) * P], w[:, NQK * P + VD:NQK * P + VD + GW],
                                         start=True, stop=True)
                    last.then_inc(gates_ready, 1)
                    pe.wait_ge(pre_ready, NCH)
                    for n in range(NQK):
                        pe.wait_ge(sq_ready, n + 1)
                        if n >= 2:
                            pe.wait_ge(rn_ready, n - 1)
                        pe.matmul(p[n % 2], ones, sq[:, n % 2, :], start=True, stop=True)\
                            .then_inc(ss_ready, 1)
                    pe.wait_ge(silu_ready, NCH)
                    for b in range(NB):
                        at_b = p[6 + b // 2][:, (b % 2) * VD:(b % 2 + 1) * VD]
                        pe.transpose(at_b[:, 0:P], act_qkv[:, NQK, b * P:(b + 1) * P], ident)
                        last = pe.transpose(at_b[:, P:VD], act_qkv[0:VD - P, NQK + 1, b * P:(b + 1) * P],
                                            ident[0:VD - P, 0:VD - P])
                    last.then_inc(v_turned, 1)
                    pe.wait_ge(g_ready, 1)
                    pe.wait_ge(gates_taken, 2)
                    g = t24[:, 0, :, :].rearrange("p b h -> p (b h)")
                    for i, m in enumerate((le, gt, ones)):
                        last = pe.matmul(p[5][:, i * NB * H1:(i + 1) * NB * H1], m, g, start=True, stop=True)
                    last.then_inc(cum_ready, 1)
                    pe.wait_ge(rn_ready, NQK)
                    pe.wait_ge(v_ready, 2)
                    pe.wait_ge(cum_exp, 1)

                    def products(h):
                        pe.wait_ge(gm_ready, h + 1)
                        if h:
                            pe.wait_ge(decay_exp, h)
                            pe.wait_ge(a_ready, h)
                            pe.wait_ge(pm_ready, h)
                        pe.wait_ge(qk_ready, NQK)
                        for b in range(NB):
                            s = slice(b * P, (b + 1) * P)
                            pe.matmul(p[0][:, s], gm[:, h % 2, b, :], le, start=True, stop=True)
                            last = pe.matmul(p[1][:, s], le, gm[:, h % 2, b, :], start=True, stop=True)
                        last.then_inc(decay_ready, 1)
                        for b in range(NB):
                            s = slice(b * P, (b + 1) * P)
                            k_b, q_b = act_qkv[:, H1 + h, s], act_qkv[:, h, s]
                            pe.matmul(p[2][:, s], k_b, k_b, start=True, stop=True)
                            last = pe.matmul(p[3][:, s], k_b, q_b, start=True, stop=True)
                        last.then_inc(kk_ready, 1)

                    products(0)
                    for h in range(H1):
                        pe.wait_ge(a_ready, h + 1)
                        if h:
                            pe.wait_ge(kt_ready, h)
                        for b in range(NB):
                            last = pe.transpose(p[4][:, b * P:(b + 1) * P], am[:, b, :], ident)
                        last.then_inc(a_turned, 1)
                        pe.wait_ge(at_ready, h + 1)
                        for b in range(NB):
                            last = pe.transpose(p[4][:, b * P:(b + 1) * P],
                                                act_qkv[:, H1 + h, b * P:(b + 1) * P], ident)
                        last.then_inc(ktok_ready, 1)
                        for i in range(1, LEVELS):
                            n = h * (LEVELS - 1) + i
                            pe.wait_ge(t_ready, n)
                            pe.wait_ge(ao_ready, n)
                            if i == 1 and h:
                                pe.wait_ge(r_ready, h)
                            for b in range(NB):
                                last = pe.matmul(p[5][:, b * P:(b + 1) * P], ao[:, i % 2, b, :],
                                                 tr[:, b, :], start=True, stop=True)
                            last.then_inc(p1_ready, 1)
                            if i == 2 and h + 1 < H1:
                                products(h + 1)
                            pe.wait_ge(p1_taken, n)
                            if i == 1 and h:
                                pe.wait_ge(u_taken, h)
                                pe.wait_ge(s_ready, h)
                            if i < LEVELS - 1:
                                for b in range(NB):
                                    last = pe.matmul(p[6][:, b * P:(b + 1) * P], tt[:, b, :],
                                                     p1[:, b, :], start=True, stop=True)
                            for b in range(NB):
                                last = pe.matmul(p[7][:, b * P:(b + 1) * P], p1[:, b, :],
                                                 tt[:, b, :], start=True, stop=True)
                            last.then_inc(delta_ready, 1)
                        for b in range(NB):
                            s = slice(b * P, (b + 1) * P)
                            pe.matmul(p[5][:, b * DV:(b + 1) * DV], act_qkv[:, H1 + h, s],
                                      state[:, h, b, :], start=True, stop=True)
                            last = pe.matmul(p[5][:, P + b * DV:P + (b + 1) * DV], act_qkv[:, h, s],
                                             state[:, h, b, :], start=True, stop=True)
                        last.then_inc(ks_ready, 1)
                        pe.wait_ge(tri_ready, h + 1)
                        pe.wait_ge(r_ready, h + 1)
                        for b in range(NB):
                            last = pe.matmul(p[6][:, b * DV:(b + 1) * DV], tt[:, b, :], r1[:, 2, b, :],
                                             start=True, stop=True)
                        last.then_inc(u_ready, 1)
                        pe.wait_ge(u_taken, h + 1)
                        pe.wait_ge(kt_ready, h + 1)
                        pe.wait_ge(pm_ready, h + 1)
                        for b in range(NB):
                            pe.matmul(p[7][:, b * DV:(b + 1) * DV], pm[:, h % 2, b, :], u[:, 0, b, :],
                                      start=True, stop=True)
                            last = pe.matmul(p[7][:, P + b * DV:P + (b + 1) * DV], kt[:, h % 2, b, :],
                                             u[:, 1, b, :], start=True, stop=True)
                        last.then_inc(o_ready, 1)
                    pe.wait_ge(on_ready, 1)
                    for b in range(NB):
                        pe.transpose(p[0][:, b * P:(b + 1) * P], o[:, b, 0:P], ident)
                        last = pe.transpose(p[1][0:VD - P, b * P:(b + 1) * P], o[:, b, P:VD], ident)
                    last.then_inc(on_turned, 1)
                    pe.wait_ge(ot_ready, 2)
                    pe.matmul(p[2], wo[:, 0, :], ot[:, 0, :], start=True, stop=False)
                    pe.matmul(p[2], wo[0:VD - P, 1, :], ot[0:VD - P, 1, :], start=False, stop=True)\
                        .then_inc(wo_ready, 1)
                    pe.wait_ge(x1_ready, 1)
                    pe.matmul(p[3], mean_m, x1[:], start=True, stop=True).then_inc(mean_ready, 1)
                    pe.wait_ge(lnsq_ready, 2)
                    pe.matmul(p[4], mean_m, sq[:, 0, :], start=True, stop=True).then_inc(var_ready, 1)
                    pe.wait_ge(var_ready, 2)

                @block.scalar
                def _(a):
                    link = linker(a, act_step)

                    def rstd(n, bank_of_var):
                        a.wait_ge(xc_ready, n)
                        a.activation(sq[:, 0, :], xc[:], ACT.Square).then_inc(lnsq_ready, 1)
                        a.wait_ge(var_ready, n)
                        link(a.activation(lg[:, 0, :], bank_of_var, ACT.Ln, bias=c(C_EPS)))
                        a.activation(rs[:, 0, :], lg[:, 0, :], ACT.Exp, scale=-0.5).then_inc(rstd_ready, 1)
                        a.wait_ge(rstd_ready, n)

                    a.preload_act_table_set(LN_EXP)
                    a.wait_ge(x_turned, 1)
                    a.activation(xt[:], p[0], ACT.Copy).then_inc(xt_ready, 1)
                    rstd(1, p[0])

                    def take(n):
                        m = P if n < NCH - 1 else VD - P
                        a.wait_ge(proj_ready, n + 1)
                        a.activation(pre[0:m, n, :, KS - 1:], blocks(p[n % 4][0:m, :]), ACT.Copy)\
                            .then_inc(pre_ready, 1)

                    def silu(n):
                        a.wait_ge(conv_ready, n + 1)
                        a.activation(act_qkv[:, n, :], cv[:, n % 2, :], ACT.Silu).then_inc(silu_ready, 1)

                    for n in range(NCH + 2):
                        if n < NCH:
                            take(n)
                        if n >= 2:
                            silu(n - 2)
                    a.wait_ge(gates_ready, 1)
                    for i in range(2):
                        src = p[4 + i][:, 0:2 * GW].rearrange("p (b n) -> p b n", b=2)
                        a.activation(sg[:, 2 * i:2 * i + 2, :], src[:, :, 0:VD], ACT.Silu)\
                            .then_inc(gates_taken, 1)
                    a.wait_ge(silu_ready, NCH)
                    a.preload_act_table_set(LN_EXP)
                    a.wait_ge(e1_asked, 1)
                    for i in (3, 4, 5):
                        a.activation(t24[:, i + 3, :, :], t24[:, i, :, :], ACT.Exp).then_inc(e1_ready, 1)
                    for n in range(NQK + 1):
                        if n < NQK:
                            if n >= 2:
                                a.wait_ge(ss_ready, n - 1)
                            a.activation(sq[:, n % 2, :], act_qkv[:, n, :], ACT.Square).then_inc(sq_ready, 1)
                        if n >= 1:
                            m = n - 1
                            a.wait_ge(ss_ready, m + 1)
                            link(a.activation(lg[:, m % 2, :], p[m % 2], ACT.Ln, bias=c(C_L2)))
                            if m >= 2:
                                a.wait_ge(qk_ready, m - 1)
                            a.activation(rs[:, m % 2, :], lg[:, m % 2, :], ACT.Exp, scale=-0.5,
                                         bias=c(C_QSC) if m < H1 else c(C_ZERO)).then_inc(rn_ready, 1)
                    a.wait_ge(v_turned, 1)
                    for i in range(2):
                        a.activation(vt[:, 2 * i:2 * i + 2, :],
                                     p[6 + i][:, 0:2 * VD].rearrange("p (b n) -> p b n", b=2), ACT.Copy)\
                            .then_inc(v_ready, 1)
                    a.wait_ge(cum_ready, 1)
                    a.activation(ex[:].rearrange("p i b h -> p (i b h)"), p[5][:, 0:3 * NB * H1], ACT.Exp)\
                        .then_inc(cum_exp, 1)

                    def decays(h):
                        a.wait_ge(decay_ready, h + 1)
                        if h >= 2:
                            a.wait_ge(pm_ready, h - 1)
                        link(a.activation(gat[:, h % 2, :, :], blocks(p[0]), ACT.Exp))
                        a.activation(gam[:, h % 2, :, :], blocks(p[1]), ACT.Exp).then_inc(decay_exp, 1)
                        a.wait_ge(decay_exp, h + 1)

                    decays(0)
                    for h in range(H1):
                        a.wait_ge(a_turned, h + 1)
                        if h:
                            a.wait_ge(ao_ready, h * (LEVELS - 1))
                        a.activation(at[:], blocks(p[4]), ACT.Copy).then_inc(at_ready, 1)
                        a.wait_ge(ktok_ready, h + 1)
                        a.activation(kt[:, h % 2, :, :], blocks(p[4]), ACT.Copy).then_inc(kt_ready, 1)
                        for i in range(1, LEVELS):
                            n = h * (LEVELS - 1) + i
                            a.wait_ge(p1_ready, n)
                            if n > 1:
                                a.wait_ge(delta_ready, n - 1)
                            a.activation(p1[:], blocks(p[5]), ACT.Copy).then_inc(p1_taken, 1)
                            if i == 2 and h + 1 < H1:
                                decays(h + 1)
                    a.wait_ge(om_ready, 1)
                    link(a.activation(om[:, 1, :], om[:, 0, :], ACT.Ln, scale=1.0 / DV, bias=c(C_EPS)))
                    a.activation(om[:, 2, :], om[:, 1, :], ACT.Exp, scale=-0.5).then_inc(ostd_ready, 1)
                    a.wait_ge(on_turned, 1)
                    a.activation(ot[:, 0, :], p[0], ACT.Copy).then_inc(ot_ready, 1)
                    a.activation(ot[0:VD - P, 1, :], p[1][0:VD - P, :], ACT.Copy).then_inc(ot_ready, 1)
                    a.wait_ge(ot_ready, 2)
                    rstd(2, p[4])

                @block.gpsimd
                def _(g):
                    for h in range(H1):
                        g.wait_ge(at_ready, h + 1)
                        for i in range(1, LEVELS):
                            n = h * (LEVELS - 1) + i
                            if n > 2:
                                g.wait_ge(p1_ready, n - 2)
                            g.tensor_tensor(ao[:, i % 2, :, :], at[:],
                                            over_batches(msk[:, M_OFF + LEVELS + i, :]), ALU.mult)\
                                .then_inc(ao_ready, 1)
                    g.wait_ge(ao_ready, H1 * (LEVELS - 1))

                @block.vector
                def _(v):
                    link = linker(v, dve_step)

                    def done(ins, sem, n):
                        ins.then_inc(sem, 1)
                        v.wait_ge(sem, n)

                    def layer_norm(n, src, bank_of_mean, dst):
                        v.wait_ge(mean_ready, n)
                        ins = v.tensor_tensor(xc[:], src, bank_of_mean, ALU.subtract)
                        ins.then_inc(xc_ready, 1)
                        v.wait_ge(xc_ready, n)
                        v.wait_ge(rstd_ready, n)
                        ins = v.tensor_tensor(dst, blocks(xc[:]), blocks(rs[:, 0, :]), ALU.mult)
                        ins.then_inc(xn_ready, 1)
                        v.wait_ge(xn_ready, n)

                    layer_norm(1, xt[:], p[1], blocks(xn[:]))
                    for n in range(NCH):
                        m = P if n < NCH - 1 else VD - P
                        v.wait_ge(pre_ready, n + 1)
                        if n >= 2:
                            v.wait_ge(silu_ready, n - 1)
                        dst = blocks(cv[0:m, n % 2, :])
                        link(v.tensor_scalar(dst, pre[0:m, n, :, 0:P], cw[0:m, n, 0:1], None, ALU.mult))
                        for s in range(1, KS):
                            ins = v.scalar_tensor_tensor(dst, pre[0:m, n, :, s:s + P], cw[0:m, n, s:s + 1],
                                                         dst, ALU.mult, ALU.add)
                            if s < KS - 1:
                                link(ins)
                        ins.then_inc(conv_ready, 1)
                        v.wait_ge(conv_ready, n + 1)
                    link(v.tensor_copy(pre[:, :, :, 0:KS - 1], pre[:, :, :, P:P + KS - 1]))
                    v.wait_ge(gates_ready, 1)
                    v.wait_ge(gates_taken, 2)
                    for i in range(2):
                        src = p[4 + i][:, 0:2 * GW].rearrange("p (b n) -> p b n", b=2)
                        link(v.tensor_copy(ba[:, 2 * i:2 * i + 2, :], src[:, :, VD:GW]))
                    beta, dec = ba[:, :, 0:H1], ba[:, :, H1:2 * H1]
                    G, BETA, POS, NB_ABS, NB_MIN, ND_ABS, E_B, E_BM, E_D, S1, S2, T = \
                        [t24[:, i, :, :] for i in range(12)]
                    link(v.tensor_tensor(dec, dec, over_batches(rows[:, H1:2 * H1]), ALU.add))
                    for dst, src in ((NB_ABS, beta), (ND_ABS, dec)):
                        link(v.tensor_scalar(T, src, -1.0, None, ALU.mult))
                        link(v.tensor_tensor(dst, T, src, ALU.min))
                    link(v.tensor_scalar(POS, dec, 0.0, None, ALU.max))
                    done(v.tensor_scalar(NB_MIN, beta, 0.0, None, ALU.min), e1_asked, 1)
                    v.wait_ge(e1_ready, 3)
                    link(v.tensor_scalar(T, E_B, 1.0, None, ALU.add))
                    link(v.reciprocal(S1, T))
                    link(v.tensor_tensor(BETA, S1, E_BM, ALU.mult))
                    link(v.tensor_scalar(T, E_D, 2.0, None, ALU.add))
                    link(v.reciprocal(S2, T))
                    link(v.tensor_tensor(S1, S2, E_D, ALU.mult))
                    link(v.tensor_tensor(S2, S1, S1, ALU.mult))
                    link(v.tensor_scalar(T, S2, 2.0 / (2 * ATANH_TERMS + 1), 2.0 / (2 * ATANH_TERMS - 1),
                                         ALU.mult, ALU.add))
                    for i in range(ATANH_TERMS - 2, -1, -1):
                        link(v.tensor_tensor(T, T, S2, ALU.mult))
                        link(v.tensor_scalar(T, T, 2.0 / (2 * i + 1), None, ALU.add))
                    link(v.tensor_tensor(T, T, S1, ALU.mult))
                    link(v.tensor_tensor(T, T, POS, ALU.add))
                    done(v.tensor_tensor(G, T, over_batches(neg_a[:]), ALU.mult), g_ready, 1)
                    for n in range(NQK):
                        v.wait_ge(rn_ready, n + 1)
                        done(v.tensor_tensor(act_qkv[:, n, :], act_qkv[:, n, :], rs[:, n % 2, :], ALU.mult),
                             qk_ready, n + 1)

                    def masked_decay(h):
                        if h >= 2:
                            v.wait_ge(decay_ready, h - 1)
                        for b in range(NB):
                            ins = v.tensor_scalar(gm[:, h % 2, b, :], gt, t24[:, 0, b, h:h + 1], None, ALU.mult)
                            if b < NB - 1:
                                link(ins)
                        done(ins, gm_ready, h + 1)

                    masked_decay(0)
                    v.wait_ge(cum_exp, 1)
                    for h in range(H1):
                        n0 = h * (LEVELS - 1)
                        v.wait_ge(kk_ready, h + 1)
                        v.wait_ge(decay_exp, h + 1)
                        if h:
                            v.wait_ge(a_turned, h)
                        link(v.tensor_tensor(gam[:, h % 2, :, :], gam[:, h % 2, :, :], over_batches(gt), ALU.mult))
                        for b in range(NB):
                            ins = v.scalar_tensor_tensor(am[:, b, :], p[2][:, b * P:(b + 1) * P],
                                                         t24[:, 1, b, h:h + 1], gam[:, h % 2, b, :],
                                                         ALU.mult, ALU.mult)
                            if b < NB - 1:
                                link(ins)
                        done(ins, a_ready, h + 1)
                        link(v.tensor_tensor(pm[:, h % 2, :, :], gat[:, h % 2, :, :], over_batches(le), ALU.mult))
                        done(v.tensor_tensor(pm[:, h % 2, :, :], pm[:, h % 2, :, :], blocks(p[3]), ALU.mult),
                             pm_ready, h + 1)
                        if h:
                            v.wait_ge(u_ready, h)
                        link(v.tensor_tensor(tmp[:], am[:], over_batches(msk[:, M_OFF, :]), ALU.mult))
                        link(v.tensor_tensor(tr[:], over_batches(ident), tmp[:], ALU.subtract))
                        v.wait_ge(at_ready, h + 1)
                        link(v.tensor_tensor(tmp[:], at[:], over_batches(msk[:, M_OFF + LEVELS, :]), ALU.mult))
                        done(v.tensor_tensor(tt[:], over_batches(ident), tmp[:], ALU.subtract), t_ready, n0 + 1)
                        if h + 1 < H1:
                            masked_decay(h + 1)
                        for i in range(1, LEVELS):
                            v.wait_ge(delta_ready, n0 + i)
                            if i < LEVELS - 1:
                                link(v.tensor_tensor(tr[:], tr[:], blocks(p[6]), ALU.subtract))
                                done(v.tensor_tensor(tt[:], tt[:], blocks(p[7]), ALU.subtract),
                                     t_ready, n0 + i + 1)
                            else:
                                done(v.tensor_tensor(tt[:], tt[:], blocks(p[7]), ALU.subtract),
                                     tri_ready, h + 1)
                        v.wait_ge(ks_ready, h + 1)
                        ks, qs = blocks(p[5][:, 0:P]), blocks(p[5][:, P:2 * P])
                        link(v.tensor_tensor(r1[:, 0, :, :], ks, along(ex[:, 0, :, h], DV), ALU.mult))
                        link(v.tensor_tensor(o2[:], qs, along(ex[:, 0, :, h], DV), ALU.mult))
                        link(v.tensor_tensor(r1[:, 1, :, :], vt[:, :, h * DV:(h + 1) * DV], r1[:, 0, :, :],
                                             ALU.subtract))
                        done(v.tensor_tensor(r1[:, 2, :, :], r1[:, 1, :, :], along(t24[:, 1, :, h], DV),
                                             ALU.mult), r_ready, h + 1)
                        v.wait_ge(u_ready, h + 1)
                        ups = blocks(p[6][:, 0:P])
                        link(v.tensor_copy(u[:, 0, :, :], ups))
                        done(v.tensor_tensor(u[:, 1, :, :], ups, along(ex[:, 1, :, h], DV), ALU.mult),
                             u_taken, h + 1)
                        v.wait_ge(o_ready, h + 1)
                        link(v.tensor_tensor(o[:, :, h * DV:(h + 1) * DV], o2[:], blocks(p[7][:, 0:P]), ALU.add))
                        link(v.tensor_tensor(state[:, h, :, :], state[:, h, :, :], along(ex[:, 2, :, h], DV),
                                             ALU.mult))
                        done(v.tensor_tensor(state[:, h, :, :], state[:, h, :, :], blocks(p[7][:, P:2 * P]),
                                             ALU.add), s_ready, h + 1)
                    flat = "p b (h d) -> p (b h) d"
                    link(v.tensor_tensor(osq[:], o[:], o[:], ALU.mult))
                    done(v.tensor_reduce(om[:, 0, :], osq[:].rearrange(flat, h=H1), AX.X, ALU.add), om_ready, 1)
                    link(v.tensor_tensor(sg[:].rearrange(flat, h=H1), sg[:].rearrange(flat, h=H1),
                                         over_batches(rows[:, 2 * H1:2 * H1 + DV], NB * H1), ALU.mult))
                    v.wait_ge(ostd_ready, 1)
                    link(v.tensor_tensor(o[:].rearrange(flat, h=H1), o[:].rearrange(flat, h=H1),
                                         along(om[:, 2, :], DV), ALU.mult))
                    done(v.tensor_tensor(o[:], o[:], sg[:], ALU.mult), on_ready, 1)
                    v.wait_ge(wo_ready, 1)
                    done(v.tensor_tensor(x1[:], p[2], xt[:], ALU.add), x1_ready, 1)
                    layer_norm(2, x1[:], p[3], y[:, :, bass.ds(t * P, P)])
            nc.all_engine_barrier(sems_to_clear=range(first, x1_stored.num + 1))


def local_layers(nc, sbuf, names, p, bank, qq, kk, y, msk, ident, c, cols, key_mask, rot, weights):
    C_EPS, C_ZERO, C_NORM, C_NSC = cols
    mean_m, heads_m = msk[:, M_MEAN, :], msk[:, M_HEADS, :]
    norm_bank, out_bank, sc = bank[0][:], bank[1][:], [bank[2], bank[3]]
    with ExitStack() as ctx:
        def sb(name, shape, dt=F32):
            return sbuf(ctx, name, shape, dt)

        w = sb("w2s", [P, WCOLS])
        tab = sb("tab", [P, NT, 4, P])
        kmask = sb("kmask", [P, NT, 2 * WIN], BF16)
        idb = sb("idb", [P, P], BF16)
        flag = sb("flag", [P, NT])
        kx = sb("kx", [P, NP2, NB, KX])
        v_tok = sb("v_tok", [P, NB, INNER])
        v_before = sb("v_before", [WIN, NB, INNER])
        yt = sb("yt", [P, NB, 1 + P])
        y1 = sb("y1", [P, NB, 1 + P])
        xs = sb("xs", [P, C])
        xc = sb("xc2", [P, C])
        sq = sb("sq2", [P, 2, C])
        lg = sb("lg2", [P, 2, C])
        rn = sb("rn2", [P, 2, C])
        turn = sb("turn", [P, 2, C])
        turn_k = sb("turn_k", [P, 2, C])
        qk = sb("qk", [P, 2, C])
        qf = sb("qf", [P, 2, C])
        e = sb("e", [P, 2 * NB, 2 * WIN])
        ew = sb("ew", [P, 2 * NB, KX])
        pt = sb("pt", [P, 2 * NB, P])
        pts = sb("pts", [WIN, 2 * NB, WIN])
        stat = sb("stat", [P, 3, 2 * NB])
        ot = sb("ot2", [P, NP2, C])
        gg = ot[:, 0:FC, :]
        hid = ot[:, FC:2 * FC, :]

        w_loaded, w_init, tab_ready = names("w_loaded", "w_init", "tab_ready")
        dve_step2, act_step2, pool_step2 = names("dve_step2", "act_step2", "pool_step2")
        (xs_ready, vproj_ready, v_kept, v_taken, qproj, kproj, rot_q, rot_k, sqq_ready, sqk_ready,
         turned, nq_ready, nk_ready, rq_ready, rk_ready, q_ready, k_ready, scores_ready,
         scores_used, exp_ready, prob_ready, wide_ready, small_ready, pt_ready, pt0_taken,
         pt1_taken, pv_ready, ot_ready) = names(
            "xs_ready", "vproj_ready", "v_kept", "v_taken", "qproj", "kproj", "rot_q", "rot_k",
            "sqq_ready", "sqk_ready", "turned", "nq_ready", "nk_ready", "rq_ready", "rk_ready",
            "q_ready", "k_ready", "scores_ready", "scores_used", "exp_ready", "prob_ready",
            "wide_ready", "small_ready", "pt_ready", "pt0_taken", "pt1_taken", "pv_ready",
            "ot2_ready")
        (att_ready, xs1_ready, mean_ready, xc_ready, sq1_ready, var_ready, rstd_ready, xn_ready,
         gate_ready, a_ready, gelu_ready, hid_ready, ffn_ready, y_ready) = names(
            "att_ready", "xs1_ready", "mean2_ready", "xc2_ready", "sq1_ready", "var2_ready",
            "rstd2_ready", "xn2_ready", "gate_ready", "a2_ready", "gelu_ready", "hid_ready",
            "ffn_ready", "y_ready")

        def vec(i, n=P):
            return w[0:n, W_VEC + i:W_VEC + i + 1]

        with nc.Block() as block:
            @block.sync
            def _(sp):
                sp.dma_start(tab[:, 0, :, :].rearrange("p i n -> p (i n)"), key_mask).then_inc(w_init, 16)
                sp.wait_ge(w_init, 16)

            @block.vector
            def _(v):
                for ap in (kx, v_tok, yt, y1, ew):
                    v.memset(ap[:], 0.0)
                v.memset(flag[:], 1.0).then_inc(tab_ready, 1)
                v.wait_ge(tab_ready, 1)
                v.memset(flag[:, 0:1], 0.0).then_inc(tab_ready, 1)
                v.tensor_copy(idb[:], ident).then_inc(tab_ready, 1)
                v.wait_ge(w_init, 16)
                v.tensor_copy(kmask[:].rearrange("p t n -> p (t n)"),
                              tab[:, 0, :, :].rearrange("p i n -> p (i n)")).then_inc(tab_ready, 1)
                v.wait_ge(tab_ready, 4)
        nc.all_engine_barrier(sems_to_clear=range(w_loaded.num, tab_ready.num + 1))

        with nc.Fori(0, DEPTH) as layer:
            with nc.Block() as block:
                @block.sync
                def _(sp):
                    sp.dma_start(w[:], weights[bass.ds(layer, 1), :, :].rearrange("l p n -> p (l n)"))\
                        .then_inc(w_loaded, 16)
                    sp.dma_start(tab[:], rot).then_inc(w_loaded, 16)
                    sp.wait_ge(w_loaded, 32)

                @block.vector
                def _(v):
                    v.wait_ge(w_loaded, 32)
                    for i in range(4):
                        v.tensor_scalar(tab[:, :, i, :], tab[:, :, i, :], vec(V_ROT + i), None, ALU.mult)\
                            .then_inc(tab_ready, 1)
                    v.wait_ge(tab_ready, 4)
            nc.all_engine_barrier(sems_to_clear=range(w_loaded.num, tab_ready.num + 1))
            with nc.Fori(0, NT) as t:
                with nc.Block(no_gpsimd_drain=True) as block:
                    @block.tensor
                    def _(pe):
                        pe.wait_ge(xs_ready, 2)
                        for b in range(NB):
                            dst = qq if b % 2 == 0 else kk
                            if b >= 2:
                                pe.wait_ge(v_taken, b - 1)
                            for i in range(2):
                                last = pe.matmul(dst[:, i, :], xs[:, b * P:(b + 1) * P],
                                                 w[:, W_V + i * 512:W_V + (i + 1) * 512],
                                                 start=True, stop=True)
                            last.then_inc(vproj_ready, 1)

                        def project(j):
                            if j == 0:
                                pe.wait_ge(v_taken, NB - 1)
                            else:
                                pe.wait_ge(rot_q, j)
                                pe.wait_ge(sqq_ready, j)
                            for i, at in enumerate((W_Q, W_QR)):
                                last = pe.matmul(qq[:, i, :], w[:, at + j * P:at + (j + 1) * P], xs[:],
                                                 start=True, stop=True)
                            last.then_inc(qproj, 1)
                            if j == 0:
                                pe.wait_ge(v_taken, NB)
                            else:
                                pe.wait_ge(rot_k, j)
                                pe.wait_ge(sqk_ready, j)
                            for i, at in enumerate((W_K, W_KR)):
                                last = pe.matmul(kk[:, i, :], w[:, at + j * P:at + (j + 1) * P], xs[:],
                                                 start=True, stop=True)
                            last.then_inc(kproj, 1)

                        def norms(j):
                            pe.wait_ge(sqq_ready, j + 1)
                            if j:
                                pe.wait_ge(rk_ready, j)
                            pe.matmul(norm_bank, heads_m, sq[:, 0, :], start=True, stop=True)\
                                .then_inc(nq_ready, 1)
                            pe.wait_ge(sqk_ready, j + 1)
                            pe.wait_ge(rq_ready, j + 1)
                            pe.matmul(norm_bank, heads_m, sq[:, 1, :], start=True, stop=True)\
                                .then_inc(nk_ready, 1)

                        def scores(j):
                            pe.wait_ge(q_ready, j + 1)
                            pe.wait_ge(k_ready, j + 1)
                            if j:
                                pe.wait_ge(pt0_taken, j)
                                pe.wait_ge(pt1_taken, j)
                            for h in range(2):
                                pe.matmul(blocks(sc[h][:, 0:NB * 2 * WIN]), idb[:],
                                          kmask[:, bass.ds(t, 1), :].to_broadcast([P, NB, 2 * WIN]),
                                          start=True, stop=False, skip_group_check=True)
                            for b in range(NB):
                                for n in range(NW):
                                    for h in range(2):
                                        r = slice(h * DH, (h + 1) * DH)
                                        last = pe.matmul(
                                            sc[h][n * WIN:(n + 1) * WIN, b * 2 * WIN:(b + 1) * 2 * WIN],
                                            qf[r, j % 2, b * P + n * WIN:b * P + (n + 1) * WIN],
                                            kx[r, j, b, n * WIN:(n + 2) * WIN],
                                            start=False, stop=True, skip_group_check=True)
                            last.then_inc(scores_ready, 1)

                        def turn_probs(j):
                            pe.wait_ge(wide_ready, NW * (j + 1))
                            pe.wait_ge(scores_used, j + 1)
                            for h in range(2):
                                for b in range(NB):
                                    last = pe.transpose(sc[h][:, b * P:(b + 1) * P],
                                                        ew[:, h * NB + b, WIN:KX], ident)
                            last.then_inc(pt_ready, 1)

                        def values(j):
                            pe.wait_ge(pt0_taken, j + 1)
                            pe.wait_ge(pt1_taken, j + 1)
                            pe.wait_ge(small_ready, j + 1)
                            if j:
                                pe.wait_ge(ot_ready, j)
                            for h in range(2):
                                col = (2 * j + h) * DH
                                r = slice(h * DH, (h + 1) * DH)
                                for b in range(NB):
                                    pe.matmul(out_bank[r, b * P:(b + 1) * P], v_tok[:, b, col:col + DH],
                                              pt[:, h * NB + b, :], start=True, stop=False,
                                              skip_group_check=True)
                                    last = pe.matmul(out_bank[r, b * P:b * P + WIN],
                                                     v_before[:, b, col:col + DH], pts[:, h * NB + b, :],
                                                     start=False, stop=True, skip_group_check=True)
                            last.then_inc(pv_ready, 1)

                        project(0)
                        norms(0)
                        scores(0)
                        for j in range(NP2):
                            if j + 1 < NP2:
                                project(j + 1)
                            turn_probs(j)
                            if j + 1 < NP2:
                                norms(j + 1)
                            values(j)
                            if j + 1 < NP2:
                                scores(j + 1)
                        pe.wait_ge(rk_ready, NP2)
                        pe.wait_ge(ot_ready, NP2)
                        for j in range(NP2):
                            last = pe.matmul(norm_bank, w[:, W_O + j * P:W_O + (j + 1) * P], ot[:, j, :],
                                             start=(j == 0), stop=(j == NP2 - 1))
                        last.then_inc(att_ready, 1)
                        pe.wait_ge(xs1_ready, 2)
                        pe.matmul(p[4], mean_m, xs[:], start=True, stop=True).then_inc(mean_ready, 1)
                        pe.wait_ge(sq1_ready, 1)
                        pe.matmul(p[5], mean_m, sq[:, 0, :], start=True, stop=True).then_inc(var_ready, 1)
                        pe.wait_ge(xn_ready, 1)
                        for i, b in enumerate((p[6], p[7], sc[0][:])):
                            n = FROWS[i]
                            pe.matmul(b[0:n, :], w[:, W_1 + FF + i * P:W_1 + FF + i * P + n], xs[:],
                                      start=True, stop=True).then_inc(gate_ready, 1)
                        for i, b in enumerate((sc[1][:], norm_bank, out_bank)):
                            n = FROWS[i]
                            pe.matmul(b[0:n, :], w[:, W_1 + i * P:W_1 + i * P + n], xs[:],
                                      start=True, stop=True).then_inc(a_ready, 1)
                        for i in range(FC):
                            n = FROWS[i]
                            pe.wait_ge(hid_ready, i + 1)
                            last = pe.matmul(p[5], w[0:n, W_2 + i * P:W_2 + (i + 1) * P], hid[0:n, i, :],
                                             start=(i == 0), stop=(i == FC - 1))
                        last.then_inc(ffn_ready, 1)
                        pe.wait_ge(ffn_ready, 1)

                    @block.scalar
                    def _(a):
                        link = linker(a, act_step2)

                        def squares(j):
                            a.wait_ge(qproj, j + 1)
                            if j:
                                a.wait_ge(nq_ready, j)
                                a.wait_ge(nk_ready, j)
                            a.activation(sq[:, 0, :], qq[:, 0, :], ACT.Square).then_inc(sqq_ready, 1)
                            a.wait_ge(kproj, j + 1)
                            a.activation(sq[:, 1, :], kk[:, 0, :], ACT.Square).then_inc(sqk_ready, 1)

                        def inverse_norms(j):
                            for i, (ready, sem, used) in enumerate(((nq_ready, rq_ready, q_ready),
                                                                    (nk_ready, rk_ready, k_ready))):
                                a.wait_ge(ready, j + 1)
                                link(a.activation(lg[:, i, :], norm_bank, ACT.Ln, scale=2.0 ** LN_SHIFT,
                                                  bias=c(C_NORM)))
                                if j:
                                    a.wait_ge(used, j)
                                a.activation(rn[:, i, :], lg[:, i, :], ACT.Exp, scale=-0.5,
                                             bias=c(C_NSC)).then_inc(sem, 1)

                        a.preload_act_table_set(LN_EXP)
                        a.wait_ge(v_kept, 1)
                        for b in range(NB):
                            a.wait_ge(vproj_ready, b + 1)
                            src = (qq if b % 2 == 0 else kk)[:].rearrange("p i n -> p (i n)")
                            a.activation(v_tok[:, b, :], src, ACT.Copy).then_inc(v_taken, 1)
                        squares(0)
                        inverse_norms(0)
                        for j in range(NP2):
                            a.wait_ge(scores_used, j + 1)
                            a.activation(e[:], e[:], ACT.Exp, scale=QK_SCALE).then_inc(exp_ready, 1)
                            if j + 1 < NP2:
                                squares(j + 1)
                            a.wait_ge(prob_ready, j + 1)
                            if j:
                                a.wait_ge(pt_ready, j)
                            for n in range(NW):
                                r = slice(n * WIN, (n + 1) * WIN)
                                a.activation(ew[r, :, n * WIN:(n + 2) * WIN], e[r, :, :], ACT.Copy)\
                                    .then_inc(wide_ready, 1)
                            if j + 1 < NP2:
                                inverse_norms(j + 1)
                            a.wait_ge(pt_ready, j + 1)
                            if j:
                                a.wait_ge(pv_ready, j)
                            a.activation(pt[:, 0:NB, :], blocks(sc[0][:]), ACT.Copy).then_inc(pt0_taken, 1)
                            a.wait_ge(pv_ready, j + 1)
                            a.activation(ot[:, j, :], out_bank, ACT.Copy).then_inc(ot_ready, 1)
                        a.wait_ge(xc_ready, 1)
                        a.wait_ge(ot_ready, NP2)
                        a.activation(sq[:, 0, :], xc[:], ACT.Square).then_inc(sq1_ready, 1)
                        a.wait_ge(var_ready, 1)
                        link(a.activation(lg[:, 0, :], p[5], ACT.Ln, bias=c(C_EPS)))
                        a.activation(rn[:, 0, :], lg[:, 0, :], ACT.Exp, scale=-0.5).then_inc(rstd_ready, 1)
                        for i, b in enumerate((p[6], p[7], sc[0][:])):
                            n = FROWS[i]
                            a.wait_ge(gate_ready, i + 1)
                            a.activation(gg[0:n, i, :], b[0:n, :], ACT.Gelu, bias=vec(V_GATE + i, n))\
                                .then_inc(gelu_ready, 1)
                        a.wait_ge(gelu_ready, FC)

                    @block.gpsimd
                    def _(g):
                        for j in range(NP2):
                            for i, (ready, used) in enumerate(((rot_q, q_ready), (rot_k, k_ready))):
                                g.wait_ge(ready, j + 1)
                                if j:
                                    g.wait_ge(used, j)
                                src = turn if i == 0 else turn_k
                                g.tensor_tensor(qk[:, i, :], src[:, 0, :], src[:, 1, :], ALU.add)\
                                    .then_inc(turned, 1)
                        g.wait_ge(turned, 2 * NP2)

                    @block.vector
                    def _(v):
                        link = linker(v, dve_step2)

                        def done(ins, sem, n):
                            ins.then_inc(sem, 1)
                            v.wait_ge(sem, n)

                        def shifted(src, sem):
                            half = P // 2
                            done(v.tensor_copy(blocks(xs[0:half, :]), src[0:half, :, 1:1 + P]), sem, 1)
                            done(v.tensor_copy(blocks(xs[half:P, :]), src[half:P, :, 0:P]), sem, 2)

                        first_flag = flag[:, bass.ds(t, 1)]
                        link(v.tensor_scalar(yt[:, :, 0:1], yt[:, :, P:P + 1], first_flag, None, ALU.mult))
                        link(v.tensor_copy(yt[:, :, 1:1 + P], y[:, :, bass.ds(t * P, P)]))
                        shifted(yt, xs_ready)
                        done(v.tensor_copy(v_before[:], v_tok[P - WIN:P, :, :]), v_kept, 1)

                        def rotate(j):
                            for i, (ready, sem, src) in enumerate(((sqq_ready, rot_q, qq), (sqk_ready, rot_k, kk))):
                                v.wait_ge(ready, j + 1)
                                if j:
                                    v.wait_ge(turned, 2 * j - 1 + i)
                                dst = turn if i == 0 else turn_k
                                for s in range(2):
                                    ins = v.tensor_tensor(
                                        blocks(dst[:, s, :]), blocks(src[:, s, :]),
                                        tab[:, bass.ds(t, 1), 2 * i + s, :].to_broadcast([P, NB, P]), ALU.mult)
                                    if s == 0:
                                        link(ins)
                                done(ins, sem, j + 1)

                        def unit(j):
                            v.wait_ge(turned, 2 * j + 1)
                            v.wait_ge(rq_ready, j + 1)
                            if j >= 2:
                                v.wait_ge(scores_ready, j - 1)
                            done(v.tensor_tensor(qf[:, j % 2, :], qk[:, 0, :], rn[:, 0, :], ALU.mult),
                                 q_ready, j + 1)
                            link(v.tensor_scalar(kx[:, j, :, 0:WIN], kx[:, j, :, P:KX], first_flag, None, ALU.mult))
                            v.wait_ge(turned, 2 * j + 2)
                            v.wait_ge(rk_ready, j + 1)
                            done(v.tensor_tensor(kx[:, j, :, WIN:KX], blocks(qk[:, 1, :]),
                                                 blocks(rn[:, 1, :]), ALU.mult), k_ready, j + 1)

                        rotate(0)
                        unit(0)
                        for j in range(NP2):
                            v.wait_ge(scores_ready, j + 1)
                            if j:
                                v.wait_ge(wide_ready, NW * j)
                            for h in range(2):
                                link(v.tensor_reduce(stat[:, 0, h * NB:(h + 1) * NB],
                                                     blocks(sc[h][:, 0:NB * 2 * WIN]), AX.X, ALU.max))
                            for h in range(2):
                                r = slice(h * NB, (h + 1) * NB)
                                ins = v.tensor_tensor(e[:, r, :], blocks(sc[h][:, 0:NB * 2 * WIN]),
                                                      along(stat[:, 0, r], 2 * WIN), ALU.subtract)
                                if h == 0:
                                    link(ins)
                            done(ins, scores_used, j + 1)
                            if j + 1 < NP2:
                                rotate(j + 1)
                            v.wait_ge(exp_ready, j + 1)
                            link(v.tensor_reduce(stat[:, 1, :], e[:], AX.X, ALU.add))
                            link(v.reciprocal(stat[:, 2, :], stat[:, 1, :]))
                            done(v.tensor_tensor(e[:], e[:], along(stat[:, 2, :], 2 * WIN), ALU.mult),
                                 prob_ready, j + 1)
                            if j:
                                v.wait_ge(pv_ready, j)
                            done(v.transpose(pts[:], e[0:WIN, :, 0:WIN]), small_ready, j + 1)
                            if j + 1 < NP2:
                                unit(j + 1)
                            v.wait_ge(pt_ready, j + 1)
                            done(v.tensor_copy(pt[:, NB:2 * NB, :], blocks(sc[1][:])), pt1_taken, j + 1)
                        v.wait_ge(att_ready, 1)
                        link(v.tensor_scalar(y1[:, :, 0:1], y1[:, :, P:P + 1], first_flag, None, ALU.mult))
                        link(v.tensor_tensor(y1[:, :, 1:1 + P], blocks(norm_bank), yt[:, :, 1:1 + P], ALU.add))
                        shifted(y1, xs1_ready)
                        v.wait_ge(mean_ready, 1)
                        done(v.tensor_tensor(xc[:], xs[:], p[4], ALU.subtract), xc_ready, 1)
                        v.wait_ge(rstd_ready, 1)
                        link(v.tensor_tensor(xc[:], xc[:], rn[:, 0, :], ALU.mult))
                        done(v.tensor_scalar(xs[:], xc[:], vec(V_G), vec(V_B), ALU.mult, ALU.add), xn_ready, 1)
                        for i, b in enumerate((sc[1][:], norm_bank, out_bank)):
                            n = FROWS[i]
                            v.wait_ge(a_ready, i + 1)
                            v.wait_ge(gelu_ready, i + 1)
                            done(v.scalar_tensor_tensor(hid[0:n, i, :], b[0:n, :], vec(V_A + i, n),
                                                        gg[0:n, i, :], ALU.add, ALU.mult), hid_ready, i + 1)
                        v.wait_ge(ffn_ready, 1)
                        done(v.scalar_tensor_tensor(y[:, :, bass.ds(t * P, P)], blocks(p[5]), vec(V_B2),
                                                    y1[:, :, 1:1 + P], ALU.add, ALU.add), y_ready, 1)
                nc.all_engine_barrier(sems_to_clear=range(dve_step2.num, y_ready.num + 1))


def final_sum(nc, sbuf, names, p, y, ident, x1_dram, out):
    with ExitStack() as ctx:
        x1 = sbuf(ctx, "x1f", [P, NB, P])
        s = sbuf(ctx, "sf", [P, NB, P])
        o = sbuf(ctx, "of", [P, NB, P])
        x1_loaded, sum_ready, sum_turned, out_ready, out_stored = names(
            "x1_loaded", "sum_ready", "sum_turned", "out_ready", "out_stored")
        with nc.Fori(0, NT) as t:
            with nc.Block(no_gpsimd_drain=True) as block:
                @block.sync
                def _(sp):
                    sp.dma_start(x1[:], x1_dram[:, :, bass.ds(t * P, P)]).then_inc(x1_loaded, 16)
                    sp.wait_ge(out_ready, 1)
                    sp.dma_start(out[:, bass.ds(t * P, P), :].rearrange("b p d -> p b d"), o[:])\
                        .then_inc(out_stored, 16)
                    sp.wait_ge(out_stored, 16)

                @block.vector
                def _(v):
                    v.wait_ge(x1_loaded, 16)
                    v.tensor_tensor(s[:], x1[:], y[:, :, bass.ds(t * P, P)], ALU.add).then_inc(sum_ready, 1)
                    v.wait_ge(sum_ready, 1)

                @block.tensor
                def _(pe):
                    pe.wait_ge(sum_ready, 1)
                    for b in range(NB):
                        last = pe.transpose(p[0][:, b * P:(b + 1) * P], s[:, b, :], ident)
                    last.then_inc(sum_turned, 1)
                    pe.wait_ge(sum_turned, 1)

                @block.scalar
                def _(a):
                    a.wait_ge(sum_turned, 1)
                    a.activation(o[:], blocks(p[0]), ACT.Copy).then_inc(out_ready, 1)
                    a.wait_ge(out_ready, 1)
            nc.all_engine_barrier(sems_to_clear=range(x1_loaded.num, out_stored.num + 1))


def shape_constants():
    i, j = np.arange(P)[:, None], np.arange(P)[None, :]
    m = np.zeros((P, NM, P), np.float32)
    m[:, M_ID], m[:, M_LE], m[:, M_GT] = i == j, i <= j, i > j
    m[:, M_MEAN], m[:, M_ONES], m[:, M_HEADS] = 1.0 / P, 1.0, i // DH == j // DH
    for n in range(LEVELS):
        s = 1 << n
        low = (i // (2 * s) == j // (2 * s)) & (i // s % 2 == 1) & (j // s % 2 == 0)
        m[:, M_OFF + n], m[:, M_OFF + LEVELS + n] = low, low.T
    key = np.zeros((P, NT, 2 * WIN), np.float32)
    r, k = (np.arange(P) % WIN)[:, None], np.arange(2 * WIN)[None, :]
    hidden = np.where(k < WIN, k < r, k - WIN > r)
    key[:] = np.where(hidden, MASKED, 0.0)[:, None, :]
    key[0:WIN, 0, 0:WIN] = MASKED
    half = np.arange(0, DH, 2, dtype=np.float32)
    inv_freq = (1.0 / 10000.0 ** (half / np.float32(DH))).astype(np.float32)
    pos = np.arange(L, dtype=np.float32)
    f = (pos[:, None] * inv_freq[None, :]).astype(np.float32).astype(np.float64)
    base = ((half + np.float32(0.4 * DH)) / np.float32(1.4 * DH)).astype(np.float64)
    scale = base[None, :] ** ((pos - L // 2) / (WIN // 2))[:, None].astype(np.float64)
    tab = np.zeros((4, P, L))
    for d in range(P):
        n = d % (DH // 2)
        sign = -1.0 if d % DH < DH // 2 else 1.0
        cos, sin, s = np.cos(f[:, n]), np.sin(f[:, n]), scale[:, n]
        tab[:, d] = cos * s, sign * sin * s, cos / s, sign * sin / s
    tab = tab.reshape(4, P, NT, P).transpose(1, 2, 0, 3).astype(np.float32)
    return m, key.reshape(P, NT * 2 * WIN), np.ascontiguousarray(tab)


def laid_out(d):
    g = {k: np.asarray(v) for k, v in d.items()}
    a = {k[8:]: v for k, v in g.items() if k.startswith("L0_attn_")}
    f = {k[7:]: v for k, v in g.items() if k.startswith("L0_ffn_")}

    def rows(m, n):
        full = np.zeros((n * P, m.shape[1]), np.float32)
        full[:m.shape[0]] = m
        return full.reshape(n, P, -1).transpose(1, 0, 2).reshape(P, -1)

    w1 = np.concatenate([a["Wq"], a["Wk"], a["Wv"], a["Wg"], a["Wb"], a["Wa"]], axis=1)
    conv = rows(np.concatenate([a["conv_q"], a["conv_k"], a["conv_v"]]), NCH).reshape(P, NCH, KS)
    wo1 = rows(a["Wo"], 2).reshape(P, 2, P)
    rows1 = np.concatenate([a["A_log"], a["dt_bias"], a["norm_w"]])
    d_of = np.arange(P) % DH
    swap = (d_of + DH // 2) % DH
    cols = np.arange(INNER)
    swapped = cols // DH * DH + (cols % DH + DH // 2) % DH
    per_layer = []
    for i in range(DEPTH):
        wq, wk = f["Wqkv"][i][:, 0:INNER], f["Wqkv"][i][:, INNER:2 * INNER]
        vec = np.zeros((P, WCOLS - W_VEC), np.float32)
        vec[:, V_G], vec[:, V_B], vec[:, V_B2] = f["ln_g"][i], f["ln_b"][i], f["b2"][i]
        for n in range(FC):
            vec[:FROWS[n], V_A + n] = f["b1"][i][n * P:n * P + FROWS[n]]
            vec[:FROWS[n], V_GATE + n] = f["b1"][i][FF + n * P:FF + n * P + FROWS[n]]
        for n, s in enumerate((f["q_scale"][i], f["k_scale"][i])):
            vec[:, V_ROT + 2 * n], vec[:, V_ROT + 2 * n + 1] = s[d_of], s[swap]
        per_layer.append(np.concatenate([f["Wqkv"][i], wq[:, swapped], wk[:, swapped], f["W1"][i],
                                         rows(f["Wo"][i], NP2), rows(f["W2"][i], FC), vec], axis=1))
    masks, key_mask, rot = shape_constants()
    return {"x": a["x"], "w1": w1, "conv": conv, "wo1": wo1, "rows1": rows1, "masks": masks,
            "key_mask": key_mask, "rot": rot, "weights": np.stack(per_layer)}


def program(nc, arrays):
    ap = {n: nc.dram_tensor(f"in_{n}", v.shape, mybir.dt.from_np(v.dtype), kind="ExternalInput").ap()
          for n, v in arrays.items()}
    out = nc.dram_tensor("out", (NB, L, P), F32, kind="ExternalOutput").ap()
    x1_dram = nc.dram_tensor("x1_dram", (P, NB, L), F32, kind="Internal").ap()
    build(nc, ap["x"], ap["w1"], ap["conv"], ap["wo1"], ap["rows1"], ap["masks"],
          ap["key_mask"], ap["rot"], ap["weights"], out, x1_dram)


def kernel(**inputs):
    import concourse.bacc as bacc
    from concourse.bass_utils import run_bass_kernel_spmd as run

    nc = bacc.Bacc("TRN2", target_bir_lowering=False, num_devices=1)
    arrays = {n: np.ascontiguousarray(v) for n, v in laid_out(inputs).items()}
    program(nc, arrays)
    r = run(nc, [{f"in_{n}": v for n, v in arrays.items()}], core_ids=[0])
    return r.results[0]["out"]
```

```python
from contextlib import ExitStack

import numpy as np

import concourse.bass as bass
from concourse import mybir

ALU = mybir.AluOpType
ACT = mybir.ActivationFunctionType
AX = mybir.AxisListType
F32 = mybir.dt.float32
BF16 = mybir.dt.bfloat16

P = 128
NB = 4
L = 1024
NT = L // P
C = NB * P
EPS = 1e-5

H1, DV, KS = 6, 32, 4
VD = H1 * DV
NQK = 2 * H1
NCH = NQK + 2
GW = VD + 2 * H1
LEVELS = 7
ATANH_TERMS = 9

DEPTH, HEADS, DH, WIN = 6, 16, 64, 32
INNER = HEADS * DH
NP2 = HEADS // 2
FF = 341
FC = 3
FROWS = [P, P, FF - 2 * P]
KX = WIN + P
NW = P // WIN
QK_SCALE = 8.0
MASKED = -1e30
LN_EXP = "natural_log_exp_and_others"
LN_SHIFT = 20

W_Q, W_K, W_V = 0, INNER, 2 * INNER
W_QR, W_KR = 3 * INNER, 4 * INNER
W_1 = 5 * INNER
W_O = W_1 + 2 * FF
W_2 = W_O + NP2 * P
W_VEC = W_2 + FC * P
V_G, V_B, V_A, V_GATE, V_B2, V_ROT = 0, 1, 2, 5, 8, 9
WCOLS = W_VEC + 13

M_ID, M_LE, M_GT, M_MEAN, M_ONES, M_HEADS, M_OFF = 0, 1, 2, 3, 4, 5, 6
NM = M_OFF + 2 * LEVELS


def linker(eng, sem):
    count = [0]

    def link(ins):
        count[0] += 1
        ins.then_inc(sem, 1)
        eng.wait_ge(sem, count[0])

    return link


def over_batches(ap, n=NB):
    return ap.unsqueeze(1).to_broadcast([ap.shape[0], n, ap.shape[1]])


def along(ap, m):
    return ap.unsqueeze(2).to_broadcast([ap.shape[0], ap.shape[1], m])


def blocks(ap, n=NB):
    return ap.rearrange("p (b n) -> p b n", b=n)


def build(nc, x, w1, conv, wo1, rows1, masks, key_mask, rot, weights, out, x1_dram):
    with ExitStack() as whole:
        def names(*words):
            return [whole.enter_context(nc.semaphore(w)) for w in words]

        def sbuf(ctx, name, shape, dt=F32):
            return ctx.enter_context(nc.sbuf_tensor(name, shape, dt))

        banks = whole.enter_context(nc.psum_tensor("banks", [P, 8, 512], F32))
        p = [banks[:, i, :] for i in range(8)]

        y = sbuf(whole, "y", [P, NB, L])
        msk = sbuf(whole, "msk", [P, NM, P])
        cst = sbuf(whole, "cst", [P, 8])
        ident = msk[:, M_ID, :]
        ones = msk[:, M_ONES, :]
        C_EPS, C_L2, C_QSC, C_ZERO, C_NORM, C_NSC = range(6)

        def c(i):
            return cst[:, i:i + 1]

        load_done, init_done = names("load_done", "init_done")
        delta_layer(nc, sbuf, names, p, y, msk, ident, ones, cst, c,
                    (C_EPS, C_L2, C_QSC, C_ZERO, C_NORM, C_NSC), load_done, init_done,
                    x, w1, conv, wo1, rows1, masks, x1_dram)
        local_layers(nc, sbuf, names, p, banks, y, msk, ident, c,
                     (C_EPS, C_ZERO, C_NORM, C_NSC), key_mask, rot, weights)
        final_sum(nc, sbuf, names, p, y, ident, x1_dram, out)


def delta_layer(nc, sbuf, names, p, y, msk, ident, ones, cst, c, cols, load_done, init_done,
                x, w1, conv, wo1, rows1, masks, x1_dram):
    C_EPS, C_L2, C_QSC, C_ZERO, C_NORM, C_NSC = cols
    le, gt, mean_m = msk[:, M_LE, :], msk[:, M_GT, :], msk[:, M_MEAN, :]
    with ExitStack() as ctx:
        def sb(name, shape, dt=F32):
            return sbuf(ctx, name, shape, dt)

        w = sb("w1s", [P, NQK * P + VD + GW])
        cw = sb("cw", [P, NCH, KS])
        wo = sb("wo1s", [P, 2, P])
        rows = sb("rows", [P, 2 * H1 + DV])
        neg_a = sb("neg_a", [P, H1])
        pre = sb("pre", [P, NCH, NB, KS - 1 + P])
        act_qkv = sb("act_qkv", [P, NCH, C])
        state = sb("state", [P, H1, NB, DV])
        xin = sb("xin", [P, NB, P])
        xt = sb("xt", [P, C])
        xc = sb("xc", [P, C])
        xn = sb("xn", [P, C])
        sq = sb("sq", [P, 2, C])
        lg = sb("lg", [P, 2, C])
        rs = sb("rs", [P, 2, C])
        cv = sb("cv", [P, 2, C])
        vt = sb("vt", [P, NB, VD])
        sg = sb("sg", [P, NB, VD])
        ba = sb("ba", [P, NB, 2 * H1])
        t24 = sb("t24", [P, 12, NB, H1])
        ex = sb("ex", [P, 3, NB, H1])
        gm = sb("gm", [P, 2, NB, P])
        gam = sb("gam", [P, 2, NB, P])
        gat = sb("gat", [P, 2, NB, P])
        am = sb("am", [P, NB, P])
        at = sb("at", [P, NB, P])
        tmp = sb("tmp", [P, NB, P])
        pm = sb("pm", [P, 2, NB, P])
        kt = sb("kt", [P, 2, NB, P])
        ao = sb("ao", [P, 2, NB, P])
        tt = sb("tt", [P, NB, P])
        tr = sb("tr", [P, NB, P])
        p1 = sb("p1", [P, NB, P])
        r1 = sb("r1", [P, 3, NB, DV])
        u = sb("u", [P, 2, NB, DV])
        o = sb("o", [P, NB, VD])
        o2 = sb("o2", [P, NB, DV])
        ot = sb("ot", [P, 2, C])
        osq = sb("osq", [P, NB, VD])
        om = sb("om", [P, 4, NB * H1])
        x1 = sb("x1", [P, C])

        dve_step, act_step, pool_step = names("dve_step", "act_step", "pool_step")
        (x_loaded, x_turned, xt_ready, mean_ready, xc_ready, lnsq_ready, var_ready, rstd_ready,
         xn_ready, proj_ready, pre_ready, conv_ready, silu_ready, gates_ready, gates_taken,
         sq_ready, ss_ready, rn_ready, qk_ready) = names(
            "x_loaded", "x_turned", "xt_ready", "mean_ready", "xc_ready", "lnsq_ready", "var_ready",
            "rstd_ready", "xn_ready", "proj_ready", "pre_ready", "conv_ready", "silu_ready",
            "gates_ready", "gates_taken", "sq_ready", "ss_ready", "rn_ready", "qk_ready")
        (v_turned, v_ready, e1_asked, e1_ready, g_ready, cum_ready, cum_exp, gm_ready, decay_ready,
         decay_exp, kk_ready, a_ready, a_turned, at_ready, t_ready, ao_ready, p1_ready, p1_taken,
         delta_ready, tri_ready, ktok_ready, kt_ready, pm_ready) = names(
            "v_turned", "v_ready", "e1_asked", "e1_ready", "g_ready", "cum_ready", "cum_exp",
            "gm_ready", "decay_ready", "decay_exp", "kk_ready", "a_ready", "a_turned", "at_ready",
            "t_ready", "ao_ready", "p1_ready", "p1_taken", "delta_ready", "tri_ready", "ktok_ready",
            "kt_ready", "pm_ready")
        (ks_ready, r_ready, u_ready, u_taken, o_ready, s_ready, o_done, om_ready, ostd_ready,
         on_ready, on_turned, ot_ready, wo_ready, x1_ready, x1_stored) = names(
            "ks_ready", "r_ready", "u_ready", "u_taken", "o_ready", "s_ready", "o_done", "om_ready",
            "ostd_ready", "on_ready", "on_turned", "ot_ready", "wo_ready", "x1_ready", "x1_stored")

        with nc.Block() as block:
            @block.sync
            def _(sp):
                for dst, src in ((w[:], w1), (cw[:], conv), (wo[:], wo1), (msk[:], masks),
                                 (rows[:], rows1.partition_broadcast(P))):
                    sp.dma_start(dst, src).then_inc(load_done, 16)
                sp.wait_ge(load_done, 5 * 16)

            @block.vector
            def _(v):
                for i, value in ((C_EPS, EPS), (C_L2, 1e-12), (C_QSC, -0.5 * float(np.log(P))),
                                 (C_ZERO, 0.0), (C_NORM, 1e-24 * 2.0 ** LN_SHIFT),
                                 (C_NSC, 0.5 * LN_SHIFT * float(np.log(2.0)))):
                    v.memset(c(i), value)
                v.memset(pre[:], 0.0)
                v.memset(act_qkv[:], 0.0)
                v.memset(cv[:], 0.0)
                v.memset(state[:], 0.0).then_inc(init_done, 1)
                v.wait_ge(init_done, 1)
                v.wait_ge(init_done, 2)
                v.tensor_scalar(neg_a[:], neg_a[:], -1.0, None, ALU.mult).then_inc(init_done, 1)
                v.wait_ge(init_done, 3)

            @block.scalar
            def _(a):
                a.wait_ge(load_done, 5 * 16)
                a.wait_ge(init_done, 1)
                a.activation(neg_a[:], rows[:, 0:H1], ACT.Exp).then_inc(init_done, 1)
                a.wait_ge(init_done, 3)

        first = dve_step.num
        with nc.Fori(0, NT) as t:
            with nc.Block(no_gpsimd_drain=True) as block:
                @block.sync
                def _(sp):
                    sp.dma_start(xin[:], x[:, bass.ds(t * P, P), :].rearrange("b p d -> p b d"))\
                        .then_inc(x_loaded, 16)
                    sp.wait_ge(x_loaded, 16)
                    sp.wait_ge(x1_ready, 1)
                    sp.dma_start(x1_dram[:, :, bass.ds(t * P, P)], blocks(x1[:])).then_inc(x1_stored, 16)
                    sp.wait_ge(x1_stored, 16)

                @block.tensor
                def _(pe):
                    pe.wait_ge(x_loaded, 16)
                    for b in range(NB):
                        last = pe.transpose(p[0][:, b * P:(b + 1) * P], xin[:, b, :], ident)
                    last.then_inc(x_turned, 1)
                    pe.wait_ge(xt_ready, 1)
                    pe.matmul(p[1], mean_m, xt[:], start=True, stop=True).then_inc(mean_ready, 1)
                    pe.wait_ge(lnsq_ready, 1)
                    pe.matmul(p[0], mean_m, sq[:, 0, :], start=True, stop=True).then_inc(var_ready, 1)
                    pe.wait_ge(xn_ready, 1)
                    for n in range(NCH):
                        m = P if n < NCH - 1 else VD - P
                        if n >= 4:
                            pe.wait_ge(pre_ready, n - 3)
                        pe.matmul(p[n % 4][0:m, :], w[:, n * P:n * P + m], xn[:], start=True, stop=True)\
                            .then_inc(proj_ready, 1)
                    for b in range(NB):
                        last = pe.matmul(p[4 + b // 2][:, (b % 2) * GW:(b % 2 + 1) * GW],
                                         xn[:, b * P:(b + 1) * P], w[:, NQK * P + VD:NQK * P + VD + GW],
                                         start=True, stop=True)
                    last.then_inc(gates_ready, 1)
                    pe.wait_ge(pre_ready, NCH)
                    for n in range(NQK):
                        pe.wait_ge(sq_ready, n + 1)
                        if n >= 2:
                            pe.wait_ge(rn_ready, n - 1)
                        pe.matmul(p[n % 2], ones, sq[:, n % 2, :], start=True, stop=True)\
                            .then_inc(ss_ready, 1)
                    pe.wait_ge(silu_ready, NCH)
                    for b in range(NB):
                        at_b = p[6 + b // 2][:, (b % 2) * VD:(b % 2 + 1) * VD]
                        pe.transpose(at_b[:, 0:P], act_qkv[:, NQK, b * P:(b + 1) * P], ident)
                        last = pe.transpose(at_b[:, P:VD], act_qkv[0:VD - P, NQK + 1, b * P:(b + 1) * P],
                                            ident[0:VD - P, 0:VD - P])
                    last.then_inc(v_turned, 1)
                    pe.wait_ge(g_ready, 1)
                    pe.wait_ge(gates_taken, 2)
                    g = t24[:, 0, :, :].rearrange("p b h -> p (b h)")
                    for i, m in enumerate((le, gt, ones)):
                        last = pe.matmul(p[5][:, i * NB * H1:(i + 1) * NB * H1], m, g, start=True, stop=True)
                    last.then_inc(cum_ready, 1)
                    pe.wait_ge(rn_ready, NQK)
                    pe.wait_ge(v_ready, 2)
                    pe.wait_ge(cum_exp, 1)

                    def products(h):
                        pe.wait_ge(gm_ready, h + 1)
                        if h:
                            pe.wait_ge(decay_exp, h)
                            pe.wait_ge(a_ready, h)
                            pe.wait_ge(pm_ready, h)
                        pe.wait_ge(qk_ready, NQK)
                        for b in range(NB):
                            s = slice(b * P, (b + 1) * P)
                            pe.matmul(p[0][:, s], gm[:, h % 2, b, :], le, start=True, stop=True)
                            last = pe.matmul(p[1][:, s], le, gm[:, h % 2, b, :], start=True, stop=True)
                        last.then_inc(decay_ready, 1)
                        for b in range(NB):
                            s = slice(b * P, (b + 1) * P)
                            k_b, q_b = act_qkv[:, H1 + h, s], act_qkv[:, h, s]
                            pe.matmul(p[2][:, s], k_b, k_b, start=True, stop=True)
                            last = pe.matmul(p[3][:, s], k_b, q_b, start=True, stop=True)
                        last.then_inc(kk_ready, 1)

                    products(0)
                    for h in range(H1):
                        pe.wait_ge(a_ready, h + 1)
                        if h:
                            pe.wait_ge(kt_ready, h)
                        for b in range(NB):
                            last = pe.transpose(p[4][:, b * P:(b + 1) * P], am[:, b, :], ident)
                        last.then_inc(a_turned, 1)
                        pe.wait_ge(at_ready, h + 1)
                        for b in range(NB):
                            last = pe.transpose(p[4][:, b * P:(b + 1) * P],
                                                act_qkv[:, H1 + h, b * P:(b + 1) * P], ident)
                        last.then_inc(ktok_ready, 1)
                        for i in range(1, LEVELS):
                            n = h * (LEVELS - 1) + i
                            pe.wait_ge(t_ready, n)
                            pe.wait_ge(ao_ready, n)
                            if i == 1 and h:
                                pe.wait_ge(r_ready, h)
                            for b in range(NB):
                                last = pe.matmul(p[5][:, b * P:(b + 1) * P], ao[:, i % 2, b, :],
                                                 tr[:, b, :], start=True, stop=True)
                            last.then_inc(p1_ready, 1)
                            if i == 2 and h + 1 < H1:
                                products(h + 1)
                            pe.wait_ge(p1_taken, n)
                            if i == 1 and h:
                                pe.wait_ge(u_taken, h)
                                pe.wait_ge(s_ready, h)
                            if i < LEVELS - 1:
                                for b in range(NB):
                                    last = pe.matmul(p[6][:, b * P:(b + 1) * P], tt[:, b, :],
                                                     p1[:, b, :], start=True, stop=True)
                            for b in range(NB):
                                last = pe.matmul(p[7][:, b * P:(b + 1) * P], p1[:, b, :],
                                                 tt[:, b, :], start=True, stop=True)
                            last.then_inc(delta_ready, 1)
                        for b in range(NB):
                            s = slice(b * P, (b + 1) * P)
                            pe.matmul(p[5][:, b * DV:(b + 1) * DV], act_qkv[:, H1 + h, s],
                                      state[:, h, b, :], start=True, stop=True)
                            last = pe.matmul(p[5][:, P + b * DV:P + (b + 1) * DV], act_qkv[:, h, s],
                                             state[:, h, b, :], start=True, stop=True)
                        last.then_inc(ks_ready, 1)
                        pe.wait_ge(tri_ready, h + 1)
                        pe.wait_ge(r_ready, h + 1)
                        for b in range(NB):
                            last = pe.matmul(p[6][:, b * DV:(b + 1) * DV], tt[:, b, :], r1[:, 2, b, :],
                                             start=True, stop=True)
                        last.then_inc(u_ready, 1)
                        pe.wait_ge(u_taken, h + 1)
                        pe.wait_ge(kt_ready, h + 1)
                        pe.wait_ge(pm_ready, h + 1)
                        for b in range(NB):
                            pe.matmul(p[7][:, b * DV:(b + 1) * DV], pm[:, h % 2, b, :], u[:, 0, b, :],
                                      start=True, stop=True)
                            last = pe.matmul(p[7][:, P + b * DV:P + (b + 1) * DV], kt[:, h % 2, b, :],
                                             u[:, 1, b, :], start=True, stop=True)
                        last.then_inc(o_ready, 1)
                    pe.wait_ge(on_ready, 1)
                    for b in range(NB):
                        pe.transpose(p[0][:, b * P:(b + 1) * P], o[:, b, 0:P], ident)
                        last = pe.transpose(p[1][0:VD - P, b * P:(b + 1) * P], o[:, b, P:VD], ident)
                    last.then_inc(on_turned, 1)
                    pe.wait_ge(ot_ready, 2)
                    pe.matmul(p[2], wo[:, 0, :], ot[:, 0, :], start=True, stop=False)
                    pe.matmul(p[2], wo[0:VD - P, 1, :], ot[0:VD - P, 1, :], start=False, stop=True)\
                        .then_inc(wo_ready, 1)
                    pe.wait_ge(x1_ready, 1)
                    pe.matmul(p[3], mean_m, x1[:], start=True, stop=True).then_inc(mean_ready, 1)
                    pe.wait_ge(lnsq_ready, 2)
                    pe.matmul(p[4], mean_m, sq[:, 0, :], start=True, stop=True).then_inc(var_ready, 1)
                    pe.wait_ge(var_ready, 2)

                @block.scalar
                def _(a):
                    link = linker(a, act_step)

                    def rstd(n, bank_of_var):
                        a.wait_ge(xc_ready, n)
                        a.activation(sq[:, 0, :], xc[:], ACT.Square).then_inc(lnsq_ready, 1)
                        a.wait_ge(var_ready, n)
                        link(a.activation(lg[:, 0, :], bank_of_var, ACT.Ln, bias=c(C_EPS)))
                        a.activation(rs[:, 0, :], lg[:, 0, :], ACT.Exp, scale=-0.5).then_inc(rstd_ready, 1)
                        a.wait_ge(rstd_ready, n)

                    a.preload_act_table_set(LN_EXP)
                    a.wait_ge(x_turned, 1)
                    a.activation(xt[:], p[0], ACT.Copy).then_inc(xt_ready, 1)
                    rstd(1, p[0])

                    def take(n):
                        m = P if n < NCH - 1 else VD - P
                        a.wait_ge(proj_ready, n + 1)
                        a.activation(pre[0:m, n, :, KS - 1:], blocks(p[n % 4][0:m, :]), ACT.Copy)\
                            .then_inc(pre_ready, 1)

                    def silu(n):
                        a.wait_ge(conv_ready, n + 1)
                        a.activation(act_qkv[:, n, :], cv[:, n % 2, :], ACT.Silu).then_inc(silu_ready, 1)

                    for n in range(NCH + 2):
                        if n < NCH:
                            take(n)
                        if n >= 2:
                            silu(n - 2)
                    a.wait_ge(gates_ready, 1)
                    for i in range(2):
                        src = p[4 + i][:, 0:2 * GW].rearrange("p (b n) -> p b n", b=2)
                        a.activation(sg[:, 2 * i:2 * i + 2, :], src[:, :, 0:VD], ACT.Silu)\
                            .then_inc(gates_taken, 1)
                    a.wait_ge(silu_ready, NCH)
                    a.preload_act_table_set(LN_EXP)
                    a.wait_ge(e1_asked, 1)
                    for i in (3, 4, 5):
                        a.activation(t24[:, i + 3, :, :], t24[:, i, :, :], ACT.Exp).then_inc(e1_ready, 1)
                    for n in range(NQK + 1):
                        if n < NQK:
                            if n >= 2:
                                a.wait_ge(ss_ready, n - 1)
                            a.activation(sq[:, n % 2, :], act_qkv[:, n, :], ACT.Square).then_inc(sq_ready, 1)
                        if n >= 1:
                            m = n - 1
                            a.wait_ge(ss_ready, m + 1)
                            link(a.activation(lg[:, m % 2, :], p[m % 2], ACT.Ln, bias=c(C_L2)))
                            if m >= 2:
                                a.wait_ge(qk_ready, m - 1)
                            a.activation(rs[:, m % 2, :], lg[:, m % 2, :], ACT.Exp, scale=-0.5,
                                         bias=c(C_QSC) if m < H1 else c(C_ZERO)).then_inc(rn_ready, 1)
                    a.wait_ge(v_turned, 1)
                    for i in range(2):
                        a.activation(vt[:, 2 * i:2 * i + 2, :],
                                     p[6 + i][:, 0:2 * VD].rearrange("p (b n) -> p b n", b=2), ACT.Copy)\
                            .then_inc(v_ready, 1)
                    a.wait_ge(cum_ready, 1)
                    a.activation(ex[:].rearrange("p i b h -> p (i b h)"), p[5][:, 0:3 * NB * H1], ACT.Exp)\
                        .then_inc(cum_exp, 1)

                    def decays(h):
                        a.wait_ge(decay_ready, h + 1)
                        if h >= 2:
                            a.wait_ge(pm_ready, h - 1)
                        link(a.activation(gat[:, h % 2, :, :], blocks(p[0]), ACT.Exp))
                        a.activation(gam[:, h % 2, :, :], blocks(p[1]), ACT.Exp).then_inc(decay_exp, 1)
                        a.wait_ge(decay_exp, h + 1)

                    decays(0)
                    for h in range(H1):
                        a.wait_ge(a_turned, h + 1)
                        if h:
                            a.wait_ge(ao_ready, h * (LEVELS - 1))
                        a.activation(at[:], blocks(p[4]), ACT.Copy).then_inc(at_ready, 1)
                        a.wait_ge(ktok_ready, h + 1)
                        a.activation(kt[:, h % 2, :, :], blocks(p[4]), ACT.Copy).then_inc(kt_ready, 1)
                        for i in range(1, LEVELS):
                            n = h * (LEVELS - 1) + i
                            a.wait_ge(p1_ready, n)
                            if n > 1:
                                a.wait_ge(delta_ready, n - 1)
                            a.activation(p1[:], blocks(p[5]), ACT.Copy).then_inc(p1_taken, 1)
                            if i == 2 and h + 1 < H1:
                                decays(h + 1)
                    a.wait_ge(om_ready, 1)
                    link(a.activation(om[:, 1, :], om[:, 0, :], ACT.Ln, scale=1.0 / DV, bias=c(C_EPS)))
                    a.activation(om[:, 2, :], om[:, 1, :], ACT.Exp, scale=-0.5).then_inc(ostd_ready, 1)
                    a.wait_ge(on_turned, 1)
                    a.activation(ot[:, 0, :], p[0], ACT.Copy).then_inc(ot_ready, 1)
                    a.activation(ot[0:VD - P, 1, :], p[1][0:VD - P, :], ACT.Copy).then_inc(ot_ready, 1)
                    a.wait_ge(ot_ready, 2)
                    rstd(2, p[4])

                @block.gpsimd
                def _(g):
                    for h in range(H1):
                        g.wait_ge(at_ready, h + 1)
                        for i in range(1, LEVELS):
                            n = h * (LEVELS - 1) + i
                            if n > 2:
                                g.wait_ge(p1_ready, n - 2)
                            g.tensor_tensor(ao[:, i % 2, :, :], at[:],
                                            over_batches(msk[:, M_OFF + LEVELS + i, :]), ALU.mult)\
                                .then_inc(ao_ready, 1)
                    g.wait_ge(ao_ready, H1 * (LEVELS - 1))

                @block.vector
                def _(v):
                    link = linker(v, dve_step)

                    def done(ins, sem, n):
                        ins.then_inc(sem, 1)
                        v.wait_ge(sem, n)

                    def layer_norm(n, src, bank_of_mean, dst):
                        v.wait_ge(mean_ready, n)
                        ins = v.tensor_tensor(xc[:], src, bank_of_mean, ALU.subtract)
                        ins.then_inc(xc_ready, 1)
                        v.wait_ge(xc_ready, n)
                        v.wait_ge(rstd_ready, n)
                        ins = v.tensor_tensor(dst, blocks(xc[:]), blocks(rs[:, 0, :]), ALU.mult)
                        ins.then_inc(xn_ready, 1)
                        v.wait_ge(xn_ready, n)

                    layer_norm(1, xt[:], p[1], blocks(xn[:]))
                    for n in range(NCH):
                        m = P if n < NCH - 1 else VD - P
                        v.wait_ge(pre_ready, n + 1)
                        if n >= 2:
                            v.wait_ge(silu_ready, n - 1)
                        dst = blocks(cv[0:m, n % 2, :])
                        link(v.tensor_scalar(dst, pre[0:m, n, :, 0:P], cw[0:m, n, 0:1], None, ALU.mult))
                        for s in range(1, KS):
                            ins = v.scalar_tensor_tensor(dst, pre[0:m, n, :, s:s + P], cw[0:m, n, s:s + 1],
                                                         dst, ALU.mult, ALU.add)
                            if s < KS - 1:
                                link(ins)
                        ins.then_inc(conv_ready, 1)
                        v.wait_ge(conv_ready, n + 1)
                    link(v.tensor_copy(pre[:, :, :, 0:KS - 1], pre[:, :, :, P:P + KS - 1]))
                    v.wait_ge(gates_ready, 1)
                    v.wait_ge(gates_taken, 2)
                    for i in range(2):
                        src = p[4 + i][:, 0:2 * GW].rearrange("p (b n) -> p b n", b=2)
                        link(v.tensor_copy(ba[:, 2 * i:2 * i + 2, :], src[:, :, VD:GW]))
                    beta, dec = ba[:, :, 0:H1], ba[:, :, H1:2 * H1]
                    G, BETA, POS, NB_ABS, NB_MIN, ND_ABS, E_B, E_BM, E_D, S1, S2, T = \
                        [t24[:, i, :, :] for i in range(12)]
                    link(v.tensor_tensor(dec, dec, over_batches(rows[:, H1:2 * H1]), ALU.add))
                    for dst, src in ((NB_ABS, beta), (ND_ABS, dec)):
                        link(v.tensor_scalar(T, src, -1.0, None, ALU.mult))
                        link(v.tensor_tensor(dst, T, src, ALU.min))
                    link(v.tensor_scalar(POS, dec, 0.0, None, ALU.max))
                    done(v.tensor_scalar(NB_MIN, beta, 0.0, None, ALU.min), e1_asked, 1)
                    v.wait_ge(e1_ready, 3)
                    link(v.tensor_scalar(T, E_B, 1.0, None, ALU.add))
                    link(v.reciprocal(S1, T))
                    link(v.tensor_tensor(BETA, S1, E_BM, ALU.mult))
                    link(v.tensor_scalar(T, E_D, 2.0, None, ALU.add))
                    link(v.reciprocal(S2, T))
                    link(v.tensor_tensor(S1, S2, E_D, ALU.mult))
                    link(v.tensor_tensor(S2, S1, S1, ALU.mult))
                    link(v.tensor_scalar(T, S2, 2.0 / (2 * ATANH_TERMS + 1), 2.0 / (2 * ATANH_TERMS - 1),
                                         ALU.mult, ALU.add))
                    for i in range(ATANH_TERMS - 2, -1, -1):
                        link(v.tensor_tensor(T, T, S2, ALU.mult))
                        link(v.tensor_scalar(T, T, 2.0 / (2 * i + 1), None, ALU.add))
                    link(v.tensor_tensor(T, T, S1, ALU.mult))
                    link(v.tensor_tensor(T, T, POS, ALU.add))
                    done(v.tensor_tensor(G, T, over_batches(neg_a[:]), ALU.mult), g_ready, 1)
                    for n in range(NQK):
                        v.wait_ge(rn_ready, n + 1)
                        done(v.tensor_tensor(act_qkv[:, n, :], act_qkv[:, n, :], rs[:, n % 2, :], ALU.mult),
                             qk_ready, n + 1)

                    def masked_decay(h):
                        if h >= 2:
                            v.wait_ge(decay_ready, h - 1)
                        for b in range(NB):
                            ins = v.tensor_scalar(gm[:, h % 2, b, :], gt, t24[:, 0, b, h:h + 1], None, ALU.mult)
                            if b < NB - 1:
                                link(ins)
                        done(ins, gm_ready, h + 1)

                    masked_decay(0)
                    v.wait_ge(cum_exp, 1)
                    for h in range(H1):
                        n0 = h * (LEVELS - 1)
                        v.wait_ge(kk_ready, h + 1)
                        v.wait_ge(decay_exp, h + 1)
                        if h:
                            v.wait_ge(a_turned, h)
                        link(v.tensor_tensor(gam[:, h % 2, :, :], gam[:, h % 2, :, :], over_batches(gt), ALU.mult))
                        for b in range(NB):
                            ins = v.scalar_tensor_tensor(am[:, b, :], p[2][:, b * P:(b + 1) * P],
                                                         t24[:, 1, b, h:h + 1], gam[:, h % 2, b, :],
                                                         ALU.mult, ALU.mult)
                            if b < NB - 1:
                                link(ins)
                        done(ins, a_ready, h + 1)
                        link(v.tensor_tensor(pm[:, h % 2, :, :], gat[:, h % 2, :, :], over_batches(le), ALU.mult))
                        done(v.tensor_tensor(pm[:, h % 2, :, :], pm[:, h % 2, :, :], blocks(p[3]), ALU.mult),
                             pm_ready, h + 1)
                        if h:
                            v.wait_ge(u_ready, h)
                        link(v.tensor_tensor(tmp[:], am[:], over_batches(msk[:, M_OFF, :]), ALU.mult))
                        link(v.tensor_tensor(tr[:], over_batches(ident), tmp[:], ALU.subtract))
                        v.wait_ge(at_ready, h + 1)
                        link(v.tensor_tensor(tmp[:], at[:], over_batches(msk[:, M_OFF + LEVELS, :]), ALU.mult))
                        done(v.tensor_tensor(tt[:], over_batches(ident), tmp[:], ALU.subtract), t_ready, n0 + 1)
                        if h + 1 < H1:
                            masked_decay(h + 1)
                        for i in range(1, LEVELS):
                            v.wait_ge(delta_ready, n0 + i)
                            if i < LEVELS - 1:
                                link(v.tensor_tensor(tr[:], tr[:], blocks(p[6]), ALU.subtract))
                                done(v.tensor_tensor(tt[:], tt[:], blocks(p[7]), ALU.subtract),
                                     t_ready, n0 + i + 1)
                            else:
                                done(v.tensor_tensor(tt[:], tt[:], blocks(p[7]), ALU.subtract),
                                     tri_ready, h + 1)
                        v.wait_ge(ks_ready, h + 1)
                        ks, qs = blocks(p[5][:, 0:P]), blocks(p[5][:, P:2 * P])
                        link(v.tensor_tensor(r1[:, 0, :, :], ks, along(ex[:, 0, :, h], DV), ALU.mult))
                        link(v.tensor_tensor(o2[:], qs, along(ex[:, 0, :, h], DV), ALU.mult))
                        link(v.tensor_tensor(r1[:, 1, :, :], vt[:, :, h * DV:(h + 1) * DV], r1[:, 0, :, :],
                                             ALU.subtract))
                        done(v.tensor_tensor(r1[:, 2, :, :], r1[:, 1, :, :], along(t24[:, 1, :, h], DV),
                                             ALU.mult), r_ready, h + 1)
                        v.wait_ge(u_ready, h + 1)
                        ups = blocks(p[6][:, 0:P])
                        link(v.tensor_copy(u[:, 0, :, :], ups))
                        done(v.tensor_tensor(u[:, 1, :, :], ups, along(ex[:, 1, :, h], DV), ALU.mult),
                             u_taken, h + 1)
                        v.wait_ge(o_ready, h + 1)
                        link(v.tensor_tensor(o[:, :, h * DV:(h + 1) * DV], o2[:], blocks(p[7][:, 0:P]), ALU.add))
                        link(v.tensor_tensor(state[:, h, :, :], state[:, h, :, :], along(ex[:, 2, :, h], DV),
                                             ALU.mult))
                        done(v.tensor_tensor(state[:, h, :, :], state[:, h, :, :], blocks(p[7][:, P:2 * P]),
                                             ALU.add), s_ready, h + 1)
                    flat = "p b (h d) -> p (b h) d"
                    link(v.tensor_tensor(osq[:], o[:], o[:], ALU.mult))
                    done(v.tensor_reduce(om[:, 0, :], osq[:].rearrange(flat, h=H1), AX.X, ALU.add), om_ready, 1)
                    link(v.tensor_tensor(sg[:].rearrange(flat, h=H1), sg[:].rearrange(flat, h=H1),
                                         over_batches(rows[:, 2 * H1:2 * H1 + DV], NB * H1), ALU.mult))
                    v.wait_ge(ostd_ready, 1)
                    link(v.tensor_tensor(o[:].rearrange(flat, h=H1), o[:].rearrange(flat, h=H1),
                                         along(om[:, 2, :], DV), ALU.mult))
                    done(v.tensor_tensor(o[:], o[:], sg[:], ALU.mult), on_ready, 1)
                    v.wait_ge(wo_ready, 1)
                    done(v.tensor_tensor(x1[:], p[2], xt[:], ALU.add), x1_ready, 1)
                    layer_norm(2, x1[:], p[3], y[:, :, bass.ds(t * P, P)])
            nc.all_engine_barrier(sems_to_clear=range(first, x1_stored.num + 1))


def local_layers(nc, sbuf, names, p, banks, y, msk, ident, c, cols, key_mask, rot, weights):
    C_EPS, C_ZERO, C_NORM, C_NSC = cols
    mean_m, heads_m = msk[:, M_MEAN, :], msk[:, M_HEADS, :]
    qq, kk, sc = banks[:, 0:2, :], banks[:, 2:4, :], banks[:, 4:6, :]
    norm_bank, out_bank = p[6], p[7]
    sc_in = sc[:, :, 0:NB * 2 * WIN].rearrange("p h (b n) -> p h b n", b=NB)
    with ExitStack() as ctx:
        def sb(name, shape, dt=F32):
            return sbuf(ctx, name, shape, dt)

        w = sb("w2s", [P, WCOLS])
        tab = sb("tab", [P, NT, 4, P])
        kmask = sb("kmask", [P, NT, 2 * WIN], BF16)
        idb = sb("idb", [P, P], BF16)
        flag = sb("flag", [P, NT])
        kx = sb("kx", [P, NP2, NB, KX])
        v_tok = sb("v_tok", [P, NB, INNER])
        v_before = sb("v_before", [WIN, NB, INNER])
        yt = sb("yt", [P, NB, 1 + P])
        y1 = sb("y1", [P, NB, 1 + P])
        xs = sb("xs", [P, C])
        xc = sb("xc2", [P, C])
        sq = sb("sq2", [P, 2, C])
        lg = sb("lg2", [P, 2, C])
        rn = sb("rn2", [P, 2, C])
        turn = sb("turn", [P, 2, C])
        turn_k = sb("turn_k", [P, 2, C])
        qk = sb("qk", [P, 2, C])
        qf = sb("qf", [P, 2, C])
        e = sb("e", [P, 2 * NB, 2 * WIN])
        et = sb("et", [P, 2, 2 * NB, 2, WIN])
        pt = sb("pt", [P, 2, 2 * NB, P])
        stat = sb("stat", [P, 3, 2 * NB])
        ot = sb("ot2", [P, NP2, C])
        gg = ot[:, 0:FC, :]
        hid = ot[:, FC:2 * FC, :]

        w_loaded, w_init, tab_ready = names("w_loaded", "w_init", "tab_ready")
        dve_step2, act_step2, pool_step2 = names("dve_step2", "act_step2", "pool_step2")
        (xs_ready, vproj_ready, v_kept, v_taken, qproj, kproj, rot_q, rot_k, sqq_ready, sqk_ready,
         turned, nq_ready, nk_ready, lnq_done, lnk_done, rq_ready, rk_ready, q_ready, k_ready,
         scores_ready, scores_used, exp_ready, max_ready, keys_kept, prob_ready, et_ready,
         own_ready, before_ready, pv_ready, ot_ready) = names(
            "xs_ready", "vproj_ready", "v_kept", "v_taken", "qproj", "kproj", "rot_q", "rot_k",
            "sqq_ready", "sqk_ready", "turned", "nq_ready", "nk_ready", "lnq_done", "lnk_done",
            "rq_ready", "rk_ready", "q_ready", "k_ready", "scores_ready", "scores_used",
            "exp_ready", "max_ready", "keys_kept", "prob_ready", "et_ready", "own_ready",
            "before_ready", "pv_ready", "ot2_ready")
        (att_ready, xs1_ready, mean_ready, xc_ready, sq1_ready, var_ready, rstd_ready, xn_ready,
         gate_ready, a_ready, gelu_ready, hid_ready, ffn_ready, y_ready) = names(
            "att_ready", "xs1_ready", "mean2_ready", "xc2_ready", "sq1_ready", "var2_ready",
            "rstd2_ready", "xn2_ready", "gate_ready", "a2_ready", "gelu_ready", "hid_ready",
            "ffn_ready", "y_ready")

        GATE_BANKS, A_BANKS, V_BANKS = (2, 3, 4), (5, 6, 7), (4, 5, 7)

        def vec(i, n=P):
            return w[0:n, W_VEC + i:W_VEC + i + 1]

        with nc.Block() as block:
            @block.sync
            def _(sp):
                sp.dma_start(tab[:, 0, :, :].rearrange("p i n -> p (i n)"), key_mask).then_inc(w_init, 16)
                sp.wait_ge(w_init, 16)

            @block.vector
            def _(v):
                for ap in (kx, v_tok, yt, y1, pt):
                    v.memset(ap[:], 0.0)
                v.memset(flag[:], 1.0).then_inc(tab_ready, 1)
                v.wait_ge(tab_ready, 1)
                v.memset(flag[:, 0:1], 0.0).then_inc(tab_ready, 1)
                v.tensor_copy(idb[:], ident).then_inc(tab_ready, 1)
                v.wait_ge(w_init, 16)
                v.tensor_copy(kmask[:].rearrange("p t n -> p (t n)"),
                              tab[:, 0, :, :].rearrange("p i n -> p (i n)")).then_inc(tab_ready, 1)
                v.wait_ge(tab_ready, 4)
        nc.all_engine_barrier(sems_to_clear=range(w_loaded.num, tab_ready.num + 1))

        with nc.Fori(0, DEPTH) as layer:
            with nc.Block() as block:
                @block.sync
                def _(sp):
                    sp.dma_start(w[:], weights[bass.ds(layer, 1), :, :].rearrange("l p n -> p (l n)"))\
                        .then_inc(w_loaded, 16)
                    sp.dma_start(tab[:], rot).then_inc(w_loaded, 16)
                    sp.wait_ge(w_loaded, 32)

                @block.vector
                def _(v):
                    v.wait_ge(w_loaded, 32)
                    for i in range(4):
                        v.tensor_scalar(tab[:, :, i, :], tab[:, :, i, :], vec(V_ROT + i), None, ALU.mult)\
                            .then_inc(tab_ready, 1)
                    v.wait_ge(tab_ready, 4)
            nc.all_engine_barrier(sems_to_clear=range(w_loaded.num, tab_ready.num + 1))
            with nc.Fori(0, NT) as t:
                with nc.Block(no_gpsimd_drain=True) as block:
                    @block.tensor
                    def _(pe):
                        pe.wait_ge(xs_ready, 2)

                        def project(j):
                            if j:
                                pe.wait_ge(rot_q, j)
                            for i, at in enumerate((W_Q, W_QR)):
                                last = pe.matmul(qq[:, i, :], w[:, at + j * P:at + (j + 1) * P], xs[:],
                                                 start=True, stop=True)
                            last.then_inc(qproj, 1)
                            if j:
                                pe.wait_ge(rot_k, j)
                            for i, at in enumerate((W_K, W_KR)):
                                last = pe.matmul(kk[:, i, :], w[:, at + j * P:at + (j + 1) * P], xs[:],
                                                 start=True, stop=True)
                            last.then_inc(kproj, 1)

                        def v_half(n):
                            b, i = n // 2, n % 2
                            if n >= len(V_BANKS):
                                pe.wait_ge(v_taken, n - len(V_BANKS) + 1)
                            pe.matmul(p[V_BANKS[n % len(V_BANKS)]], xs[:, b * P:(b + 1) * P],
                                      w[:, W_V + i * 512:W_V + (i + 1) * 512], start=True, stop=True)\
                                .then_inc(vproj_ready, 1)

                        def norm_q(j):
                            pe.wait_ge(sqq_ready, j + 1)
                            if j:
                                pe.wait_ge(rk_ready, j)
                            pe.matmul(norm_bank, heads_m, sq[:, 0, :], start=True, stop=True)\
                                .then_inc(nq_ready, 1)

                        def norm_k(j):
                            pe.wait_ge(sqk_ready, j + 1)
                            pe.wait_ge(lnq_done, j + 1)
                            pe.matmul(norm_bank, heads_m, sq[:, 1, :], start=True, stop=True)\
                                .then_inc(nk_ready, 1)

                        def scores(j):
                            pe.wait_ge(q_ready, j + 1)
                            pe.wait_ge(k_ready, j + 1)
                            if j:
                                pe.wait_ge(scores_used, j)
                            for h in range(2):
                                pe.matmul(blocks(sc[:, h, 0:NB * 2 * WIN]), idb[:],
                                          kmask[:, bass.ds(t, 1), :].to_broadcast([P, NB, 2 * WIN]),
                                          start=True, stop=False, skip_group_check=True)
                            for b in range(NB):
                                for n in range(NW):
                                    for h in range(2):
                                        r = slice(h * DH, (h + 1) * DH)
                                        last = pe.matmul(
                                            sc[n * WIN:(n + 1) * WIN, h, b * 2 * WIN:(b + 1) * 2 * WIN],
                                            qf[r, j % 2, b * P + n * WIN:b * P + (n + 1) * WIN],
                                            kx[r, j, b, n * WIN:(n + 2) * WIN],
                                            start=False, stop=True, skip_group_check=True)
                            last.then_inc(scores_ready, 1)

                        def values(j):
                            pe.wait_ge(own_ready, j + 1)
                            pe.wait_ge(before_ready, j + 1)
                            if j:
                                pe.wait_ge(ot_ready, j)
                            for h in range(2):
                                col = (2 * j + h) * DH
                                r = slice(h * DH, (h + 1) * DH)
                                for b in range(NB):
                                    pe.matmul(out_bank[r, b * P:(b + 1) * P], v_tok[:, b, col:col + DH],
                                              pt[:, j % 2, h * NB + b, :], start=True, stop=False,
                                              skip_group_check=True)
                                    last = pe.matmul(out_bank[r, b * P:b * P + WIN],
                                                     v_before[:, b, col:col + DH],
                                                     et[0:WIN, j % 2, h * NB + b, 0, :],
                                                     start=False, stop=True, skip_group_check=True)
                            last.then_inc(pv_ready, 1)

                        project(0)
                        for n in range(3):
                            v_half(n)
                        norm_q(0)
                        v_half(3)
                        norm_k(0)
                        for n in range(4, 2 * NB):
                            v_half(n)
                        pe.wait_ge(v_taken, 2 * NB)
                        scores(0)
                        for j in range(NP2):
                            if j + 1 < NP2:
                                project(j + 1)
                                norm_q(j + 1)
                                norm_k(j + 1)
                            values(j)
                            if j + 1 < NP2:
                                scores(j + 1)
                        pe.wait_ge(rk_ready, NP2)
                        pe.wait_ge(ot_ready, NP2)
                        for j in range(NP2):
                            last = pe.matmul(norm_bank, w[:, W_O + j * P:W_O + (j + 1) * P], ot[:, j, :],
                                             start=(j == 0), stop=(j == NP2 - 1))
                        last.then_inc(att_ready, 1)
                        pe.wait_ge(xs1_ready, 2)
                        pe.matmul(p[0], mean_m, xs[:], start=True, stop=True).then_inc(mean_ready, 1)
                        pe.wait_ge(sq1_ready, 1)
                        pe.matmul(p[1], mean_m, sq[:, 0, :], start=True, stop=True).then_inc(var_ready, 1)
                        pe.wait_ge(xn_ready, 1)
                        for i, b in enumerate(GATE_BANKS):
                            n = FROWS[i]
                            pe.matmul(p[b][0:n, :], w[:, W_1 + FF + i * P:W_1 + FF + i * P + n], xs[:],
                                      start=True, stop=True).then_inc(gate_ready, 1)
                        for i, b in enumerate(A_BANKS):
                            n = FROWS[i]
                            pe.matmul(p[b][0:n, :], w[:, W_1 + i * P:W_1 + i * P + n], xs[:],
                                      start=True, stop=True).then_inc(a_ready, 1)
                        for i in range(FC):
                            n = FROWS[i]
                            pe.wait_ge(hid_ready, i + 1)
                            last = pe.matmul(p[1], w[0:n, W_2 + i * P:W_2 + (i + 1) * P], hid[0:n, i, :],
                                             start=(i == 0), stop=(i == FC - 1))
                        last.then_inc(ffn_ready, 1)
                        pe.wait_ge(ffn_ready, 1)

                    @block.scalar
                    def _(a):
                        link = linker(a, act_step2)

                        def squares(j):
                            a.wait_ge(qproj, j + 1)
                            if j:
                                a.wait_ge(nq_ready, j)
                            a.activation(sq[:, 0, :], qq[:, 0, :], ACT.Square).then_inc(sqq_ready, 1)
                            a.wait_ge(kproj, j + 1)
                            if j:
                                a.wait_ge(nk_ready, j)
                            a.activation(sq[:, 1, :], kk[:, 0, :], ACT.Square).then_inc(sqk_ready, 1)

                        def inverse_norm(j, i):
                            ready, ln_sem, sem, used = ((nq_ready, lnq_done, rq_ready, q_ready),
                                                        (nk_ready, lnk_done, rk_ready, k_ready))[i]
                            a.wait_ge(ready, j + 1)
                            a.activation(lg[:, i, :], norm_bank, ACT.Ln, scale=2.0 ** LN_SHIFT,
                                         bias=c(C_NORM)).then_inc(ln_sem, 1)
                            a.wait_ge(ln_sem, j + 1)
                            if j:
                                a.wait_ge(used, j)
                            a.activation(rn[:, i, :], lg[:, i, :], ACT.Exp, scale=-0.5,
                                         bias=c(C_NSC)).then_inc(sem, 1)

                        def take_v(n):
                            b, i = n // 2, n % 2
                            a.wait_ge(vproj_ready, n + 1)
                            a.activation(v_tok[:, b, i * 512:(i + 1) * 512], p[V_BANKS[n % len(V_BANKS)]],
                                         ACT.Copy).then_inc(v_taken, 1)

                        a.preload_act_table_set(LN_EXP)
                        squares(0)
                        a.wait_ge(v_kept, 1)
                        for n in range(3):
                            take_v(n)
                        inverse_norm(0, 0)
                        take_v(3)
                        inverse_norm(0, 1)
                        for n in range(4, 2 * NB):
                            take_v(n)
                        for j in range(NP2):
                            a.wait_ge(scores_used, j + 1)
                            a.activation(e[:], e[:], ACT.Exp, scale=QK_SCALE).then_inc(exp_ready, 1)
                            if j + 1 < NP2:
                                squares(j + 1)
                            a.wait_ge(et_ready, j + 1)
                            if j >= 2:
                                a.wait_ge(pv_ready, j - 1)
                            for n in range(NW):
                                r = slice(n * WIN, (n + 1) * WIN)
                                last = a.activation(pt[r, j % 2, :, n * WIN:(n + 1) * WIN],
                                                    et[r, j % 2, :, 1, :], ACT.Copy)
                            last.then_inc(own_ready, 1)
                            if j + 1 < NP2:
                                inverse_norm(j + 1, 0)
                                inverse_norm(j + 1, 1)
                            a.wait_ge(pv_ready, j + 1)
                            a.activation(ot[:, j, :], out_bank, ACT.Copy).then_inc(ot_ready, 1)
                        a.wait_ge(xc_ready, 1)
                        a.wait_ge(ot_ready, NP2)
                        a.activation(sq[:, 0, :], xc[:], ACT.Square).then_inc(sq1_ready, 1)
                        a.wait_ge(var_ready, 1)
                        link(a.activation(lg[:, 0, :], p[1], ACT.Ln, bias=c(C_EPS)))
                        a.activation(rn[:, 0, :], lg[:, 0, :], ACT.Exp, scale=-0.5).then_inc(rstd_ready, 1)
                        for i, b in enumerate(GATE_BANKS):
                            n = FROWS[i]
                            a.wait_ge(gate_ready, i + 1)
                            a.activation(gg[0:n, i, :], p[b][0:n, :], ACT.Gelu, bias=vec(V_GATE + i, n))\
                                .then_inc(gelu_ready, 1)
                        a.wait_ge(gelu_ready, FC)

                    @block.gpsimd
                    def _(g):
                        for j in range(NP2):
                            for i, (ready, used) in enumerate(((rot_q, q_ready), (rot_k, k_ready))):
                                g.wait_ge(ready, j + 1)
                                if j:
                                    g.wait_ge(used, j)
                                src = turn if i == 0 else turn_k
                                g.tensor_tensor(qk[:, i, :], src[:, 0, :], src[:, 1, :], ALU.add)\
                                    .then_inc(turned, 1)
                        g.wait_ge(turned, 2 * NP2)

                    @block.vector
                    def _(v):
                        link = linker(v, dve_step2)

                        def done(ins, sem, n):
                            ins.then_inc(sem, 1)
                            v.wait_ge(sem, n)

                        def shifted(src, sem):
                            half = P // 2
                            done(v.tensor_copy(blocks(xs[0:half, :]), src[0:half, :, 1:1 + P]), sem, 1)
                            done(v.tensor_copy(blocks(xs[half:P, :]), src[half:P, :, 0:P]), sem, 2)

                        first_flag = flag[:, bass.ds(t, 1)]
                        link(v.tensor_scalar(yt[:, :, 0:1], yt[:, :, P:P + 1], first_flag, None, ALU.mult))
                        link(v.tensor_copy(yt[:, :, 1:1 + P], y[:, :, bass.ds(t * P, P)]))
                        shifted(yt, xs_ready)
                        done(v.tensor_copy(v_before[:], v_tok[P - WIN:P, :, :]), v_kept, 1)

                        def rotate(j, i):
                            ready, sem, src, dst = ((sqq_ready, rot_q, qq, turn), (sqk_ready, rot_k, kk, turn_k))[i]
                            v.wait_ge(ready, j + 1)
                            if j:
                                v.wait_ge(turned, 2 * j - 1 + i)
                            table = tab[:, bass.ds(t, 1), 2 * i:2 * i + 2, :].rearrange("p o s n -> p (o s) n")
                            v.tensor_tensor(dst[:].rearrange("p s (b n) -> p s b n", b=NB),
                                            src.rearrange("p s (b n) -> p s b n", b=NB),
                                            table.unsqueeze(2).to_broadcast([P, 2, NB, P]), ALU.mult)\
                                .then_inc(sem, 1)

                        def keep_keys(j):
                            v.tensor_scalar(kx[:, j, :, 0:WIN], kx[:, j, :, P:KX], first_flag, None, ALU.mult)\
                                .then_inc(keys_kept, 1)

                        def unit(j):
                            v.wait_ge(turned, 2 * j + 1)
                            v.wait_ge(rq_ready, j + 1)
                            if j >= 2:
                                v.wait_ge(scores_ready, j - 1)
                            v.tensor_tensor(qf[:, j % 2, :], qk[:, 0, :], rn[:, 0, :], ALU.mult)\
                                .then_inc(q_ready, 1)
                            v.wait_ge(keys_kept, j + 1)
                            v.wait_ge(turned, 2 * j + 2)
                            v.wait_ge(rk_ready, j + 1)
                            v.tensor_tensor(kx[:, j, :, WIN:KX], blocks(qk[:, 1, :]),
                                            blocks(rn[:, 1, :]), ALU.mult).then_inc(k_ready, 1)

                        rotate(0, 0)
                        rotate(0, 1)
                        keep_keys(0)
                        unit(0)
                        for j in range(NP2):
                            v.wait_ge(scores_ready, j + 1)
                            v.tensor_reduce(stat[:, 0, :].rearrange("p (h b) -> p h b", h=2), sc_in, AX.X,
                                            ALU.max).then_inc(max_ready, 1)
                            v.wait_ge(max_ready, j + 1)
                            if j:
                                v.wait_ge(et_ready, j)
                            v.tensor_tensor(e[:].rearrange("p (h b) n -> p h b n", h=2), sc_in,
                                            stat[:, 0, :].rearrange("p (h b) -> p h b", h=2).unsqueeze(3)
                                            .to_broadcast([P, 2, NB, 2 * WIN]), ALU.subtract)\
                                .then_inc(scores_used, 1)
                            if j + 1 < NP2:
                                keep_keys(j + 1)
                            v.wait_ge(exp_ready, j + 1)
                            link(v.tensor_reduce(stat[:, 1, :], e[:], AX.X, ALU.add))
                            link(v.reciprocal(stat[:, 2, :], stat[:, 1, :]))
                            v.tensor_tensor(e[:], e[:], along(stat[:, 2, :], 2 * WIN), ALU.mult)\
                                .then_inc(prob_ready, 1)
                            v.wait_ge(prob_ready, j + 1)
                            if j >= 2:
                                v.wait_ge(pv_ready, j - 1)
                            v.transpose(et[:, j % 2, :, :, :].rearrange("p m s n -> p (m s n)"),
                                        e[:].rearrange("p m n -> p (m n)")).then_inc(et_ready, 1)
                            v.wait_ge(et_ready, j + 1)
                            for n in range(1, NW):
                                last = v.tensor_copy(pt[(n - 1) * WIN:n * WIN, j % 2, :, n * WIN:(n + 1) * WIN],
                                                     et[n * WIN:(n + 1) * WIN, j % 2, :, 0, :])
                            last.then_inc(before_ready, 1)
                            if j + 1 < NP2:
                                rotate(j + 1, 0)
                                rotate(j + 1, 1)
                                unit(j + 1)
                        v.wait_ge(att_ready, 1)
                        link(v.tensor_scalar(y1[:, :, 0:1], y1[:, :, P:P + 1], first_flag, None, ALU.mult))
                        link(v.tensor_tensor(y1[:, :, 1:1 + P], blocks(norm_bank), yt[:, :, 1:1 + P], ALU.add))
                        shifted(y1, xs1_ready)
                        v.wait_ge(mean_ready, 1)
                        done(v.tensor_tensor(xc[:], xs[:], p[0], ALU.subtract), xc_ready, 1)
                        v.wait_ge(rstd_ready, 1)
                        link(v.tensor_tensor(xc[:], xc[:], rn[:, 0, :], ALU.mult))
                        done(v.tensor_scalar(xs[:], xc[:], vec(V_G), vec(V_B), ALU.mult, ALU.add), xn_ready, 1)
                        for i, b in enumerate(A_BANKS):
                            n = FROWS[i]
                            v.wait_ge(a_ready, i + 1)
                            v.wait_ge(gelu_ready, i + 1)
                            done(v.scalar_tensor_tensor(hid[0:n, i, :], p[b][0:n, :], vec(V_A + i, n),
                                                        gg[0:n, i, :], ALU.add, ALU.mult), hid_ready, i + 1)
                        v.wait_ge(ffn_ready, 1)
                        done(v.scalar_tensor_tensor(y[:, :, bass.ds(t * P, P)], blocks(p[1]), vec(V_B2),
                                                    y1[:, :, 1:1 + P], ALU.add, ALU.add), y_ready, 1)
                nc.all_engine_barrier(sems_to_clear=range(dve_step2.num, y_ready.num + 1))


def final_sum(nc, sbuf, names, p, y, ident, x1_dram, out):
    with ExitStack() as ctx:
        x1 = sbuf(ctx, "x1f", [P, NB, P])
        s = sbuf(ctx, "sf", [P, NB, P])
        o = sbuf(ctx, "of", [P, NB, P])
        x1_loaded, sum_ready, sum_turned, out_ready, out_stored = names(
            "x1_loaded", "sum_ready", "sum_turned", "out_ready", "out_stored")
        with nc.Fori(0, NT) as t:
            with nc.Block(no_gpsimd_drain=True) as block:
                @block.sync
                def _(sp):
                    sp.dma_start(x1[:], x1_dram[:, :, bass.ds(t * P, P)]).then_inc(x1_loaded, 16)
                    sp.wait_ge(out_ready, 1)
                    sp.dma_start(out[:, bass.ds(t * P, P), :].rearrange("b p d -> p b d"), o[:])\
                        .then_inc(out_stored, 16)
                    sp.wait_ge(out_stored, 16)

                @block.vector
                def _(v):
                    v.wait_ge(x1_loaded, 16)
                    v.tensor_tensor(s[:], x1[:], y[:, :, bass.ds(t * P, P)], ALU.add).then_inc(sum_ready, 1)
                    v.wait_ge(sum_ready, 1)

                @block.tensor
                def _(pe):
                    pe.wait_ge(sum_ready, 1)
                    for b in range(NB):
                        last = pe.transpose(p[0][:, b * P:(b + 1) * P], s[:, b, :], ident)
                    last.then_inc(sum_turned, 1)
                    pe.wait_ge(sum_turned, 1)

                @block.scalar
                def _(a):
                    a.wait_ge(sum_turned, 1)
                    a.activation(o[:], blocks(p[0]), ACT.Copy).then_inc(out_ready, 1)
                    a.wait_ge(out_ready, 1)
            nc.all_engine_barrier(sems_to_clear=range(x1_loaded.num, out_stored.num + 1))


def shape_constants():
    i, j = np.arange(P)[:, None], np.arange(P)[None, :]
    m = np.zeros((P, NM, P), np.float32)
    m[:, M_ID], m[:, M_LE], m[:, M_GT] = i == j, i <= j, i > j
    m[:, M_MEAN], m[:, M_ONES], m[:, M_HEADS] = 1.0 / P, 1.0, i // DH == j // DH
    for n in range(LEVELS):
        s = 1 << n
        low = (i // (2 * s) == j // (2 * s)) & (i // s % 2 == 1) & (j // s % 2 == 0)
        m[:, M_OFF + n], m[:, M_OFF + LEVELS + n] = low, low.T
    key = np.zeros((P, NT, 2 * WIN), np.float32)
    r, k = (np.arange(P) % WIN)[:, None], np.arange(2 * WIN)[None, :]
    hidden = np.where(k < WIN, k < r, k - WIN > r)
    key[:] = np.where(hidden, MASKED, 0.0)[:, None, :]
    key[0:WIN, 0, 0:WIN] = MASKED
    half = np.arange(0, DH, 2, dtype=np.float32)
    inv_freq = (1.0 / 10000.0 ** (half / np.float32(DH))).astype(np.float32)
    pos = np.arange(L, dtype=np.float32)
    f = (pos[:, None] * inv_freq[None, :]).astype(np.float32).astype(np.float64)
    base = ((half + np.float32(0.4 * DH)) / np.float32(1.4 * DH)).astype(np.float64)
    scale = base[None, :] ** ((pos - L // 2) / (WIN // 2))[:, None].astype(np.float64)
    tab = np.zeros((4, P, L))
    for d in range(P):
        n = d % (DH // 2)
        sign = -1.0 if d % DH < DH // 2 else 1.0
        cos, sin, s = np.cos(f[:, n]), np.sin(f[:, n]), scale[:, n]
        tab[:, d] = cos * s, sign * sin * s, cos / s, sign * sin / s
    tab = tab.reshape(4, P, NT, P).transpose(1, 2, 0, 3).astype(np.float32)
    return m, key.reshape(P, NT * 2 * WIN), np.ascontiguousarray(tab)


def laid_out(d):
    g = {k: np.asarray(v) for k, v in d.items()}
    a = {k[8:]: v for k, v in g.items() if k.startswith("L0_attn_")}
    f = {k[7:]: v for k, v in g.items() if k.startswith("L0_ffn_")}

    def rows(m, n):
        full = np.zeros((n * P, m.shape[1]), np.float32)
        full[:m.shape[0]] = m
        return full.reshape(n, P, -1).transpose(1, 0, 2).reshape(P, -1)

    w1 = np.concatenate([a["Wq"], a["Wk"], a["Wv"], a["Wg"], a["Wb"], a["Wa"]], axis=1)
    conv = rows(np.concatenate([a["conv_q"], a["conv_k"], a["conv_v"]]), NCH).reshape(P, NCH, KS)
    wo1 = rows(a["Wo"], 2).reshape(P, 2, P)
    rows1 = np.concatenate([a["A_log"], a["dt_bias"], a["norm_w"]])
    d_of = np.arange(P) % DH
    swap = (d_of + DH // 2) % DH
    cols = np.arange(INNER)
    swapped = cols // DH * DH + (cols % DH + DH // 2) % DH
    per_layer = []
    for i in range(DEPTH):
        wq, wk = f["Wqkv"][i][:, 0:INNER], f["Wqkv"][i][:, INNER:2 * INNER]
        vec = np.zeros((P, WCOLS - W_VEC), np.float32)
        vec[:, V_G], vec[:, V_B], vec[:, V_B2] = f["ln_g"][i], f["ln_b"][i], f["b2"][i]
        for n in range(FC):
            vec[:FROWS[n], V_A + n] = f["b1"][i][n * P:n * P + FROWS[n]]
            vec[:FROWS[n], V_GATE + n] = f["b1"][i][FF + n * P:FF + n * P + FROWS[n]]
        for n, s in enumerate((f["q_scale"][i], f["k_scale"][i])):
            vec[:, V_ROT + 2 * n], vec[:, V_ROT + 2 * n + 1] = s[d_of], s[swap]
        per_layer.append(np.concatenate([f["Wqkv"][i], wq[:, swapped], wk[:, swapped], f["W1"][i],
                                         rows(f["Wo"][i], NP2), rows(f["W2"][i], FC), vec], axis=1))
    masks, key_mask, rot = shape_constants()
    return {"x": a["x"], "w1": w1, "conv": conv, "wo1": wo1, "rows1": rows1, "masks": masks,
            "key_mask": key_mask, "rot": rot, "weights": np.stack(per_layer)}


def program(nc, arrays):
    ap = {n: nc.dram_tensor(f"in_{n}", v.shape, mybir.dt.from_np(v.dtype), kind="ExternalInput").ap()
          for n, v in arrays.items()}
    out = nc.dram_tensor("out", (NB, L, P), F32, kind="ExternalOutput").ap()
    x1_dram = nc.dram_tensor("x1_dram", (P, NB, L), F32, kind="Internal").ap()
    build(nc, ap["x"], ap["w1"], ap["conv"], ap["wo1"], ap["rows1"], ap["masks"],
          ap["key_mask"], ap["rot"], ap["weights"], out, x1_dram)


def kernel(**inputs):
    import concourse.bacc as bacc
    from concourse.bass_utils import run_bass_kernel_spmd as run

    nc = bacc.Bacc("TRN2", target_bir_lowering=False, num_devices=1)
    arrays = {n: np.ascontiguousarray(v) for n, v in laid_out(inputs).items()}
    program(nc, arrays)
    r = run(nc, [{f"in_{n}": v for n, v in arrays.items()}], core_ids=[0])
    return r.results[0]["out"]
```

```python
from contextlib import ExitStack

import numpy as np

import concourse.bass as bass
from concourse import mybir

ALU = mybir.AluOpType
ACT = mybir.ActivationFunctionType
AX = mybir.AxisListType
F32 = mybir.dt.float32
BF16 = mybir.dt.bfloat16

P = 128
NB = 4
L = 1024
NT = L // P
C = NB * P
EPS = 1e-5

H1, DV, KS = 6, 32, 4
VD = H1 * DV
NQK = 2 * H1
NCH = NQK + 2
GW = VD + 2 * H1
LEVELS = 7
ATANH_TERMS = 9
PRE = 4

DEPTH, HEADS, DH, WIN = 6, 16, 64, 32
INNER = HEADS * DH
NP2 = HEADS // 2
FF = 341
FC = 3
FROWS = [P, P, FF - 2 * P]
KX = WIN + P
NW = P // WIN
QK_SCALE = 8.0
MASKED = -1e30
LN_EXP = "natural_log_exp_and_others"
LN_SHIFT = 20

W_Q, W_K, W_V = 0, INNER, 2 * INNER
W_QR, W_KR = 3 * INNER, 4 * INNER
W_1 = 5 * INNER
W_O = W_1 + 2 * FF
W_2 = W_O + NP2 * P
W_VEC = W_2 + FC * P
V_G, V_B, V_A, V_GATE, V_B2, V_ROT = 0, 1, 2, 5, 8, 9
WCOLS = W_VEC + 13

M_ID, M_LE, M_GT, M_MEAN, M_ONES, M_HEADS, M_OFF = 0, 1, 2, 3, 4, 5, 6
NM = M_OFF + 2 * LEVELS


def linker(eng, sem):
    count = [0]

    def link(ins):
        count[0] += 1
        ins.then_inc(sem, 1)
        eng.wait_ge(sem, count[0])

    return link


def over_batches(ap, n=NB):
    return ap.unsqueeze(1).to_broadcast([ap.shape[0], n, ap.shape[1]])


def along(ap, m):
    return ap.unsqueeze(2).to_broadcast([ap.shape[0], ap.shape[1], m])


def blocks(ap, n=NB):
    return ap.rearrange("p (b n) -> p b n", b=n)


def build(nc, x, w1, conv, wo1, rows1, masks, key_mask, rot, weights, out, x1_dram):
    with ExitStack() as whole:
        def names(*words):
            return [whole.enter_context(nc.semaphore(w)) for w in words]

        def sbuf(ctx, name, shape, dt=F32):
            return ctx.enter_context(nc.sbuf_tensor(name, shape, dt))

        banks = whole.enter_context(nc.psum_tensor("banks", [P, 8, 512], F32))
        p = [banks[:, i, :] for i in range(8)]

        y = sbuf(whole, "y", [P, NB, 1 + L])
        msk = sbuf(whole, "msk", [P, NM, P])
        cst = sbuf(whole, "cst", [P, 8])
        ident = msk[:, M_ID, :]
        ones = msk[:, M_ONES, :]
        C_EPS, C_L2, C_QSC, C_ZERO, C_NORM, C_NSC = range(6)

        def c(i):
            return cst[:, i:i + 1]

        load_done, init_done = names("load_done", "init_done")
        delta_layer(nc, sbuf, names, p, y, msk, ident, ones, cst, c,
                    (C_EPS, C_L2, C_QSC, C_ZERO, C_NORM, C_NSC), load_done, init_done,
                    x, w1, conv, wo1, rows1, masks, x1_dram)
        local_layers(nc, sbuf, names, p, banks, y, msk, ident, c,
                     (C_EPS, C_ZERO, C_NORM, C_NSC), key_mask, rot, weights)
        final_sum(nc, sbuf, names, p, y, ident, x1_dram, out)


def delta_layer(nc, sbuf, names, p, y, msk, ident, ones, cst, c, cols, load_done, init_done,
                x, w1, conv, wo1, rows1, masks, x1_dram):
    C_EPS, C_L2, C_QSC, C_ZERO, C_NORM, C_NSC = cols
    le, gt, mean_m = msk[:, M_LE, :], msk[:, M_GT, :], msk[:, M_MEAN, :]
    with ExitStack() as ctx:
        def sb(name, shape, dt=F32):
            return sbuf(ctx, name, shape, dt)

        w = sb("w1s", [P, NQK * P + VD + GW])
        cw = sb("cw", [P, NCH, KS])
        wo = sb("wo1s", [P, 2, P])
        rows = sb("rows", [P, 2 * H1 + DV])
        neg_a = sb("neg_a", [P, H1])
        pre = sb("pre", [P, PRE, NB, KS - 1 + P])
        tail = sb("tail", [P, NCH, NB, KS - 1])
        act_qkv = sb("act_qkv", [P, NCH, C])
        state = sb("state", [P, H1, NB, DV])
        xin = sb("xin", [P, NB, P])
        xt = sb("xt", [P, C])
        xc = sb("xc", [P, C])
        xn = sb("xn", [P, C])
        sq = sb("sq", [P, 2, C])
        lg = sb("lg", [P, 2, C])
        rs = sb("rs", [P, 2, C])
        cv = sb("cv", [P, PRE, C])
        vt = sb("vt", [P, NB, VD])
        sg = sb("sg", [P, NB, VD])
        ba = sb("ba", [P, NB, 2 * H1])
        t24 = sb("t24", [P, 12, NB, H1])
        ex = sb("ex", [P, 3, NB, H1])
        gm = sb("gm", [P, 2, NB, P])
        gam = sb("gam", [P, 2, NB, P])
        gat = sb("gat", [P, 2, NB, P])
        am = sb("am", [P, 2, NB, P])
        at = sb("at", [P, 2, NB, P])
        tmp = sb("tmp", [P, 2, NB, P])
        kt = sb("kt", [P, 2, NB, P])
        tt = sb("tt", [P, 2, NB, P])
        tr = sb("tr", [P, 2, NB, P])
        p1 = sb("p1", [P, 2, NB, P])
        pm = sb("pm", [P, 4, NB, P])
        ao = sb("ao", [P, 4, NB, P])
        r1 = sb("r1", [P, 2, 3, NB, DV])
        u = sb("u", [P, 2, 2, NB, DV])
        o = sb("o", [P, NB, VD])
        o2 = sb("o2", [P, 2, NB, DV])
        ot = sb("ot", [P, 2, C])
        osq = sb("osq", [P, NB, VD])
        om = sb("om", [P, 4, NB * H1])
        x1 = sb("x1", [P, C])

        dve_step, act_step, pool_step = names("dve_step", "act_step", "pool_step")
        (x_loaded, x_turned, xt_ready, mean_ready, xc_ready, lnsq_ready, var_ready, rstd_ready,
         xn_ready, proj_ready, pre_ready, conv_ready, silu_ready, gates_ready, gates_taken,
         sq_ready, ss_ready, rn_ready, qk_ready, front_ready, tail_kept, tap_ready, ln_done,
         conv_step) = names(
            "x_loaded", "x_turned", "xt_ready", "mean_ready", "xc_ready", "lnsq_ready", "var_ready",
            "rstd_ready", "xn_ready", "proj_ready", "pre_ready", "conv_ready", "silu_ready",
            "gates_ready", "gates_taken", "sq_ready", "ss_ready", "rn_ready", "qk_ready",
            "front_ready", "tail_kept", "tap_ready", "ln_done", "conv_step")
        (v_turned, v_ready, e1_asked, e1_ready, g_ready, cum_ready, cum_exp, gm_ready, decay_ready,
         decay_exp, kk_ready, a_ready, a_turned, at_ready, t_ready, ao_ready, p1_ready, p1_taken,
         delta_ready, tri_ready, ktok_ready, kt_ready, pm_ready) = names(
            "v_turned", "v_ready", "e1_asked", "e1_ready", "g_ready", "cum_ready", "cum_exp",
            "gm_ready", "decay_ready", "decay_exp", "kk_ready", "a_ready", "a_turned", "at_ready",
            "t_ready", "ao_ready", "p1_ready", "p1_taken", "delta_ready", "tri_ready", "ktok_ready",
            "kt_ready", "pm_ready")
        (ks_ready, r_ready, u_ready, u_taken, o_ready, s_ready, o_done, om_ready, ostd_ready,
         on_ready, on_turned, ot_ready, wo_ready, x1_ready, x1_stored) = names(
            "ks_ready", "r_ready", "u_ready", "u_taken", "o_ready", "s_ready", "o_done", "om_ready",
            "ostd_ready", "on_ready", "on_turned", "ot_ready", "wo_ready", "x1_ready", "x1_stored")

        with nc.Block() as block:
            @block.sync
            def _(sp):
                for dst, src in ((w[:], w1), (cw[:], conv), (wo[:], wo1), (msk[:], masks),
                                 (rows[:], rows1.partition_broadcast(P))):
                    sp.dma_start(dst, src).then_inc(load_done, 16)
                sp.wait_ge(load_done, 5 * 16)

            @block.vector
            def _(v):
                for i, value in ((C_EPS, EPS), (C_L2, 1e-12), (C_QSC, -0.5 * float(np.log(P))),
                                 (C_ZERO, 0.0), (C_NORM, 1e-24 * 2.0 ** LN_SHIFT),
                                 (C_NSC, 0.5 * LN_SHIFT * float(np.log(2.0)))):
                    v.memset(c(i), value)
                v.memset(tail[:], 0.0)
                v.memset(act_qkv[:], 0.0)
                v.memset(cv[:], 0.0)
                v.memset(state[:], 0.0).then_inc(init_done, 1)
                v.wait_ge(init_done, 1)
                v.wait_ge(init_done, 2)
                v.tensor_scalar(neg_a[:], neg_a[:], -1.0, None, ALU.mult).then_inc(init_done, 1)
                v.wait_ge(init_done, 3)

            @block.scalar
            def _(a):
                a.wait_ge(load_done, 5 * 16)
                a.wait_ge(init_done, 1)
                a.activation(neg_a[:], rows[:, 0:H1], ACT.Exp).then_inc(init_done, 1)
                a.wait_ge(init_done, 3)

        first = dve_step.num
        with nc.Fori(0, NT) as t:
            with nc.Block(no_gpsimd_drain=True) as block:
                @block.sync
                def _(sp):
                    sp.dma_start(xin[:], x[:, bass.ds(t * P, P), :].rearrange("b p d -> p b d"))\
                        .then_inc(x_loaded, 16)
                    sp.wait_ge(x_loaded, 16)
                    sp.wait_ge(x1_ready, 1)
                    sp.dma_start(x1_dram[:, :, bass.ds(t * P, P)], blocks(x1[:])).then_inc(x1_stored, 16)
                    sp.wait_ge(x1_stored, 16)

                @block.tensor
                def _(pe):
                    pe.wait_ge(x_loaded, 16)
                    for b in range(NB):
                        last = pe.transpose(p[0][:, b * P:(b + 1) * P], xin[:, b, :], ident)
                    last.then_inc(x_turned, 1)
                    pe.wait_ge(xt_ready, 1)
                    pe.matmul(p[1], mean_m, xt[:], start=True, stop=True).then_inc(mean_ready, 1)
                    pe.wait_ge(lnsq_ready, 1)
                    pe.matmul(p[0], mean_m, sq[:, 0, :], start=True, stop=True).then_inc(var_ready, 1)
                    pe.wait_ge(xn_ready, 1)
                    for n in range(NCH):
                        m = P if n < NCH - 1 else VD - P
                        if n >= 4:
                            pe.wait_ge(tap_ready, n - 3)
                        pe.matmul(p[n % 4][0:m, :], w[:, n * P:n * P + m], xn[:], start=True, stop=True)\
                            .then_inc(proj_ready, 1)
                    for b in range(NB):
                        last = pe.matmul(p[4 + b // 2][:, (b % 2) * GW:(b % 2 + 1) * GW],
                                         xn[:, b * P:(b + 1) * P], w[:, NQK * P + VD:NQK * P + VD + GW],
                                         start=True, stop=True)
                    last.then_inc(gates_ready, 1)
                    pe.wait_ge(silu_ready, NCH)
                    for b in range(NB):
                        at_b = p[6 + b // 2][:, (b % 2) * VD:(b % 2 + 1) * VD]
                        pe.transpose(at_b[:, 0:P], act_qkv[:, NQK, b * P:(b + 1) * P], ident)
                        last = pe.transpose(at_b[:, P:VD], act_qkv[0:VD - P, NQK + 1, b * P:(b + 1) * P],
                                            ident[0:VD - P, 0:VD - P])
                    last.then_inc(v_turned, 1)
                    def norms(chunks):
                        for n in chunks:
                            pe.wait_ge(sq_ready, n + 1)
                            if n >= 2:
                                pe.wait_ge(ln_done, n - 1)
                            pe.matmul(p[n % 2], ones, sq[:, n % 2, :], start=True, stop=True)\
                                .then_inc(ss_ready, 1)

                    def decay(h):
                        pe.wait_ge(gm_ready, h + 1)
                        if h:
                            pe.wait_ge(pm_ready, h)
                        for b in range(NB):
                            s = slice(b * P, (b + 1) * P)
                            pe.matmul(p[6][:, s], gm[:, h % 2, b, :], le, start=True, stop=True)
                            last = pe.matmul(p[7][:, s], le, gm[:, h % 2, b, :], start=True, stop=True)
                        last.then_inc(decay_ready, 1)

                    def products(h):
                        pe.wait_ge(decay_exp, h + 1)
                        for b in range(NB):
                            s = slice(b * P, (b + 1) * P)
                            k_b, q_b = act_qkv[:, H1 + h, s], act_qkv[:, h, s]
                            pe.matmul(p[6][:, s], k_b, k_b, start=True, stop=True)
                            last = pe.matmul(p[7][:, s], k_b, q_b, start=True, stop=True)
                        last.then_inc(kk_ready, 1)

                    def turn_a(h):
                        pe.wait_ge(a_ready, h + 1)
                        pe.wait_ge(pm_ready, h - h % 2 + 2)
                        for b in range(NB):
                            last = pe.transpose(p[6 + h % 2][:, b * P:(b + 1) * P], am[:, h % 2, b, :], ident)
                        last.then_inc(a_turned, 1)

                    def turn_k(h):
                        pe.wait_ge(at_ready, h + 1)
                        for b in range(NB):
                            last = pe.transpose(p[6 + h % 2][:, b * P:(b + 1) * P],
                                                act_qkv[:, H1 + h, b * P:(b + 1) * P], ident)
                        last.then_inc(ktok_ready, 1)

                    pe.wait_ge(tap_ready, NCH)
                    norms(range(H1))
                    pe.wait_ge(g_ready, 1)
                    pe.wait_ge(gates_taken, 2)
                    g = t24[:, 0, :, :].rearrange("p b h -> p (b h)")
                    for i, m in enumerate((le, gt, ones)):
                        last = pe.matmul(p[5][:, i * NB * H1:(i + 1) * NB * H1], m, g, start=True, stop=True)
                    last.then_inc(cum_ready, 1)
                    pe.wait_ge(v_ready, 2)
                    decay(0)
                    norms(range(H1, NQK))
                    pe.wait_ge(cum_exp, 1)
                    pe.wait_ge(qk_ready, NQK)
                    products(0)
                    decay(1)
                    products(1)
                    for h in range(2):
                        turn_a(h)
                    for h in range(2):
                        turn_k(h)
                    for pair in range(H1 // 2):
                        heads = (2 * pair, 2 * pair + 1)
                        for i in range(1, LEVELS):
                            n = [pair * 2 * (LEVELS - 1) + 2 * (i - 1) + x + 1 for x in range(2)]
                            for x in range(2):
                                pe.wait_ge(t_ready, n[x])
                                pe.wait_ge(ao_ready, n[x])
                                if i == 1 and pair:
                                    pe.wait_ge(r_ready, 2 * pair - 1 + x)
                                for b in range(NB):
                                    last = pe.matmul(p[3 * x][:, b * P:(b + 1) * P], ao[:, 2 * x + i % 2, b, :],
                                                     tr[:, x, b, :], start=True, stop=True)
                                last.then_inc(p1_ready, 1)
                            if pair + 1 < H1 // 2 and 1 <= i <= 4:
                                if i == 1:
                                    pe.wait_ge(kt_ready, 2 * pair + 2)
                                (decay, products)[(i - 1) % 2](2 * pair + 2 + (i - 1) // 2)
                            for x in range(2):
                                pe.wait_ge(p1_taken, n[x])
                                if i == 1 and pair:
                                    pe.wait_ge(u_taken, 2 * pair - 1 + x)
                                    pe.wait_ge(s_ready, 2 * pair - 1 + x)
                                if i < LEVELS - 1:
                                    for b in range(NB):
                                        pe.matmul(p[3 * x + 1][:, b * P:(b + 1) * P], tt[:, x, b, :],
                                                  p1[:, x, b, :], start=True, stop=True)
                                for b in range(NB):
                                    last = pe.matmul(p[3 * x + 2][:, b * P:(b + 1) * P], p1[:, x, b, :],
                                                     tt[:, x, b, :], start=True, stop=True)
                                last.then_inc(delta_ready, 1)
                        for x, h in enumerate(heads):
                            for b in range(NB):
                                s = slice(b * P, (b + 1) * P)
                                pe.matmul(p[3 * x][:, b * DV:(b + 1) * DV], act_qkv[:, H1 + h, s],
                                          state[:, h, b, :], start=True, stop=True)
                                last = pe.matmul(p[3 * x][:, P + b * DV:P + (b + 1) * DV], act_qkv[:, h, s],
                                                 state[:, h, b, :], start=True, stop=True)
                            last.then_inc(ks_ready, 1)
                        if pair + 1 < H1 // 2:
                            for x in range(2):
                                turn_a(2 * pair + 2 + x)
                        for x, h in enumerate(heads):
                            pe.wait_ge(tri_ready, h + 1)
                            pe.wait_ge(r_ready, h + 1)
                            for b in range(NB):
                                last = pe.matmul(p[3 * x + 1][:, b * DV:(b + 1) * DV], tt[:, x, b, :],
                                                 r1[:, x, 2, b, :], start=True, stop=True)
                            last.then_inc(u_ready, 1)
                        for x, h in enumerate(heads):
                            pe.wait_ge(u_taken, h + 1)
                            pe.wait_ge(kt_ready, h + 1)
                            pe.wait_ge(pm_ready, h + 1)
                            for b in range(NB):
                                pe.matmul(p[3 * x + 2][:, b * DV:(b + 1) * DV], pm[:, h % 4, b, :],
                                          u[:, x, 0, b, :], start=True, stop=True)
                                last = pe.matmul(p[3 * x + 2][:, P + b * DV:P + (b + 1) * DV], kt[:, x, b, :],
                                                 u[:, x, 1, b, :], start=True, stop=True)
                            last.then_inc(o_ready, 1)
                        if pair + 1 < H1 // 2:
                            for x in range(2):
                                turn_k(2 * pair + 2 + x)
                    pe.wait_ge(on_ready, 1)
                    for b in range(NB):
                        pe.transpose(p[0][:, b * P:(b + 1) * P], o[:, b, 0:P], ident)
                        last = pe.transpose(p[1][0:VD - P, b * P:(b + 1) * P], o[:, b, P:VD], ident)
                    last.then_inc(on_turned, 1)
                    pe.wait_ge(ot_ready, 2)
                    pe.matmul(p[2], wo[:, 0, :], ot[:, 0, :], start=True, stop=False)
                    pe.matmul(p[2], wo[0:VD - P, 1, :], ot[0:VD - P, 1, :], start=False, stop=True)\
                        .then_inc(wo_ready, 1)
                    pe.wait_ge(x1_ready, 1)
                    pe.matmul(p[3], mean_m, x1[:], start=True, stop=True).then_inc(mean_ready, 1)
                    pe.wait_ge(lnsq_ready, 2)
                    pe.matmul(p[4], mean_m, sq[:, 0, :], start=True, stop=True).then_inc(var_ready, 1)
                    pe.wait_ge(var_ready, 2)

                @block.scalar
                def _(a):
                    link = linker(a, act_step)

                    def rstd(n, bank_of_var):
                        a.wait_ge(xc_ready, n)
                        a.activation(sq[:, 0, :], xc[:], ACT.Square).then_inc(lnsq_ready, 1)
                        a.wait_ge(var_ready, n)
                        link(a.activation(lg[:, 0, :], bank_of_var, ACT.Ln, bias=c(C_EPS)))
                        a.activation(rs[:, 0, :], lg[:, 0, :], ACT.Exp, scale=-0.5).then_inc(rstd_ready, 1)
                        a.wait_ge(rstd_ready, n)

                    a.preload_act_table_set(LN_EXP)
                    a.wait_ge(x_turned, 1)
                    a.activation(xt[:], p[0], ACT.Copy).then_inc(xt_ready, 1)
                    rstd(1, p[0])

                    def take(n):
                        m = P if n < NCH - 1 else VD - P
                        a.wait_ge(proj_ready, n + 1)
                        if n >= PRE:
                            a.wait_ge(conv_ready, n - PRE + 1)
                            a.wait_ge(tail_kept, n - PRE + 1)
                        a.activation(pre[0:m, n % PRE, :, KS - 1:], blocks(p[n % 4][0:m, :]), ACT.Copy)\
                            .then_inc(pre_ready, 1)

                    def last_tap(n):
                        m = P if n < NCH - 1 else VD - P
                        if n >= PRE:
                            a.wait_ge(silu_ready, n - PRE + 1)
                        a.activation(cv[0:m, n % PRE, :], p[n % 4][0:m, :], ACT.Copy,
                                     scale=cw[0:m, n, KS - 1:KS]).then_inc(tap_ready, 1)

                    def silu(n):
                        a.wait_ge(conv_ready, n + 1)
                        a.activation(act_qkv[:, n, :], cv[:, n % PRE, :], ACT.Silu).then_inc(silu_ready, 1)

                    for n in range(NCH + PRE):
                        if n < NCH:
                            take(n)
                        if n >= PRE:
                            silu(n - PRE)
                        if n < NCH:
                            last_tap(n)
                    a.wait_ge(gates_ready, 1)
                    for i in range(2):
                        src = p[4 + i][:, 0:2 * GW].rearrange("p (b n) -> p b n", b=2)
                        a.activation(sg[:, 2 * i:2 * i + 2, :], src[:, :, 0:VD], ACT.Silu)\
                            .then_inc(gates_taken, 1)
                    a.wait_ge(silu_ready, NCH)
                    a.preload_act_table_set(LN_EXP)
                    a.wait_ge(e1_asked, 1)
                    for i in (3, 4, 5):
                        a.activation(t24[:, i + 3, :, :], t24[:, i, :, :], ACT.Exp).then_inc(e1_ready, 1)
                    def decays(h):
                        a.wait_ge(decay_ready, h + 1)
                        if h >= 2:
                            a.wait_ge(pm_ready, h - 1)
                        a.activation(gat[:, h % 2, :, :], blocks(p[6]), ACT.Exp)
                        a.activation(gam[:, h % 2, :, :], blocks(p[7]), ACT.Exp).then_inc(decay_exp, 1)

                    def take_at(h):
                        a.wait_ge(a_turned, h + 1)
                        if h >= 2:
                            a.wait_ge(ao_ready, (h // 2) * 2 * (LEVELS - 1))
                        a.activation(at[:, h % 2, :, :], blocks(p[6 + h % 2]), ACT.Copy).then_inc(at_ready, 1)

                    def take_kt(h):
                        a.wait_ge(ktok_ready, h + 1)
                        a.activation(kt[:, h % 2, :, :], blocks(p[6 + h % 2]), ACT.Copy).then_inc(kt_ready, 1)

                    a.wait_ge(v_turned, 1)
                    for i in range(2):
                        a.activation(vt[:, 2 * i:2 * i + 2, :],
                                     p[6 + i][:, 0:2 * VD].rearrange("p (b n) -> p b n", b=2), ACT.Copy)\
                            .then_inc(v_ready, 1)
                    for n in range(NQK + 1):
                        if n < NQK:
                            a.wait_ge(ss_ready, n + 1)
                            if n >= 2:
                                a.wait_ge(rn_ready, n - 1)
                            a.activation(lg[:, n % 2, :], p[n % 2], ACT.Ln, bias=c(C_L2)).then_inc(ln_done, 1)
                        if n >= 1:
                            m = n - 1
                            a.wait_ge(ln_done, m + 1)
                            if m >= 2:
                                a.wait_ge(qk_ready, m - 1)
                            a.activation(rs[:, m % 2, :], lg[:, m % 2, :], ACT.Exp, scale=-0.5,
                                         bias=c(C_QSC) if m < H1 else c(C_ZERO)).then_inc(rn_ready, 1)
                        if n == H1:
                            a.wait_ge(cum_ready, 1)
                            a.activation(ex[:].rearrange("p i b h -> p (i b h)"), p[5][:, 0:3 * NB * H1], ACT.Exp)\
                                .then_inc(cum_exp, 1)
                            decays(0)
                    decays(1)
                    for h in range(2):
                        take_at(h)
                    for h in range(2):
                        take_kt(h)
                    for pair in range(H1 // 2):
                        more = pair + 1 < H1 // 2
                        for i in range(1, LEVELS):
                            for x in range(2):
                                n = pair * 2 * (LEVELS - 1) + 2 * (i - 1) + x + 1
                                a.wait_ge(p1_ready, n)
                                a.activation(p1[:, x, :, :], blocks(p[3 * x]), ACT.Copy).then_inc(p1_taken, 1)
                            if more and i in (1, 3):
                                decays(2 * pair + 2 + i // 2)
                        if more:
                            for x in range(2):
                                take_at(2 * pair + 2 + x)
                            for x in range(2):
                                take_kt(2 * pair + 2 + x)
                    a.wait_ge(om_ready, 1)
                    link(a.activation(om[:, 1, :], om[:, 0, :], ACT.Ln, scale=1.0 / DV, bias=c(C_EPS)))
                    a.activation(om[:, 2, :], om[:, 1, :], ACT.Exp, scale=-0.5).then_inc(ostd_ready, 1)
                    a.wait_ge(on_turned, 1)
                    a.activation(ot[:, 0, :], p[0], ACT.Copy).then_inc(ot_ready, 1)
                    a.activation(ot[0:VD - P, 1, :], p[1][0:VD - P, :], ACT.Copy).then_inc(ot_ready, 1)
                    a.wait_ge(ot_ready, 2)
                    rstd(2, p[4])

                @block.gpsimd
                def _(g):
                    for n in range(NCH):
                        m = P if n < NCH - 1 else VD - P
                        src = pre[0:m, n % PRE, :, :]
                        if n >= PRE:
                            g.wait_ge(conv_ready, n - PRE + 1)
                        g.tensor_copy(src[:, :, 0:KS - 1], tail[0:m, n, :, :]).then_inc(front_ready, 1)
                        g.wait_ge(front_ready, n + 1)
                        g.wait_ge(pre_ready, n + 1)
                        g.tensor_copy(tail[0:m, n, :, :], src[:, :, P:P + KS - 1]).then_inc(tail_kept, 1)
                    g.wait_ge(tail_kept, NCH)
                    for n in range(NQK):
                        g.wait_ge(silu_ready, n + 1)
                        if n >= 2:
                            g.wait_ge(ss_ready, n - 1)
                        g.tensor_tensor(sq[:, n % 2, :], act_qkv[:, n, :], act_qkv[:, n, :], ALU.mult)\
                            .then_inc(sq_ready, 1)
                    for pair in range(H1 // 2):
                        for i in range(1, LEVELS):
                            for x in range(2):
                                if i == 1:
                                    g.wait_ge(at_ready, 2 * pair + x + 1)
                                n = pair * 2 * (LEVELS - 1) + 2 * (i - 1) + x + 1
                                if n > 4:
                                    g.wait_ge(p1_ready, n - 4)
                                g.tensor_tensor(ao[:, 2 * x + i % 2, :, :], at[:, x, :, :],
                                                over_batches(msk[:, M_OFF + LEVELS + i, :]), ALU.mult)\
                                    .then_inc(ao_ready, 1)
                    g.wait_ge(ao_ready, H1 * (LEVELS - 1))

                @block.vector
                def _(v):
                    link = linker(v, dve_step)

                    def done(ins, sem, n):
                        ins.then_inc(sem, 1)
                        v.wait_ge(sem, n)

                    def layer_norm(n, src, bank_of_mean, dst):
                        v.wait_ge(mean_ready, n)
                        ins = v.tensor_tensor(xc[:], src, bank_of_mean, ALU.subtract)
                        ins.then_inc(xc_ready, 1)
                        v.wait_ge(xc_ready, n)
                        v.wait_ge(rstd_ready, n)
                        ins = v.tensor_tensor(dst, blocks(xc[:]), blocks(rs[:, 0, :]), ALU.mult)
                        ins.then_inc(xn_ready, 1)
                        v.wait_ge(xn_ready, n)

                    layer_norm(1, xt[:], p[1], blocks(xn[:]))
                    def tap_count(n, tap):
                        return n // 2 * 2 * (KS - 2) + 2 * tap + n % 2 + 1

                    for pair in range(0, NCH, 2):
                        v.wait_ge(pre_ready, pair + 2)
                        v.wait_ge(front_ready, pair + 2)
                        v.wait_ge(tap_ready, pair + 2)
                        for tap in range(KS - 1):
                            for n in (pair, pair + 1):
                                m = P if n < NCH - 1 else VD - P
                                if tap:
                                    v.wait_ge(conv_step, tap_count(n, tap - 1))
                                dst = blocks(cv[0:m, n % PRE, :])
                                ins = v.scalar_tensor_tensor(dst, pre[0:m, n % PRE, :, tap:tap + P],
                                                             cw[0:m, n, tap:tap + 1], dst, ALU.mult, ALU.add)
                                ins.then_inc(conv_step if tap < KS - 2 else conv_ready, 1)
                    v.wait_ge(conv_ready, NCH)
                    v.wait_ge(gates_ready, 1)
                    v.wait_ge(gates_taken, 2)
                    for i in range(2):
                        src = p[4 + i][:, 0:2 * GW].rearrange("p (b n) -> p b n", b=2)
                        link(v.tensor_copy(ba[:, 2 * i:2 * i + 2, :], src[:, :, VD:GW]))
                    beta, dec = ba[:, :, 0:H1], ba[:, :, H1:2 * H1]
                    G, BETA, POS, NB_ABS, NB_MIN, ND_ABS, E_B, E_BM, E_D, S1, S2, T = \
                        [t24[:, i, :, :] for i in range(12)]
                    link(v.tensor_tensor(dec, dec, over_batches(rows[:, H1:2 * H1]), ALU.add))
                    for dst, src in ((NB_ABS, beta), (ND_ABS, dec)):
                        link(v.tensor_scalar(T, src, -1.0, None, ALU.mult))
                        link(v.tensor_tensor(dst, T, src, ALU.min))
                    link(v.tensor_scalar(POS, dec, 0.0, None, ALU.max))
                    done(v.tensor_scalar(NB_MIN, beta, 0.0, None, ALU.min), e1_asked, 1)
                    v.wait_ge(e1_ready, 3)
                    link(v.tensor_scalar(T, E_B, 1.0, None, ALU.add))
                    link(v.reciprocal(S1, T))
                    link(v.tensor_tensor(BETA, S1, E_BM, ALU.mult))
                    link(v.tensor_scalar(T, E_D, 2.0, None, ALU.add))
                    link(v.reciprocal(S2, T))
                    link(v.tensor_tensor(S1, S2, E_D, ALU.mult))
                    link(v.tensor_tensor(S2, S1, S1, ALU.mult))
                    link(v.tensor_scalar(T, S2, 2.0 / (2 * ATANH_TERMS + 1), 2.0 / (2 * ATANH_TERMS - 1),
                                         ALU.mult, ALU.add))
                    for i in range(ATANH_TERMS - 2, -1, -1):
                        link(v.tensor_tensor(T, T, S2, ALU.mult))
                        link(v.tensor_scalar(T, T, 2.0 / (2 * i + 1), None, ALU.add))
                    link(v.tensor_tensor(T, T, S1, ALU.mult))
                    link(v.tensor_tensor(T, T, POS, ALU.add))
                    done(v.tensor_tensor(G, T, over_batches(neg_a[:]), ALU.mult), g_ready, 1)
                    def masked_decay(h):
                        if h >= 2:
                            v.wait_ge(decay_ready, h - 1)
                        for b in range(NB):
                            ins = v.tensor_scalar(gm[:, h % 2, b, :], gt, t24[:, 0, b, h:h + 1], None, ALU.mult)
                        ins.then_inc(gm_ready, 1)

                    for h in range(2):
                        masked_decay(h)
                    for n in range(NQK):
                        v.wait_ge(rn_ready, n + 1)
                        done(v.tensor_tensor(act_qkv[:, n, :], act_qkv[:, n, :], rs[:, n % 2, :], ALU.mult),
                             qk_ready, n + 1)

                    def weigh(h):
                        x = h % 2
                        v.wait_ge(decay_exp, h + 1)
                        if h >= 2:
                            v.wait_ge(a_turned, h - 1)
                            if h >= 4:
                                v.wait_ge(o_ready, h - 3)
                        v.tensor_tensor(pm[:, h % 4, :, :], gat[:, x, :, :], over_batches(le), ALU.mult)
                        link(v.tensor_tensor(gam[:, x, :, :], gam[:, x, :, :], over_batches(gt), ALU.mult))
                        v.wait_ge(kk_ready, h + 1)
                        for b in range(NB):
                            ins = v.scalar_tensor_tensor(am[:, x, b, :], p[6][:, b * P:(b + 1) * P],
                                                         t24[:, 1, b, h:h + 1], gam[:, x, b, :],
                                                         ALU.mult, ALU.mult)
                        ins.then_inc(a_ready, 1)
                        v.tensor_tensor(pm[:, h % 4, :, :], pm[:, h % 4, :, :], blocks(p[7]), ALU.mult)\
                            .then_inc(pm_ready, 1)

                    def first_t(h):
                        x = h % 2
                        v.wait_ge(a_ready, h + 1)
                        link(v.tensor_tensor(tmp[:, x, :, :], am[:, x, :, :], over_batches(msk[:, M_OFF, :]),
                                             ALU.mult))
                        if h >= 2:
                            v.wait_ge(p1_ready, h // 2 * 2 * (LEVELS - 1) - 1 + x)
                        link(v.tensor_tensor(tr[:, x, :, :], over_batches(ident), tmp[:, x, :, :], ALU.subtract))

                    def first_tt(h):
                        x = h % 2
                        v.wait_ge(at_ready, h + 1)
                        link(v.tensor_tensor(tmp[:, x, :, :], at[:, x, :, :],
                                             over_batches(msk[:, M_OFF + LEVELS, :]), ALU.mult))
                        v.tensor_tensor(tt[:, x, :, :], over_batches(ident), tmp[:, x, :, :], ALU.subtract)\
                            .then_inc(t_ready, 1)

                    v.wait_ge(cum_exp, 1)
                    for h in range(2):
                        weigh(h)
                    for h in range(2):
                        first_t(h)
                    for h in range(2):
                        first_tt(h)
                    for pair in range(H1 // 2):
                        heads = (2 * pair, 2 * pair + 1)
                        more = pair + 1 < H1 // 2
                        if more:
                            masked_decay(2 * pair + 2)
                            masked_decay(2 * pair + 3)
                        for i in range(1, LEVELS):
                            if more and i == LEVELS - 1:
                                for x in range(2):
                                    first_t(2 * pair + 2 + x)
                            for x, h in enumerate(heads):
                                n = pair * 2 * (LEVELS - 1) + 2 * (i - 1) + x + 1
                                v.wait_ge(delta_ready, n)
                                v.wait_ge(t_ready, n)
                                if i < LEVELS - 1:
                                    v.tensor_tensor(tr[:, x, :, :], tr[:, x, :, :], blocks(p[3 * x + 1]),
                                                    ALU.subtract)
                                    v.tensor_tensor(tt[:, x, :, :], tt[:, x, :, :], blocks(p[3 * x + 2]),
                                                    ALU.subtract).then_inc(t_ready, 1)
                                else:
                                    v.tensor_tensor(tt[:, x, :, :], tt[:, x, :, :], blocks(p[3 * x + 2]),
                                                    ALU.subtract).then_inc(tri_ready, 1)
                            if more and i in (2, 4):
                                weigh(2 * pair + 1 + i // 2)
                        for x, h in enumerate(heads):
                            v.wait_ge(ks_ready, h + 1)
                            ks, qs = blocks(p[3 * x][:, 0:P]), blocks(p[3 * x][:, P:2 * P])
                            link(v.tensor_tensor(r1[:, x, 0, :, :], ks, along(ex[:, 0, :, h], DV), ALU.mult))
                            v.tensor_tensor(o2[:, x, :, :], qs, along(ex[:, 0, :, h], DV), ALU.mult)
                            link(v.tensor_tensor(r1[:, x, 1, :, :], vt[:, :, h * DV:(h + 1) * DV],
                                                 r1[:, x, 0, :, :], ALU.subtract))
                            v.tensor_tensor(r1[:, x, 2, :, :], r1[:, x, 1, :, :], along(t24[:, 1, :, h], DV),
                                            ALU.mult).then_inc(r_ready, 1)
                        for x, h in enumerate(heads):
                            v.wait_ge(u_ready, h + 1)
                            ups = blocks(p[3 * x + 1][:, 0:P])
                            v.tensor_copy(u[:, x, 0, :, :], ups)
                            v.tensor_tensor(u[:, x, 1, :, :], ups, along(ex[:, 1, :, h], DV),
                                            ALU.mult).then_inc(u_taken, 1)
                        if more:
                            for x in range(2):
                                first_tt(2 * pair + 2 + x)
                        for x, h in enumerate(heads):
                            v.wait_ge(o_ready, h + 1)
                            v.tensor_tensor(o[:, :, h * DV:(h + 1) * DV], o2[:, x, :, :],
                                            blocks(p[3 * x + 2][:, 0:P]), ALU.add)
                            link(v.tensor_tensor(state[:, h, :, :], state[:, h, :, :], along(ex[:, 2, :, h], DV),
                                                 ALU.mult))
                            v.tensor_tensor(state[:, h, :, :], state[:, h, :, :],
                                            blocks(p[3 * x + 2][:, P:2 * P]), ALU.add).then_inc(s_ready, 1)
                            v.wait_ge(s_ready, h + 1)
                    flat = "p b (h d) -> p (b h) d"
                    link(v.tensor_tensor(osq[:], o[:], o[:], ALU.mult))
                    done(v.tensor_reduce(om[:, 0, :], osq[:].rearrange(flat, h=H1), AX.X, ALU.add), om_ready, 1)
                    link(v.tensor_tensor(sg[:].rearrange(flat, h=H1), sg[:].rearrange(flat, h=H1),
                                         over_batches(rows[:, 2 * H1:2 * H1 + DV], NB * H1), ALU.mult))
                    v.wait_ge(ostd_ready, 1)
                    link(v.tensor_tensor(o[:].rearrange(flat, h=H1), o[:].rearrange(flat, h=H1),
                                         along(om[:, 2, :], DV), ALU.mult))
                    done(v.tensor_tensor(o[:], o[:], sg[:], ALU.mult), on_ready, 1)
                    v.wait_ge(wo_ready, 1)
                    done(v.tensor_tensor(x1[:], p[2], xt[:], ALU.add), x1_ready, 1)
                    layer_norm(2, x1[:], p[3], y[:, :, bass.ds(t * P + 1, P)])
            nc.all_engine_barrier(sems_to_clear=range(first, x1_stored.num + 1))


def local_layers(nc, sbuf, names, p, banks, y, msk, ident, c, cols, key_mask, rot, weights):
    C_EPS, C_ZERO, C_NORM, C_NSC = cols
    mean_m, heads_m = msk[:, M_MEAN, :], msk[:, M_HEADS, :]
    qq, kk, sc = banks[:, 0:2, :], banks[:, 2:4, :], banks[:, 4:6, :]
    norm_bank, out_bank = p[6], p[7]
    sc_in = sc[:, :, 0:NB * 2 * WIN].rearrange("p h (b n) -> p h b n", b=NB)
    with ExitStack() as ctx:
        def sb(name, shape, dt=F32):
            return sbuf(ctx, name, shape, dt)

        w = sb("w2s", [P, WCOLS])
        tab = sb("tab", [P, NT, 4, P])
        kmask = sb("kmask", [P, NT, 2 * WIN], BF16)
        idb = sb("idb", [P, P], BF16)
        kx = sb("kx", [P, NP2, NB, KX])
        v_tok = sb("v_tok", [P, NB, INNER])
        v_before = sb("v_before", [WIN, NB, INNER])
        y1 = sb("y1", [P, NB, 1 + P])
        xs = sb("xs", [P, C])
        xf = sb("xf", [P, C])
        xc = sb("xc2", [P, C])
        sq = sb("sq2", [P, 2, C])
        lg = sb("lg2", [P, 2, C])
        rn = sb("rn2", [P, 2, C])
        turn = sb("turn", [P, 2, C])
        turn_k = sb("turn_k", [P, 2, C])
        qf = sb("qf", [P, 2, C])
        e = sb("e", [P, 2 * NB, 2 * WIN])
        et = sb("et", [P, 2, 2 * NB, 2, WIN])
        pt = sb("pt", [P, 2, 2 * NB, P])
        stat = sb("stat", [P, 3, 2 * NB])
        ot = sb("ot2", [P, NP2, C])
        hid = msk[:, M_OFF:M_OFF + FC * NB, :].rearrange("p (i b) n -> p i (b n)", b=NB)

        w_loaded, w_init, tab_ready = names("w_loaded", "w_init", "tab_ready")
        dve_step2, act_step2, next_loaded = names("dve_step2", "act_step2", "next_loaded")
        (xs_ready, vproj_ready, v_kept, v_taken, qproj, kproj, qrproj, krproj, rot_q, rot_k, sqq_ready, sqk_ready,
         turned, nq_ready, nk_ready, lnq_done, lnk_done, rq_ready, rk_ready, q_ready, k_ready,
         scores_ready, scores_used, exp_ready, max_ready, keys_kept, prob_ready, et_ready,
         own_ready, before_ready, pv_ready, ot_ready) = names(
            "xs_ready", "vproj_ready", "v_kept", "v_taken", "qproj", "kproj", "qrproj", "krproj", "rot_q", "rot_k",
            "sqq_ready", "sqk_ready", "turned", "nq_ready", "nk_ready", "lnq_done", "lnk_done",
            "rq_ready", "rk_ready", "q_ready", "k_ready", "scores_ready", "scores_used",
            "exp_ready", "max_ready", "keys_kept", "prob_ready", "et_ready", "own_ready",
            "before_ready", "pv_ready", "ot2_ready")
        (att_ready, xs1_ready, mean_ready, xc_ready, sq1_ready, var_ready, rstd_ready, xn_ready,
         gate_ready, a_ready, gelu_ready, hid_ready, ffn_ready, y_ready) = names(
            "att_ready", "xs1_ready", "mean2_ready", "xc2_ready", "sq1_ready", "var2_ready",
            "rstd2_ready", "xn2_ready", "gate_ready", "a2_ready", "gelu_ready", "hid_ready",
            "ffn_ready", "y_ready")

        FFN_BANKS, V_BANKS = (6, 2, 3), (4, 5)
        GATE_AFTER, A_AFTER, OUT_AFTER = 1, 3, 5

        def vec(i, n=P):
            return w[0:n, W_VEC + i:W_VEC + i + 1]

        with nc.Block() as block:
            @block.sync
            def _(sp):
                sp.dma_start(tab[:, 0, :, :].rearrange("p i n -> p (i n)"), key_mask).then_inc(w_init, 16)
                sp.dma_start(w[:, 0:W_1], weights[0, :, 0:W_1]).then_inc(w_loaded, 16)
                sp.wait_ge(tab_ready, 2)
                sp.dma_start(tab[:], rot).then_inc(w_loaded, 16)
                sp.wait_ge(w_loaded, 32)

            @block.vector
            def _(v):
                for ap in (y[:, :, 0:1], kx[:], v_tok[:], y1[:], pt[:]):
                    v.memset(ap, 0.0)
                v.tensor_copy(idb[:], ident).then_inc(tab_ready, 1)
                v.wait_ge(w_init, 16)
                v.tensor_copy(kmask[:].rearrange("p t n -> p (t n)"),
                              tab[:, 0, :, :].rearrange("p i n -> p (i n)")).then_inc(tab_ready, 1)
                v.wait_ge(tab_ready, 2)
        nc.all_engine_barrier(sems_to_clear=range(w_loaded.num, tab_ready.num + 1))

        def tile(attend, t_att, feed, t_ffn, next_layer=None):
            with nc.Block(no_gpsimd_drain=True) as block:
                if next_layer is not None:
                    @block.sync
                    def _(sp):
                        sp.dma_start(w[:, 0:W_1], weights[bass.ds(next_layer, 1), :, 0:W_1]
                                     .rearrange("l p n -> p (l n)")).then_inc(next_loaded, 16)
                        sp.dma_start(tab[:], rot).then_inc(next_loaded, 16)
                        sp.wait_ge(next_loaded, 32)

                @block.tensor
                def _(pe):
                    def project(j):
                        def product(bank, at, sem):
                            pe.matmul(bank, w[:, at + j * P:at + (j + 1) * P], xs[:], start=True, stop=True)\
                                .then_inc(sem, 1)

                        if feed and j == GATE_AFTER + 2:
                            pe.wait_ge(gelu_ready, FC)
                        if feed and j == A_AFTER + 2:
                            pe.wait_ge(hid_ready, FC)
                        if j:
                            pe.wait_ge(rot_q, j)
                        product(p[0], W_Q, qproj)
                        if j:
                            pe.wait_ge(rot_k, j)
                        product(p[2], W_K, kproj)
                        product(p[1], W_QR, qrproj)
                        if j:
                            norm_q(j)
                        product(p[3], W_KR, krproj)
                        if j:
                            norm_k(j)

                    def v_half(n):
                        b, i = n // 2, n % 2
                        if n >= len(V_BANKS):
                            pe.wait_ge(v_taken, n - len(V_BANKS) + 1)
                        pe.matmul(p[V_BANKS[n % len(V_BANKS)]], xs[:, b * P:(b + 1) * P],
                                  w[:, W_V + i * 512:W_V + (i + 1) * 512], start=True, stop=True)\
                            .then_inc(vproj_ready, 1)

                    def norm_q(j):
                        pe.wait_ge(sqq_ready, j + 1)
                        if j:
                            pe.wait_ge(rk_ready, j)
                        elif feed:
                            pe.wait_ge(xs1_ready, 1)
                        if feed and j == OUT_AFTER + 2:
                            pe.wait_ge(y_ready, 1)
                        pe.matmul(norm_bank, heads_m, sq[:, 0, :], start=True, stop=True)\
                            .then_inc(nq_ready, 1)

                    def norm_k(j):
                        pe.wait_ge(sqk_ready, j + 1)
                        pe.wait_ge(lnq_done, j + 1)
                        pe.matmul(norm_bank, heads_m, sq[:, 1, :], start=True, stop=True)\
                            .then_inc(nk_ready, 1)

                    def scores(j):
                        pe.wait_ge(q_ready, j + 1)
                        pe.wait_ge(k_ready, j + 1)
                        if j:
                            pe.wait_ge(scores_used, j)
                        for h in range(2):
                            pe.matmul(blocks(sc[:, h, 0:NB * 2 * WIN]), idb[:],
                                      kmask[:, bass.ds(t_att, 1), :].to_broadcast([P, NB, 2 * WIN]),
                                      start=True, stop=False, skip_group_check=True)
                        for b in range(NB):
                            for n in range(NW):
                                for h in range(2):
                                    r = slice(h * DH, (h + 1) * DH)
                                    last = pe.matmul(
                                        sc[n * WIN:(n + 1) * WIN, h, b * 2 * WIN:(b + 1) * 2 * WIN],
                                        qf[r, j % 2, b * P + n * WIN:b * P + (n + 1) * WIN],
                                        kx[r, j, b, n * WIN:(n + 2) * WIN],
                                        start=False, stop=True, skip_group_check=True)
                        last.then_inc(scores_ready, 1)

                    def values(j):
                        pe.wait_ge(own_ready, j + 1)
                        pe.wait_ge(before_ready, j + 1)
                        if j:
                            pe.wait_ge(ot_ready, j)
                        for h in range(2):
                            col = (2 * j + h) * DH
                            r = slice(h * DH, (h + 1) * DH)
                            for b in range(NB):
                                pe.matmul(out_bank[r, b * P:(b + 1) * P], v_tok[:, b, col:col + DH],
                                          pt[:, j % 2, h * NB + b, :], start=True, stop=False,
                                          skip_group_check=True)
                                last = pe.matmul(out_bank[r, b * P:b * P + WIN],
                                                 v_before[:, b, col:col + DH],
                                                 et[0:WIN, j % 2, h * NB + b, 0, :],
                                                 start=False, stop=True, skip_group_check=True)
                        last.then_inc(pv_ready, 1)

                    def output(pairs):
                        for j in pairs:
                            pe.wait_ge(ot_ready, j + 1)
                            pe.matmul(norm_bank, w[:, W_O + j * P:W_O + (j + 1) * P], ot[:, j, :],
                                      start=(j == 0), stop=(j == NP2 - 1)).then_inc(att_ready, 1)

                    def mean():
                        pe.wait_ge(xs1_ready, 2)
                        pe.matmul(out_bank, mean_m, xf[:], start=True, stop=True).then_inc(mean_ready, 1)

                    def variance():
                        pe.wait_ge(sq1_ready, 1)
                        pe.matmul(out_bank, mean_m, hid[:, 0, :], start=True, stop=True).then_inc(var_ready, 1)

                    def banks_free(j):
                        pe.wait_ge(rk_ready, j + 1)
                        pe.wait_ge(rot_k, j + 1)

                    def up(first, sem):
                        for i, b in enumerate(FFN_BANKS):
                            n = FROWS[i]
                            pe.matmul(p[b][0:n, :], w[:, W_1 + first + i * P:W_1 + first + i * P + n], xf[:],
                                      start=True, stop=True).then_inc(sem, 1)

                    def gates():
                        pe.wait_ge(xn_ready, 1)
                        up(FF, gate_ready)

                    def linear():
                        pe.wait_ge(gelu_ready, FC)
                        up(0, a_ready)

                    def down():
                        for i in range(FC):
                            n = FROWS[i]
                            pe.wait_ge(hid_ready, i + 1)
                            last = pe.matmul(norm_bank, w[0:n, W_2 + i * P:W_2 + (i + 1) * P], hid[0:n, i, :],
                                             start=(i == 0), stop=(i == FC - 1))
                        last.then_inc(ffn_ready, 1)

                    if not attend:
                        mean()
                        variance()
                        gates()
                        linear()
                        down()
                        pe.wait_ge(ffn_ready, 1)
                        return
                    pe.wait_ge(xs_ready, 2)
                    project(0)
                    if feed:
                        mean()
                    v_half(0)
                    v_half(1)
                    norm_q(0)
                    v_half(2)
                    norm_k(0)
                    v_half(3)
                    v_half(4)
                    if feed:
                        variance()
                    for n in range(5, 2 * NB):
                        v_half(n)
                    pe.wait_ge(v_taken, 2 * NB)
                    scores(0)
                    if feed:
                        pe.wait_ge(rstd_ready, 1)
                    for j in range(NP2):
                        if j + 1 < NP2:
                            project(j + 1)
                        if j:
                            values(j - 1)
                        if feed and j in (GATE_AFTER, A_AFTER, OUT_AFTER):
                            banks_free(j + 1)
                            {GATE_AFTER: gates, A_AFTER: linear, OUT_AFTER: down}[j]()
                        if j + 1 < NP2:
                            scores(j + 1)
                    pe.wait_ge(rk_ready, NP2)
                    output(range(NP2 - 2))
                    values(NP2 - 1)
                    output(range(NP2 - 2, NP2))
                    pe.wait_ge(att_ready, NP2)

                @block.scalar
                def _(a):
                    link = linker(a, act_step2)

                    def square_q(j):
                        a.wait_ge(qproj, j + 1)
                        if j:
                            a.wait_ge(nq_ready, j)
                        a.activation(sq[:, 0, :], qq[:, 0, :], ACT.Square).then_inc(sqq_ready, 1)

                    def square_k(j):
                        a.wait_ge(kproj, j + 1)
                        if j:
                            a.wait_ge(nk_ready, j)
                        a.activation(sq[:, 1, :], kk[:, 0, :], ACT.Square).then_inc(sqk_ready, 1)

                    def inverse_norm(j, i):
                        ready, ln_sem, sem, used = ((nq_ready, lnq_done, rq_ready, q_ready),
                                                    (nk_ready, lnk_done, rk_ready, k_ready))[i]
                        a.wait_ge(ready, j + 1)
                        a.activation(lg[:, i, :], norm_bank, ACT.Ln, scale=2.0 ** LN_SHIFT,
                                     bias=c(C_NORM)).then_inc(ln_sem, 1)
                        a.wait_ge(ln_sem, j + 1)
                        if j:
                            a.wait_ge(used, j)
                        a.activation(rn[:, i, :], lg[:, i, :], ACT.Exp, scale=-0.5,
                                     bias=c(C_NSC)).then_inc(sem, 1)

                    def take_v(n):
                        b, i = n // 2, n % 2
                        a.wait_ge(vproj_ready, n + 1)
                        a.activation(v_tok[:, b, i * 512:(i + 1) * 512], p[V_BANKS[n % len(V_BANKS)]],
                                     ACT.Copy).then_inc(v_taken, 1)

                    def square_1():
                        a.wait_ge(xc_ready, 1)
                        a.activation(hid[:, 0, :], xc[:], ACT.Square).then_inc(sq1_ready, 1)

                    def rstd():
                        a.wait_ge(var_ready, 1)
                        link(a.activation(hid[:, 1, :], out_bank, ACT.Ln, bias=c(C_EPS)))
                        a.activation(hid[:, 2, :], hid[:, 1, :], ACT.Exp, scale=-0.5).then_inc(rstd_ready, 1)

                    def gelus():
                        a.wait_ge(xn_ready, 1)
                        for i, b in enumerate(FFN_BANKS):
                            n = FROWS[i]
                            a.wait_ge(gate_ready, i + 1)
                            a.activation(hid[0:n, i, :], p[b][0:n, :], ACT.Gelu, bias=vec(V_GATE + i, n))\
                                .then_inc(gelu_ready, 1)

                    a.preload_act_table_set(LN_EXP)
                    if not attend:
                        square_1()
                        rstd()
                        gelus()
                        a.wait_ge(gelu_ready, FC)
                        return
                    square_q(0)
                    square_k(0)
                    a.wait_ge(v_kept, 1)
                    take_v(0)
                    take_v(1)
                    if feed:
                        square_1()
                    inverse_norm(0, 0)
                    take_v(2)
                    inverse_norm(0, 1)
                    take_v(3)
                    take_v(4)
                    if feed:
                        rstd()
                    for n in range(5, 2 * NB):
                        take_v(n)
                    def take_out(j):
                        a.wait_ge(pv_ready, j + 1)
                        a.activation(ot[:, j, :], out_bank, ACT.Copy).then_inc(ot_ready, 1)

                    for j in range(NP2):
                        if j + 1 < NP2:
                            square_q(j + 1)
                        a.wait_ge(scores_used, j + 1)
                        a.activation(e[:], e[:], ACT.Exp, scale=QK_SCALE).then_inc(exp_ready, 1)
                        if j + 1 < NP2:
                            square_k(j + 1)
                            inverse_norm(j + 1, 0)
                            inverse_norm(j + 1, 1)
                        if j == NP2 - 1:
                            take_out(j - 1)
                        a.wait_ge(et_ready, j + 1)
                        if j >= 2:
                            a.wait_ge(pv_ready, j - 1)
                        for n in range(NW):
                            r = slice(n * WIN, (n + 1) * WIN)
                            last = a.activation(pt[r, j % 2, :, n * WIN:(n + 1) * WIN],
                                                et[r, j % 2, :, 1, :], ACT.Copy)
                        last.then_inc(own_ready, 1)
                        if 0 < j < NP2 - 1:
                            take_out(j - 1)
                        if feed and j == GATE_AFTER:
                            gelus()
                            a.preload_act_table_set(LN_EXP)
                    take_out(NP2 - 1)
                    a.wait_ge(ot_ready, NP2)

                @block.gpsimd
                def _(g):
                    if not attend:
                        return
                    for j in range(NP2):
                        for ready, pair in ((rot_q, turn), (rot_k, turn_k)):
                            g.wait_ge(ready, j + 1)
                            g.tensor_tensor(pair[:, 0, :], pair[:, 0, :], pair[:, 1, :], ALU.add)\
                                .then_inc(turned, 1)
                    g.wait_ge(turned, 2 * NP2)

                @block.vector
                def _(v):
                    link = linker(v, dve_step2)

                    def done(ins, sem, n):
                        ins.then_inc(sem, 1)
                        v.wait_ge(sem, n)

                    def shifted(dst, src, at, sem):
                        half = P // 2
                        done(v.tensor_copy(blocks(dst[0:half, :]), src[0:half, :, bass.ds(at + 1, P)]), sem, 1)
                        done(v.tensor_copy(blocks(dst[half:P, :]), src[half:P, :, bass.ds(at, P)]), sem, 2)

                    def residual():
                        link(v.tensor_copy(y1[:, :, 0:1], y1[:, :, P:P + 1]))
                        link(v.tensor_tensor(y1[:, :, 1:1 + P], blocks(norm_bank),
                                             y[:, :, bass.ds(t_ffn * P + 1, P)], ALU.add))
                        shifted(xf, y1, 0, xs1_ready)

                    def centre():
                        v.wait_ge(mean_ready, 1)
                        done(v.tensor_tensor(xc[:], xf[:], out_bank, ALU.subtract), xc_ready, 1)

                    def normed():
                        v.wait_ge(rstd_ready, 1)
                        link(v.tensor_tensor(xc[:], xc[:], hid[:, 2, :], ALU.mult))
                        done(v.tensor_scalar(xf[:], xc[:], vec(V_G), vec(V_B), ALU.mult, ALU.add), xn_ready, 1)

                    def hidden():
                        for i, b in enumerate(FFN_BANKS):
                            n = FROWS[i]
                            v.wait_ge(a_ready, i + 1)
                            v.wait_ge(gelu_ready, i + 1)
                            done(v.scalar_tensor_tensor(hid[0:n, i, :], p[b][0:n, :], vec(V_A + i, n),
                                                        hid[0:n, i, :], ALU.add, ALU.mult), hid_ready, i + 1)

                    def finish():
                        v.wait_ge(ffn_ready, 1)
                        done(v.scalar_tensor_tensor(y[:, :, bass.ds(t_ffn * P + 1, P)], blocks(norm_bank),
                                                    vec(V_B2), y1[:, :, 1:1 + P], ALU.add, ALU.add), y_ready, 1)

                    if not attend:
                        residual()
                        centre()
                        normed()
                        hidden()
                        finish()
                        return
                    shifted(xs, y, t_att * P, xs_ready)
                    done(v.tensor_copy(v_before[:], v_tok[P - WIN:P, :, :]), v_kept, 1)
                    if feed:
                        residual()

                    def rotate(j, i):
                        squared, ready, sem, src, dst = ((sqq_ready, qrproj, rot_q, qq, turn),
                                                         (sqk_ready, krproj, rot_k, kk, turn_k))[i]
                        v.wait_ge(squared, j + 1)
                        v.wait_ge(ready, j + 1)
                        if j:
                            v.wait_ge((q_ready, k_ready)[i], j)
                        table = tab[:, bass.ds(t_att, 1), 2 * i:2 * i + 2, :].rearrange("p o s n -> p (o s) n")
                        v.tensor_tensor(dst[:].rearrange("p s (b n) -> p s b n", b=NB),
                                        src.rearrange("p s (b n) -> p s b n", b=NB),
                                        table.unsqueeze(2).to_broadcast([P, 2, NB, P]), ALU.mult)\
                            .then_inc(sem, 1)

                    def keep_keys(j):
                        v.tensor_copy(kx[:, j, :, 0:WIN], kx[:, j, :, P:KX])\
                            .then_inc(keys_kept, 1)

                    def unit(j):
                        v.wait_ge(turned, 2 * j + 1)
                        v.wait_ge(rq_ready, j + 1)
                        if j >= 2:
                            v.wait_ge(scores_ready, j - 1)
                        v.tensor_tensor(qf[:, j % 2, :], turn[:, 0, :], rn[:, 0, :], ALU.mult)\
                            .then_inc(q_ready, 1)
                        v.wait_ge(keys_kept, j + 1)
                        v.wait_ge(turned, 2 * j + 2)
                        v.wait_ge(rk_ready, j + 1)
                        v.tensor_tensor(kx[:, j, :, WIN:KX], blocks(turn_k[:, 0, :]),
                                        blocks(rn[:, 1, :]), ALU.mult).then_inc(k_ready, 1)

                    rotate(0, 0)
                    rotate(0, 1)
                    if feed:
                        centre()
                    keep_keys(0)
                    unit(0)
                    if feed:
                        normed()
                    for j in range(NP2):
                        v.wait_ge(scores_ready, j + 1)
                        v.tensor_reduce(stat[:, 0, :].rearrange("p (h b) -> p h b", h=2), sc_in, AX.X,
                                        ALU.max).then_inc(max_ready, 1)
                        v.wait_ge(max_ready, j + 1)
                        if j:
                            v.wait_ge(et_ready, j)
                        v.tensor_tensor(e[:].rearrange("p (h b) n -> p h b n", h=2), sc_in,
                                        stat[:, 0, :].rearrange("p (h b) -> p h b", h=2).unsqueeze(3)
                                        .to_broadcast([P, 2, NB, 2 * WIN]), ALU.subtract)\
                            .then_inc(scores_used, 1)
                        if j + 1 < NP2:
                            keep_keys(j + 1)
                        v.wait_ge(exp_ready, j + 1)
                        link(v.tensor_reduce(stat[:, 1, :], e[:], AX.X, ALU.add))
                        if j + 1 < NP2:
                            rotate(j + 1, 0)
                        link(v.reciprocal(stat[:, 2, :], stat[:, 1, :]))
                        v.tensor_tensor(e[:], e[:], along(stat[:, 2, :], 2 * WIN), ALU.mult)\
                            .then_inc(prob_ready, 1)
                        if j + 1 < NP2:
                            rotate(j + 1, 1)
                        v.wait_ge(prob_ready, j + 1)
                        if j >= 2:
                            v.wait_ge(pv_ready, j - 1)
                        v.transpose(et[:, j % 2, :, :, :].rearrange("p m s n -> p (m s n)"),
                                    e[:].rearrange("p m n -> p (m n)")).then_inc(et_ready, 1)
                        if j + 1 < NP2:
                            unit(j + 1)
                        v.wait_ge(et_ready, j + 1)
                        for n in range(1, NW):
                            last = v.tensor_copy(pt[(n - 1) * WIN:n * WIN, j % 2, :, n * WIN:(n + 1) * WIN],
                                                 et[n * WIN:(n + 1) * WIN, j % 2, :, 0, :])
                        last.then_inc(before_ready, 1)
                        if feed and j == A_AFTER:
                            hidden()
                        if feed and j == OUT_AFTER:
                            finish()
                    v.wait_ge(before_ready, NP2)
            nc.all_engine_barrier(sems_to_clear=range(dve_step2.num, y_ready.num + 1))

        def start_layer(layer):
            with nc.Block() as block:
                @block.sync
                def _(sp):
                    sp.dma_start(w[:, W_1:], weights[bass.ds(layer, 1), :, W_1:].rearrange("l p n -> p (l n)"))\
                        .then_inc(w_loaded, 16)
                    sp.wait_ge(w_loaded, 16)

                @block.vector
                def _(v):
                    v.memset(kx[:, :, :, P:KX], 0.0)
                    v.memset(y1[:, :, P:P + 1], 0.0)
                    v.wait_ge(w_loaded, 16)
                    for i in range(4):
                        v.tensor_scalar(tab[:, :, i, :], tab[:, :, i, :], vec(V_ROT + i), None, ALU.mult)\
                            .then_inc(tab_ready, 1)
                    v.wait_ge(tab_ready, 4)
            nc.all_engine_barrier(sems_to_clear=range(w_loaded.num, tab_ready.num + 1))

        def run_layer(layer, next_layer):
            start_layer(layer)
            tile(True, 0, False, None)
            with nc.Fori(0, NT - 1) as t:
                tile(True, t + 1, True, t)
            tile(False, None, True, NT - 1, next_layer)

        with nc.Fori(0, DEPTH - 1) as layer:
            run_layer(layer, layer + 1)
        run_layer(DEPTH - 1, None)


def final_sum(nc, sbuf, names, p, y, ident, x1_dram, out):
    with ExitStack() as ctx:
        x1 = sbuf(ctx, "x1f", [P, NB, P])
        s = sbuf(ctx, "sf", [P, NB, P])
        o = sbuf(ctx, "of", [P, NB, P])
        x1_loaded, sum_ready, sum_turned, out_ready, out_stored = names(
            "x1_loaded", "sum_ready", "sum_turned", "out_ready", "out_stored")
        with nc.Fori(0, NT) as t:
            with nc.Block(no_gpsimd_drain=True) as block:
                @block.sync
                def _(sp):
                    sp.dma_start(x1[:], x1_dram[:, :, bass.ds(t * P, P)]).then_inc(x1_loaded, 16)
                    sp.wait_ge(out_ready, 1)
                    sp.dma_start(out[:, bass.ds(t * P, P), :].rearrange("b p d -> p b d"), o[:])\
                        .then_inc(out_stored, 16)
                    sp.wait_ge(out_stored, 16)

                @block.vector
                def _(v):
                    v.wait_ge(x1_loaded, 16)
                    v.tensor_tensor(s[:], x1[:], y[:, :, bass.ds(t * P + 1, P)], ALU.add).then_inc(sum_ready, 1)
                    v.wait_ge(sum_ready, 1)

                @block.tensor
                def _(pe):
                    pe.wait_ge(sum_ready, 1)
                    for b in range(NB):
                        last = pe.transpose(p[0][:, b * P:(b + 1) * P], s[:, b, :], ident)
                    last.then_inc(sum_turned, 1)
                    pe.wait_ge(sum_turned, 1)

                @block.scalar
                def _(a):
                    a.wait_ge(sum_turned, 1)
                    a.activation(o[:], blocks(p[0]), ACT.Copy).then_inc(out_ready, 1)
                    a.wait_ge(out_ready, 1)
            nc.all_engine_barrier(sems_to_clear=range(x1_loaded.num, out_stored.num + 1))


def shape_constants():
    i, j = np.arange(P)[:, None], np.arange(P)[None, :]
    m = np.zeros((P, NM, P), np.float32)
    m[:, M_ID], m[:, M_LE], m[:, M_GT] = i == j, i <= j, i > j
    m[:, M_MEAN], m[:, M_ONES], m[:, M_HEADS] = 1.0 / P, 1.0, i // DH == j // DH
    for n in range(LEVELS):
        s = 1 << n
        low = (i // (2 * s) == j // (2 * s)) & (i // s % 2 == 1) & (j // s % 2 == 0)
        m[:, M_OFF + n], m[:, M_OFF + LEVELS + n] = low, low.T
    key = np.zeros((P, NT, 2 * WIN), np.float32)
    r, k = (np.arange(P) % WIN)[:, None], np.arange(2 * WIN)[None, :]
    hidden = np.where(k < WIN, k < r, k - WIN > r)
    key[:] = np.where(hidden, MASKED, 0.0)[:, None, :]
    key[0:WIN, 0, 0:WIN] = MASKED
    half = np.arange(0, DH, 2, dtype=np.float32)
    inv_freq = (1.0 / 10000.0 ** (half / np.float32(DH))).astype(np.float32)
    pos = np.arange(L, dtype=np.float32)
    f = (pos[:, None] * inv_freq[None, :]).astype(np.float32).astype(np.float64)
    base = ((half + np.float32(0.4 * DH)) / np.float32(1.4 * DH)).astype(np.float64)
    scale = base[None, :] ** ((pos - L // 2) / (WIN // 2))[:, None].astype(np.float64)
    tab = np.zeros((4, P, L))
    for d in range(P):
        n = d % (DH // 2)
        sign = -1.0 if d % DH < DH // 2 else 1.0
        cos, sin, s = np.cos(f[:, n]), np.sin(f[:, n]), scale[:, n]
        tab[:, d] = cos * s, sign * sin * s, cos / s, sign * sin / s
    tab = tab.reshape(4, P, NT, P).transpose(1, 2, 0, 3).astype(np.float32)
    return m, key.reshape(P, NT * 2 * WIN), np.ascontiguousarray(tab)


def laid_out(d):
    g = {k: np.asarray(v) for k, v in d.items()}
    a = {k[8:]: v for k, v in g.items() if k.startswith("L0_attn_")}
    f = {k[7:]: v for k, v in g.items() if k.startswith("L0_ffn_")}

    def rows(m, n):
        full = np.zeros((n * P, m.shape[1]), np.float32)
        full[:m.shape[0]] = m
        return full.reshape(n, P, -1).transpose(1, 0, 2).reshape(P, -1)

    w1 = np.concatenate([a["Wq"], a["Wk"], a["Wv"], a["Wg"], a["Wb"], a["Wa"]], axis=1)
    conv = rows(np.concatenate([a["conv_q"], a["conv_k"], a["conv_v"]]), NCH).reshape(P, NCH, KS)
    wo1 = rows(a["Wo"], 2).reshape(P, 2, P)
    rows1 = np.concatenate([a["A_log"], a["dt_bias"], a["norm_w"]])
    d_of = np.arange(P) % DH
    swap = (d_of + DH // 2) % DH
    cols = np.arange(INNER)
    swapped = cols // DH * DH + (cols % DH + DH // 2) % DH
    per_layer = []
    for i in range(DEPTH):
        wq, wk = f["Wqkv"][i][:, 0:INNER], f["Wqkv"][i][:, INNER:2 * INNER]
        vec = np.zeros((P, WCOLS - W_VEC), np.float32)
        vec[:, V_G], vec[:, V_B], vec[:, V_B2] = f["ln_g"][i], f["ln_b"][i], f["b2"][i]
        for n in range(FC):
            vec[:FROWS[n], V_A + n] = f["b1"][i][n * P:n * P + FROWS[n]]
            vec[:FROWS[n], V_GATE + n] = f["b1"][i][FF + n * P:FF + n * P + FROWS[n]]
        for n, s in enumerate((f["q_scale"][i], f["k_scale"][i])):
            vec[:, V_ROT + 2 * n], vec[:, V_ROT + 2 * n + 1] = s[d_of], s[swap]
        per_layer.append(np.concatenate([f["Wqkv"][i], wq[:, swapped], wk[:, swapped], f["W1"][i],
                                         rows(f["Wo"][i], NP2), rows(f["W2"][i], FC), vec], axis=1))
    masks, key_mask, rot = shape_constants()
    return {"x": a["x"], "w1": w1, "conv": conv, "wo1": wo1, "rows1": rows1, "masks": masks,
            "key_mask": key_mask, "rot": rot, "weights": np.stack(per_layer)}


def program(nc, arrays):
    ap = {n: nc.dram_tensor(f"in_{n}", v.shape, mybir.dt.from_np(v.dtype), kind="ExternalInput").ap()
          for n, v in arrays.items()}
    out = nc.dram_tensor("out", (NB, L, P), F32, kind="ExternalOutput").ap()
    x1_dram = nc.dram_tensor("x1_dram", (P, NB, L), F32, kind="Internal").ap()
    build(nc, ap["x"], ap["w1"], ap["conv"], ap["wo1"], ap["rows1"], ap["masks"],
          ap["key_mask"], ap["rot"], ap["weights"], out, x1_dram)


def kernel(**inputs):
    import concourse.bacc as bacc
    from concourse.bass_utils import run_bass_kernel_spmd as run

    nc = bacc.Bacc("TRN2", target_bir_lowering=False, num_devices=1)
    arrays = {n: np.ascontiguousarray(v) for n, v in laid_out(inputs).items()}
    program(nc, arrays)
    r = run(nc, [{f"in_{n}": v for n, v in arrays.items()}], core_ids=[0])
    return r.results[0]["out"]
```
